# Optimizing a Trainium2 kernel written in Bass

```python
import numpy as np
import jax
import jax.numpy as jnp

def _softmax(x, axis=-1):
    return jax.nn.softmax(x, axis=axis)

def _gelu(x):
    return jax.nn.gelu(x, approximate=True)

def _silu(x):
    return jax.nn.silu(x)

def _sigmoid(x):
    return jax.nn.sigmoid(x)

def _layernorm(x, axis=-1, eps=1e-05):
    m = jnp.mean(x, axis=axis, keepdims=True)
    v = jnp.var(x, axis=axis, keepdims=True)
    return (x - m) / jnp.sqrt(v + eps)

def _scatter_add(tgt, idx, src, axis=0):
    return tgt.at[idx].add(src)

def _segment_sum(src, seg, n):
    return jax.ops.segment_sum(src, seg, n)
kernel_name = 'mk_adaln_d2_jaxref_r8_c693ea'

def setup_inputs(seed: int=0):
    np.random.seed(seed)
    _w = jnp.asarray

    def _L0_attn_setup():
        import jax, jax.numpy as jnp
        import numpy as np
        DIMS = 128
        HEADS = 16
        HEAD_DIM = DIMS // HEADS
        key = jax.random.key(seed)
        k_x, k_q, k_k, k_v = jax.random.split(key, 4)
        scale = 1.0 / np.sqrt(DIMS)
        return {'input_seq_embs': jax.random.normal(k_x, (4, 512, DIMS), dtype=jnp.float32), 'W_Q': jax.random.normal(k_q, (DIMS, DIMS), dtype=jnp.float32) * scale, 'W_K': jax.random.normal(k_k, (DIMS, DIMS), dtype=jnp.float32) * scale, 'W_V': jax.random.normal(k_v, (DIMS, DIMS), dtype=jnp.float32) * scale}
    _L0_attn_in = _L0_attn_setup()

    def _L0_ffn_setup():
        import jax, jax.numpy as jnp
        import numpy as np
        DIM = 128
        HIDDEN = 384
        SCALE = 1.0 / 127.0

        def _dequant(w_int, dtype):
            return w_int.astype(dtype) * jnp.asarray(SCALE, dtype)
        key = jax.random.key(seed)
        k_x, k_g, k_u, k_d = jax.random.split(key, 4)
        x = jax.random.normal(k_x, (4, 256, DIM), dtype=jnp.float32)
        w_gate = jax.random.randint(k_g, (HIDDEN, DIM), -127, 128, dtype=jnp.int32)
        w_up = jax.random.randint(k_u, (HIDDEN, DIM), -127, 128, dtype=jnp.int32)
        w_down = jax.random.randint(k_d, (DIM, HIDDEN), -127, 128, dtype=jnp.int32)
        return {'x': x, 'w_gate': w_gate, 'w_up': w_up, 'w_down': w_down}
    _L0_ffn_in = _L0_ffn_setup()
    _L0_c = _w((lambda *s: np.random.randn(*s).astype(np.float32) * 0.05)(1, 128))
    _L0_wmod = _w((lambda *s: np.random.randn(*s).astype(np.float32) * 0.05)(128, 6 * 128) * 128 ** (-0.5))

    def _L1_attn_setup():
        import math
        import jax, jax.numpy as jnp
        import numpy as np
        B, L, D_MODEL = (2, 256, 128)
        N_HEAD, HEAD_DIM = (16, 64)
        ATT_SCALE = 1.0
        key = jax.random.key(seed)
        ks = jax.random.split(key, 6)
        HD = N_HEAD * HEAD_DIM

        def xavier(k, fan_in, fan_out):
            lim = math.sqrt(6.0 / (fan_in + fan_out))
            return jax.random.uniform(k, (fan_in, fan_out), jnp.float32, -lim, lim)
        return {'x': jax.random.normal(ks[0], (B, L, D_MODEL), jnp.float32), 'Wq': xavier(ks[1], D_MODEL, HD), 'bq': jnp.zeros((HD,), jnp.float32), 'Wk': xavier(ks[2], D_MODEL, HD), 'bk': jnp.zeros((HD,), jnp.float32), 'Wv': xavier(ks[3], D_MODEL, HD), 'bv': jnp.zeros((HD,), jnp.float32), 'Wo': xavier(ks[4], HD, D_MODEL), 'bo': jax.random.uniform(ks[5], (D_MODEL,), jnp.float32, -1.0 / math.sqrt(HD), 1.0 / math.sqrt(HD))}
    _L1_attn_in = _L1_attn_setup()

    def _L1_ffn_setup():
        import jax, jax.numpy as jnp
        import numpy as np
        B, S, D, F, E, K = (4, 256, 128, 256, 8, 2)
        key = jax.random.key(seed)
        ks = jax.random.split(key, 9)
        sc = 0.02
        return {'hidden_states': jax.random.normal(ks[0], (B, S, D), jnp.float32), 'router_w': jax.random.normal(ks[1], (E, D), jnp.float32) * sc, 'w_gate': jax.random.normal(ks[2], (E, D, F), jnp.float32) * sc, 'w_up': jax.random.normal(ks[3], (E, D, F), jnp.float32) * sc, 'w_down': jax.random.normal(ks[4], (E, F, D), jnp.float32) * sc, 'sw_gate': jax.random.normal(ks[5], (D, F), jnp.float32) * sc, 'sw_up': jax.random.normal(ks[6], (D, F), jnp.float32) * sc, 'sw_down': jax.random.normal(ks[7], (F, D), jnp.float32) * sc, 'gate_w': jax.random.normal(ks[8], (1, D), jnp.float32) * sc}
    _L1_ffn_in = _L1_ffn_setup()
    _L1_c = _w((lambda *s: np.random.randn(*s).astype(np.float32) * 0.05)(1, 128))
    _L1_wmod = _w((lambda *s: np.random.randn(*s).astype(np.float32) * 0.05)(128, 6 * 128) * 128 ** (-0.5))
    _d = {'L0_attn_input_seq_embs': _L0_attn_in['input_seq_embs'], 'L0_attn_W_Q': _L0_attn_in['W_Q'], 'L0_attn_W_K': _L0_attn_in['W_K'], 'L0_attn_W_V': _L0_attn_in['W_V'], 'L0_ffn_w_gate': _L0_ffn_in['w_gate'], 'L0_ffn_w_up': _L0_ffn_in['w_up'], 'L0_ffn_w_down': _L0_ffn_in['w_down'], 'L0_c': _L0_c, 'L0_wmod': _L0_wmod, 'L1_attn_Wq': _L1_attn_in['Wq'], 'L1_attn_bq': _L1_attn_in['bq'], 'L1_attn_Wk': _L1_attn_in['Wk'], 'L1_attn_bk': _L1_attn_in['bk'], 'L1_attn_Wv': _L1_attn_in['Wv'], 'L1_attn_bv': _L1_attn_in['bv'], 'L1_attn_Wo': _L1_attn_in['Wo'], 'L1_attn_bo': _L1_attn_in['bo'], 'L1_ffn_router_w': _L1_ffn_in['router_w'], 'L1_ffn_w_gate': _L1_ffn_in['w_gate'], 'L1_ffn_w_up': _L1_ffn_in['w_up'], 'L1_ffn_w_down': _L1_ffn_in['w_down'], 'L1_ffn_sw_gate': _L1_ffn_in['sw_gate'], 'L1_ffn_sw_up': _L1_ffn_in['sw_up'], 'L1_ffn_sw_down': _L1_ffn_in['sw_down'], 'L1_ffn_gate_w': _L1_ffn_in['gate_w'], 'L1_c': _L1_c, 'L1_wmod': _L1_wmod}
    _x0 = _d['L0_attn_input_seq_embs']
    _d['L0_attn_input_seq_embs'] = jax.random.normal(jax.random.fold_in(jax.random.key(seed), 1), (1, 2048, 128), dtype=_x0.dtype)
    del _x0
    return _d

def reference(L0_attn_input_seq_embs, L0_attn_W_Q, L0_attn_W_K, L0_attn_W_V, L0_ffn_w_gate, L0_ffn_w_up, L0_ffn_w_down, L0_c, L0_wmod, L1_attn_Wq, L1_attn_bq, L1_attn_Wk, L1_attn_bk, L1_attn_Wv, L1_attn_bv, L1_attn_Wo, L1_attn_bo, L1_ffn_router_w, L1_ffn_w_gate, L1_ffn_w_up, L1_ffn_w_down, L1_ffn_sw_gate, L1_ffn_sw_up, L1_ffn_sw_down, L1_ffn_gate_w, L1_c, L1_wmod):

    def _L0_attn_ref(input_seq_embs, W_Q, W_K, W_V):
        import jax, jax.numpy as jnp
        import numpy as np
        DIMS = 128
        HEADS = 16
        HEAD_DIM = DIMS // HEADS
        B, L, d = input_seq_embs.shape
        H, hd = (HEADS, HEAD_DIM)
        Q = (input_seq_embs @ W_Q.T).reshape(B, L, H, hd)
        K = (input_seq_embs @ W_K.T).reshape(B, L, H, hd)
        V = (input_seq_embs @ W_V.T).reshape(B, L, H, hd)
        sK = jax.nn.softmax(jnp.swapaxes(K, -1, -2), axis=-1)
        tran_V = jnp.einsum('bldh,blhe->blde', sK, V)
        out = jnp.einsum('blhd,blde->blhe', jax.nn.softmax(Q, axis=-1), tran_V)
        return out.reshape(B, L, d)

    def _L0_ffn_ref(x, w_gate, w_up, w_down):
        import jax, jax.numpy as jnp
        import numpy as np
        DIM = 128
        HIDDEN = 384
        SCALE = 1.0 / 127.0

        def _dequant(w_int, dtype):
            return w_int.astype(dtype) * jnp.asarray(SCALE, dtype)
        wg = _dequant(w_gate, x.dtype)
        wu = _dequant(w_up, x.dtype)
        wd = _dequant(w_down, x.dtype)
        gate = jnp.einsum('bsd,hd->bsh', x, wg)
        up = jnp.einsum('bsd,hd->bsh', x, wu)
        h = jax.nn.silu(gate) * up
        return jnp.einsum('bsh,dh->bsd', h, wd)

    def _L1_attn_ref(x, Wq, bq, Wk, bk, Wv, bv, Wo, bo):
        import math
        import jax, jax.numpy as jnp
        import numpy as np
        B, L, D_MODEL = (2, 256, 128)
        N_HEAD, HEAD_DIM = (16, 64)
        ATT_SCALE = 1.0
        b, l, _ = x.shape
        q = (x @ Wq + bq).reshape(b, l, N_HEAD, HEAD_DIM)
        k = (x @ Wk + bk).reshape(b, l, N_HEAD, HEAD_DIM)
        v = (x @ Wv + bv).reshape(b, l, N_HEAD, HEAD_DIM)
        scale = 1.0 / math.sqrt(HEAD_DIM ** ATT_SCALE)
        scores = jnp.einsum('blhd,bmhd->bhlm', q, k) * scale
        attn = jnp.einsum('bhlm,bmhd->blhd', scores, v)
        out = attn.reshape(b, l, N_HEAD * HEAD_DIM) @ Wo + bo
        return out

    def _L1_ffn_ref(hidden_states, router_w, w_gate, w_up, w_down, sw_gate, sw_up, sw_down, gate_w):
        import jax, jax.numpy as jnp
        import numpy as np
        B, S, D, F, E, K = (4, 256, 128, 256, 8, 2)
        bsz, seq_len, d = hidden_states.shape
        x = hidden_states.reshape(-1, d)
        T = x.shape[0]
        n_exp = router_w.shape[0]
        logits = x @ router_w.T
        probs = jax.nn.softmax(logits, axis=-1)
        rw, sel = jax.lax.top_k(probs, K)
        cw = jnp.zeros((T, n_exp), x.dtype).at[jnp.arange(T)[:, None], sel].set(rw)
        g = jnp.einsum('td,edf->etf', x, w_gate)
        u = jnp.einsum('td,edf->etf', x, w_up)
        h = jax.nn.silu(g) * u
        y = jnp.einsum('etf,efd->etd', h, w_down)
        moe_out = jnp.einsum('te,etd->td', cw, y)
        shared = jax.nn.silu(x @ sw_gate) * (x @ sw_up) @ sw_down
        gate = jax.nn.sigmoid(x @ gate_w.T)
        out = moe_out + gate * shared
        return out.reshape(bsz, seq_len, d)
    x = L0_attn_input_seq_embs
    mod = (_silu(L0_c) @ L0_wmod).reshape(L0_c.shape[0], 6, 1, -1)
    sa, ca, ga, sb, cb, gb = (mod[:, 0], mod[:, 1], mod[:, 2], mod[:, 3], mod[:, 4], mod[:, 5])
    ga = (2 * (ga >= 0) - 1) * jnp.maximum(jnp.abs(ga), 0.25)
    gb = (2 * (gb >= 0) - 1) * jnp.maximum(jnp.abs(gb), 0.25)
    h = _layernorm(x, axis=-1) * (1 + ca) + sa
    x = x + ga * _L0_attn_ref(h, L0_attn_W_Q, L0_attn_W_K, L0_attn_W_V)
    h = _layernorm(x, axis=-1) * (1 + cb) + sb
    x = x + gb * _L0_ffn_ref(h, L0_ffn_w_gate, L0_ffn_w_up, L0_ffn_w_down)
    mod = (_silu(L1_c) @ L1_wmod).reshape(L1_c.shape[0], 6, 1, -1)
    sa, ca, ga, sb, cb, gb = (mod[:, 0], mod[:, 1], mod[:, 2], mod[:, 3], mod[:, 4], mod[:, 5])
    ga = (2 * (ga >= 0) - 1) * jnp.maximum(jnp.abs(ga), 0.25)
    gb = (2 * (gb >= 0) - 1) * jnp.maximum(jnp.abs(gb), 0.25)
    h = _layernorm(x, axis=-1) * (1 + ca) + sa
    x = x + ga * _L1_attn_ref(h, L1_attn_Wq, L1_attn_bq, L1_attn_Wk, L1_attn_bk, L1_attn_Wv, L1_attn_bv, L1_attn_Wo, L1_attn_bo)
    h = _layernorm(x, axis=-1) * (1 + cb) + sb
    x = x + gb * _L1_ffn_ref(h, L1_ffn_router_w, L1_ffn_w_gate, L1_ffn_w_up, L1_ffn_w_down, L1_ffn_sw_gate, L1_ffn_sw_up, L1_ffn_sw_down, L1_ffn_gate_w)
    return x

_drawn_inputs = setup_inputs


def setup_inputs(seed=0):
    import zlib

    import numpy as np

    out = dict(_drawn_inputs(seed))
    spreads = {'L1_attn_bq': (0.0, 0.348), 'L1_attn_bk': (0.0, 0.1), 'L1_attn_bv': (0.0, 0.1)}
    factors = {'L1_attn_bo': 200.0,
     'L1_ffn_router_w': 50.099,
     'L1_ffn_w_gate': 50.562,
     'L1_ffn_w_up': 45.451,
     'L1_ffn_w_down': 45.475,
     'L1_ffn_sw_gate': 53.409,
     'L1_ffn_sw_up': 47.22,
     'L1_ffn_sw_down': 47.214,
     'L1_ffn_gate_w': 64.0}
    for name, (base, spread) in spreads.items():
        noise = np.random.default_rng([zlib.crc32(name.encode()), seed]).standard_normal(out[name].shape)
        drawn = base * np.exp(spread * noise) if base else spread * noise
        out[name] = jnp.asarray(drawn.astype(out[name].dtype))
    for name, factor in factors.items():
        out[name] = (out[name] * factor).astype(out[name].dtype)
    return out
```

```python
import concourse.bass as bass
from concourse import mybir
from contextlib import ExitStack
import numpy as np

F32 = mybir.dt.float32
F16 = mybir.dt.float16
I32 = mybir.dt.int32
U32 = mybir.dt.uint32
ALU = mybir.AluOpType
ACT = mybir.ActivationFunctionType
AX = mybir.AxisListType

TOKENS, D = 2048, 128
T = TOKENS // 128
PAIRS = T // 2
H0, HD0 = 16, 8
HID0 = 384
C0 = HID0 // 128
HW1 = 1024
C1 = HW1 // 128
SCALE1 = 1.0 / 8.0
FE, NE = 256, 8
SLOTS = 2 * T + NE - 1
EPS = 1e-5
GATHERS = 6


def constants():
    p = np.arange(128)
    ident = np.eye(128, dtype=np.float32)
    fold = np.concatenate([np.eye(64), np.eye(64)], 0).astype(np.float32)
    iota128 = np.tile(p.astype(np.float32), (128, 1))
    slot = np.tile(np.arange(SLOTS, dtype=np.float32), (128, 1))
    token = (np.arange(T)[None, :] * 128 + p[:, None]).astype(np.float32)
    first = np.tile(np.arange(8, 0, -1, dtype=np.float32), (128, 1))
    before = np.tile(np.tril(np.ones((8, 8)), -1).astype(np.float32).reshape(1, 64), (128, 1))
    pad_row = (3 * TOKENS + 128 * np.arange(SLOTS)[None, :] + p[:, None]).astype(np.float32)
    ones = np.ones((128, 128), np.float32)
    parts = dict(ident=ident, fold=fold, iota=iota128, slot=slot, token=token, first=first,
                 before=before, pad=pad_row, ones=ones)
    at, cols = {}, 0
    for name, a in parts.items():
        at[name] = (cols, cols + a.shape[1])
        cols += a.shape[1]
    tri = (p[:, None] < p[None, :]).astype(np.float16)
    half = np.concatenate([tri, np.ones((128, 128), np.float16)], 1)
    return np.concatenate(list(parts.values()), 1), at, half


def build(nc, x_in, wqkv0, wgu0, wd0, c0, wmod0, wq1, wk1, wv1, bqc1, bk1, bv1, wo1, bo1,
          router, wgu1, wd1, swgu1, swd1, c1, wmod1, const_f, const_h, out):
    _, at, _ = constants()
    z_dram = nc.dram_tensor("z_rows", [TOKENS, D], F32)
    y_dram = nc.dram_tensor("y_rows", [2 * TOKENS + 128 * SLOTS, D], F32)
    ctx = ExitStack()
    with ctx:
        def sb(name, shape, dt=F32):
            return ctx.enter_context(nc.sbuf_tensor(name, shape, dt))

        def ps(name, shape=(128, 512), dt=F32):
            return ctx.enter_context(nc.psum_tensor(name, list(shape), dt))

        def sem(name):
            return ctx.enter_context(nc.semaphore(name))

        ncf = max(b for _, b in at.values())
        CF = sb("CF", [128, ncf])
        CH = sb("CH", [128, 256], F16)

        def cf(name):
            a, b = at[name]
            return CF[:, a:b]
        ident, fold, iota, slot_iota = cf("ident"), cf("fold"), cf("iota"), cf("slot")
        token_id, first_w, before, pad_row, ones = cf("token"), cf("first"), cf("before"), cf("pad"), cf("ones")
        tri_h, ones_h = CH[:, 0:128], CH[:, 128:256]
        minus_half = sb("minus_half", [128, T])
        X = sb("X", [128, T, D])
        WQKV0 = sb("WQKV0", [128, 3 * D])
        WGU0i = sb("WGU0i", [128, 2 * HID0], I32)
        WGU0 = sb("WGU0", [128, 2 * HID0])
        WD0i = sb("WD0i", [128, HID0], I32)
        WD0g = sb("WD0g", [128, HID0])
        WD0 = sb("WD0", [128, C0, D])
        CM = sb("CM", [128, 2])
        SC = sb("SC", [128, 2])
        WM = sb("WM", [128, 2, 6 * D])
        MOD = sb("MOD", [128, 2, 6])
        ONEC = sb("ONEC", [128, 2, 2])
        GT = sb("GT", [128, 2, 2])
        GA = sb("GA", [128, 2, 2])
        GS = sb("GS", [128, 2, 2])
        W1 = sb("W1", [128, 3, HW1])
        W1s = sb("W1s", [128, 3, HW1])
        WQT = sb("WQT", [128, C1, D + 1])
        WO1 = sb("WO1", [128, C1, D])
        BQC = sb("BQC", [128, C1])
        BKV = sb("BKV", [1, 2, HW1])
        BKVs = sb("BKVs", [1, 2, HW1])
        BO = sb("BO", [128, 1])
        RT = sb("RT", [128, NE + 1])
        WGU1 = sb("WGU1", [128, NE, 2 * FE])
        WD1 = sb("WD1", [128, NE + 1, 2, D])
        WD1g = sb("WD1g", [128, NE + 1, 2, D])
        SGU = sb("SGU", [128, 2 * FE])
        DG = sb("DG", [128, 128])
        GBB = sb("GBB", [128, D])

        ST = sb("ST", [128, T, 6])
        MV = sb("MV", [128, 4, T, 2])
        VE = sb("VE", [128, 4, T])
        RS = sb("RS", [128, 4, T])
        Z = sb("Z", [128, 2, 2, D])
        HT = sb("HT", [128, 2, 256])
        QKV = sb("QKV", [128, 2, 2, 3 * D])
        MX = sb("MX", [128, 2, 48])
        S0 = sb("S0", [128, 2, 2, 2 * D])
        E0 = sb("E0", [128, 2, 2, 2 * D])
        SM = sb("SM", [128, 2, 48])
        RC = sb("RC", [128, 2, 48])
        QH = sb("QH", [128, 2, 2, D])
        QN = sb("QN", [128, 2, 2, D])
        P1 = sb("P1", [128, 2, 1024])
        P2 = sb("P2", [128, 2, 1024])
        TVT = sb("TVT", [128, 2, 128])
        TV = sb("TV", [128, 2, 64])
        AT = sb("AT", [128, 2, 128])
        Z2 = sb("Z2", [128, 2, D])
        H2T = sb("H2T", [128, 256])
        SG = sb("SG", [128, C0 * 256])
        HID = sb("HID", [128, C0 * 256])
        Z3 = sb("Z3", [128, T, D + 1])
        Z3T = sb("Z3T", [128, TOKENS])
        GZ = sb("GZ", [128, D + 1])
        MROW = sb("MROW", [1, 128])
        NTOK = sb("NTOK", [1, 1])
        A1 = sb("A1", [128, HW1])
        A1b = sb("A1b", [1, HW1])
        KV = sb("KV", [128, C1, 128])
        DO = sb("DO", [128, C1, 128])
        MT = sb("MT", [128, D + 1])
        MC = sb("MC", [128, 2 * D])
        BOG = sb("BOG", [128, 1])
        Z4 = Z3[:, :, 0:D]
        H4T = Z3T
        LG = sb("LG", [128, T, NE + 1])
        GATE = sb("GATE", [128, T])
        SS = [QKV[:, 0, :, :].rearrange("p t c -> p (t c)")[:, 0:512], QKV[:, 1, :, :].rearrange("p t c -> p (t c)")[:, 0:512]]
        HS = [S0[:, :, :, :].rearrange("p a b c -> p (a b c)"), E0[:, :, :, :].rearrange("p a b c -> p (a b c)")]
        PR = sb("PR", [128, T, NE])
        PX = sb("PX", [128, T, NE])
        RM = sb("RM", [128, T])
        RSUM = sb("RSUM", [128, T])
        WK = sb("WK", [128, 2, T])
        OH = sb("OH", [128, 2, T, NE])
        SCR = sb("SCR", [128, T, NE])
        MH = sb("MH", [128, T + 1, NE], F16)
        RK = sb("RK", [128, T + 1, NE])
        NTI = sb("NTI", [128, NE], I32)
        NTF = sb("NTF", [128, NE])
        STT = sb("STT", [128, NE, NE])
        START = sb("START", [128, NE])
        ENDT = sb("ENDT", [128, NE])
        SLOT = sb("SLOT", [128, 2 * T])
        SLI = sb("SLI", [128, 2 * T], I32)
        TLI = sb("TLI", [128, 2 * T], I32)
        RWI = sb("RWI", [128, 2 * T], I32)
        TLF = sb("TLF", [128, 2 * T])
        RWF = sb("RWF", [128, 2 * T])
        BH = P1[:, :, :].rearrange("p a b -> p (a b)").bitcast(F16).rearrange("p (k r) -> p k r", r=128)
        AH = P2[:, :, :].rearrange("p a b -> p (a b)").bitcast(F16)[:, 0:2 * T * 2 * SLOTS]\
            .rearrange("p (k c) -> p k c", c=2 * SLOTS)
        IDX = sb("IDX", [128, 2 * SLOTS])
        GI = sb("GI", [128, SLOTS], I32)
        PADF = sb("PADF", [128, SLOTS])
        DF = sb("DF", [128, SLOTS])
        DI = sb("DI", [128, SLOTS], I32)
        GEQ = sb("GEQ", [1, SLOTS, NE])
        EXF = sb("EXF", [1, SLOTS])
        EXI = sb("EXI", [1, SLOTS], I32)
        W1f = W1[:, :, :].rearrange("p a b -> p (a b)")
        GX = [W1f[:, 128 * b:128 * b + 128] for b in range(GATHERS)]
        YX = [W1f[:, 768 + 128 * b:896 + 128 * b] for b in range(GATHERS)]
        XT = [W1f[:, 1536 + 128 * b:1664 + 128 * b] for b in range(2)]
        SX = [W1f[:, 1792 + 256 * b:2048 + 256 * b] for b in range(2)]
        HX = [W1f[:, 2304 + 256 * b:2560 + 256 * b] for b in range(2)]
        HXT = [A1[:, 256 * b:256 * b + 256] for b in range(2)]
        YB = [a.rearrange("p (k t d) -> p k t d", k=2, t=4) for a in
              (W1s[:, 0, :], W1s[:, 1, :], W1s[:, 2, :], WO1[:, :, :].rearrange("p c d -> p (c d)"))]

        B = [ps(f"bank{i}") for i in range(8)]

        s_cf, s_x, s_w0, s_wi, s_c, s_w1, s_we = (sem(n) for n in
            ("const_in", "x_in", "w0_in", "w0int_in", "c_in", "w1_in", "we_in"))
        s = {}

        def S(name):
            if name not in s:
                s[name] = sem(name)
            return s[name]

        blk = ctx.enter_context(nc.Block())

        xv = x_in.rearrange("(t p) d -> p t d", p=128)
        outv = out.rearrange("(t p) d -> p t d", p=128)

        @blk.sync
        def _(sp):
            for g in range(4):
                sp.dma_start(X[:, 4 * g:4 * g + 4, :], xv[:, 4 * g:4 * g + 4, :]).then_inc(S(f"x_in{g}"), 16)
            sp.dma_start(CF[:, :], const_f).then_inc(s_cf, 16)
            sp.dma_start(WQKV0[:, :], wqkv0).then_inc(s_w0, 16)
            sp.dma_start(WGU0i[:, :], wgu0).then_inc(s_wi, 16)
            for w, src in enumerate((wq1, wk1, wv1)):
                sp.dma_start(W1[:, w, :], src).then_inc(s_w1, 16)
            sp.dma_start(WO1[:, :, :], wo1.rearrange("(c p) d -> p c d", p=128)).then_inc(s_w1, 16)
            sp.dma_start(BQC[:, :], bqc1).then_inc(s_w1, 16)
            sp.dma_start(BKV[0:1, 0, :], bk1).then_inc(s_w1, 16)
            sp.dma_start(BKV[0:1, 1, :], bv1).then_inc(s_w1, 16)
            sp.dma_start(BO[:, :], bo1).then_inc(s_w1, 16)
            sp.dma_start(CH[:, :], const_h).then_inc(s_we, 16)
            sp.dma_start(RT[:, :], router).then_inc(s_we, 16)
            sp.dma_start(SGU[:, :], swgu1).then_inc(s_we, 16)
            sp.dma_start(WGU1[:, :, :], wgu1).then_inc(s_we, 16)
            sp.dma_start(WD1[:, 0:NE, :, :], wd1).then_inc(s_we, 16)
            sp.dma_start(WD1[:, NE, :, :], swd1).then_inc(s_we, 16)
            zv = z_dram.ap().rearrange("(t p) d -> p t d", p=128)
            for g in range(4):
                sp.wait_ge(S("z4"), 4 * g + 4)
                sp.dma_start(zv[:, 4 * g:4 * g + 4, :], Z4[:, 4 * g:4 * g + 4, :]).then_inc(S("z_rows"), 16)
            for b in range(GATHERS):
                sp.wait_ge(S(f"scattered{b}"), 16 * len(range(b, SLOTS, GATHERS)))
            yv = y_dram.ap()[0:2 * TOKENS, :].rearrange("(k t p) d -> p k t d", p=128, k=2)
            for g in range(4):
                for k in range(2):
                    sp.dma_start(YB[g][:, k, :, :], yv[:, k, 4 * g:4 * g + 4, :]).then_inc(S(f"y_in{g}"), 16)
            for g in range(4):
                sp.wait_ge(S("x5"), 4 * g + 4)
                sp.dma_start(outv[:, 4 * g:4 * g + 4, :], X[:, 4 * g:4 * g + 4, :]).then_inc(S("out"), 16)
            sp.wait_ge(S("out"), 64)

        def lead(i):
            return [i + k if 0 <= i + k < PAIRS else None for k in (2, 1, 0, -1, -2)]

        STEPS = range(-2, PAIRS + 2)

        def heads(ap):
            return ap.rearrange("p t (h d) -> p t h d", d=HD0)

        def p1_out(j, a, b):
            return P1[:, j, 64 * a:64 * b].rearrange("p (h d e) -> p h d e", d=HD0, e=HD0)

        def p1_k(q, j, a, b):
            e = E0[:, q, j, D + HD0 * a:D + HD0 * b].rearrange("p (h d) -> p h d", d=HD0)
            return e.unsqueeze(3).broadcast_to([128, b - a, HD0, HD0])

        def p1_v(q, j, a, b):
            v = QKV[:, q, j, 2 * D + HD0 * a:2 * D + HD0 * b].rearrange("p (h e) -> p h e", e=HD0)
            return v.unsqueeze(2).broadcast_to([128, b - a, HD0, HD0])

        def p2_out(j, a, b):
            return P2[:, j, 128 * a:128 * b].rearrange("p (d h e) -> p d h e", h=H0, e=HD0)

        def p2_q(q, j, a, b):
            v = QN[:, q, j, :].rearrange("p (h d) -> p d h", d=HD0)[:, a:b, :]
            return v.unsqueeze(3).broadcast_to([128, b - a, H0, HD0])

        def p2_t(j, a, b):
            v = TV[:, j, :].rearrange("p (d e) -> p d e", e=HD0)[:, a:b, :]
            return v.unsqueeze(2).broadcast_to([128, b - a, H0, HD0])

        K1, K2 = 12, 6

        @blk.scalar
        def _(act):
            act.dma_start(CM[:, 0:1], c0).then_inc(s_c, 16)
            act.dma_start(CM[:, 1:2], c1).then_inc(s_c, 16)
            act.dma_start(WM[:, 0, :], wmod0).then_inc(s_c, 16)
            act.dma_start(WM[:, 1, :], wmod1).then_inc(s_c, 16)
            act.dma_start(WD0i[:, :], wd0).then_inc(s_c, 16)
            act.wait_ge(s_c, 80)
            nc.scalar.activation(SC[:, :], CM[:, :], ACT.Silu).then_inc(S("silu_c"), 1)
            act.wait_ge(S("mod_ps"), 1)
            nc.scalar.activation(MOD[:, :, :], B[5][:, 0:12].rearrange("p (l m) -> p l m", l=2), ACT.Copy)\
                .then_inc(S("mod_sb"), 1)

            def front_hT(p):
                act.wait_ge(S("zT_ps"), p + 1)
                if p == 0:
                    act.wait_ge(S("one_c"), 1)
                    act.wait_ge(S("mod_sb"), 1)
                nc.scalar.activation(HT[:, p % 2, :], B[0][:, 0:256], ACT.Identity, bias=MOD[:, 0, 0:1],
                                     scale=ONEC[:, 0, 0:1]).then_inc(S("hT"), 1)

            def front_qkv(p):
                act.wait_ge(S("qkv_ps"), p + 1)
                if p >= 2:
                    act.wait_ge(S("p1d"), 2 * (p - 1))
                    act.wait_ge(S("p1p"), 2 * (p - 1))
                for j in range(2):
                    nc.scalar.activation(QKV[:, p % 2, j, :], B[j][:, 0:3 * D], ACT.Copy).then_inc(S("qkv_sb"), 1)

            def front_exp(p):
                act.wait_ge(S("sub"), 2 * (p + 1))
                nc.scalar.activation(E0[:, p % 2, :, :], S0[:, p % 2, :, :], ACT.Exp).then_inc(S("exp"), 1)

            def mid_tvT(p, j):
                act.wait_ge(S("tvT_ps"), 2 * p + j + 1)
                nc.scalar.activation(TVT[:, j, :], B[3 + j][:, 0:128], ACT.Copy).then_inc(S("tvT"), 1)

            def mid_tv(p, j):
                act.wait_ge(S("tv_ps"), 2 * p + j + 1)
                if p >= 1:
                    act.wait_ge(S("p2p"), 2 * p - 1 + j)
                    act.wait_ge(S("p2d"), 2 * p - 1 + j)
                nc.scalar.activation(TV[:, j, :], B[3 + j][:, 128:192], ACT.Copy)\
                    .then_inc(S("tv"), 1)

            def mid_aT(p, j):
                act.wait_ge(S("aT_ps"), 2 * p + j + 1)
                if p == 0 and j == 0:
                    act.wait_ge(S("gate_ok"), 1)
                nc.scalar.activation(AT[:, j, :], B[3 + j][:, 192:320], ACT.Identity,
                                     scale=GT[:, 0, 0:1]).then_inc(S("aT"), 1)

            def back_h2T(p):
                act.wait_ge(S("z2T_ps"), p + 1)
                nc.scalar.activation(H2T[:, :], B[2][:, 256:512], ACT.Identity, bias=MOD[:, 0, 3:4],
                                     scale=ONEC[:, 0, 1:2]).then_inc(S("h2T"), 1)

            def back_silu(p):
                act.wait_ge(S("gu_ps"), 3 * p + 1)
                if p >= 1:
                    act.wait_ge(S("hid"), 2 * p)
                nc.scalar.activation(SG[:, 0:512], B[5][:, :], ACT.Silu, scale=1.0 / 127.0).then_inc(S("silu"), 1)
                act.wait_ge(S("gu_ps"), 3 * p + 2)
                nc.scalar.activation(SG[:, 512:768], B[6][:, 0:256], ACT.Silu, scale=1.0 / 127.0)\
                    .then_inc(S("silu"), 1)

            for i in STEPS:
                n, f, m, b, _ = lead(i)
                if f is not None:
                    front_qkv(f)
                if b is not None:
                    back_h2T(b)
                if m is not None:
                    mid_tvT(m, 0)
                    mid_tvT(m, 1)
                    mid_tv(m, 0)
                    mid_tv(m, 1)
                if f is not None:
                    front_exp(f)
                if i == -1:
                    act.wait_ge(S("gate_ok"), 1)
                    nc.scalar.activation(WD0g[:, :], WD0i[:, :], ACT.Identity, scale=GT[:, 0, 1:2])\
                        .then_inc(S("wd0_scaled"), 1)
                    act.wait_ge(S("wd0_ps"), 1)
                    nc.scalar.activation(WD0[:, :, :], B[7][:, 0:384].rearrange("p (c d) -> p c d", c=C0),
                                         ACT.Copy, scale=1.0 / (127.0 * 127.0)).then_inc(S("wd0_ok"), 1)
                if b is not None:
                    back_silu(b)
                if m is not None:
                    mid_aT(m, 0)
                    mid_aT(m, 1)
                if n is not None:
                    front_hT(n)
                if i == 0:
                    act.wait_ge(S("prep_ps"), 1)
                    for h in range(2):
                        nc.scalar.activation(WQT[:, 4 * h:4 * h + 4, 0:128],
                                             B[5 + h][:, :].rearrange("p (c d) -> p c d", c=4), ACT.Copy)\
                            .then_inc(S("prep_sb"), 1)

            for g in range(4):
                act.wait_ge(S("z3T_ps"), g + 1)
                nc.scalar.activation(Z3T[:, 512 * g:512 * g + 512], B[(2, 7)[g % 2]][:, :], ACT.Copy)\
                    .then_inc(S("z3T"), 1)
                if g == 1:
                    act.wait_ge(S("a_ps"), 1)
                    nc.scalar.activation(A1[:, 0:512], B[0][:, :], ACT.Copy).then_inc(S("a_sb"), 1)
                    act.wait_ge(S("a_ps"), 3)
                    nc.scalar.activation(A1b[0:1, 0:512], B[3][0:1, :], ACT.Copy).then_inc(S("a_sb"), 1)
            act.wait_ge(S("kv_zero"), 1)
            act.wait_ge(S("kv_ps"), 1)
            act.wait_ge(S("a_sb"), 2)
            for lo in (0, 64):
                nc.scalar.activation(KV[lo:lo + 64, 0:4, lo:lo + 64],
                                     B[5][lo:lo + 64, :].rearrange("p (c k) -> p c k", c=4)[:, :, lo:lo + 64],
                                     ACT.Copy).then_inc(S("kv_sb_a"), 1)
            act.wait_ge(S("do_ps"), 1)
            nc.scalar.activation(DO[:, 0:4, :], B[0][:, :].rearrange("p (c d) -> p c d", c=4), ACT.Copy)\
                .then_inc(S("do_sb_a"), 1)
            act.wait_ge(S("mc_ps"), 1)
            nc.scalar.activation(MC[:, :], B[4][:, 0:256], ACT.Copy).then_inc(S("mc"), 1)
            for g in range(4):
                act.wait_ge(S("h4T_ps"), g + 1)
                nc.scalar.activation(H4T[:, 512 * g:512 * g + 512], B[2 + g % 2][:, :], ACT.Identity,
                                     bias=MOD[:, 1, 3:4], scale=ONEC[:, 1, 1:2]).then_inc(S("h4T"), 1)

            def shared_silu(n):
                act.wait_ge(S("sgu_ps"), n + 1)
                if n >= 2:
                    act.wait_ge(S("shid"), n - 1)
                nc.scalar.activation(SS[n % 2], B[(5, 7)[n % 2]][:, :], ACT.Silu).then_inc(S("ssilu"), 1)

            act.wait_ge(S("rt_sub"), 1)
            nc.scalar.activation(PX[:, :, :], PR[:, :, :], ACT.Exp).then_inc(S("rt_exp"), 1)
            nc.scalar.activation(GATE[:, :], LG[:, :, NE], ACT.Exp, scale=-1.0).then_inc(S("gate_e"), 1)
            for n in range(8):
                shared_silu(n)

            def expert_x(j):
                act.wait_ge(S("xt_ps"), j + 1)
                if j >= 2:
                    act.wait_ge(S("egu_ps"), j - 1)
                nc.scalar.activation(XT[j % 2], B[j % 2][:, 0:128], ACT.Identity, bias=MOD[:, 1, 3:4],
                                     scale=ONEC[:, 1, 1:2]).then_inc(S("xt"), 1)

            def expert_silu(j):
                act.wait_ge(S("egu_ps"), j + 1)
                if j >= 2:
                    act.wait_ge(S("ehid"), j - 1)
                nc.scalar.activation(SX[j % 2], B[2 + j % 2][:, 0:FE], ACT.Silu).then_inc(S("esilu"), 1)

            for j in range(-2, SLOTS):
                if j + 2 < SLOTS:
                    expert_x(j + 2)
                if 0 <= j + 1 < SLOTS:
                    expert_silu(j + 1)

        @blk.tensor
        def _(pe):
            mm = nc.tensor.matmul
            pe.wait_ge(S("silu_c"), 1)
            for l in range(2):
                for m in range(6):
                    last = mm(B[5][:, 6 * l + m:6 * l + m + 1], WM[:, l, D * m:D * m + D], SC[:, l:l + 1],
                              start=True, stop=True)
            last.then_inc(S("mod_ps"), 1)
            pe.wait_ge(s_cf, 16)

            def front(p):
                for j in range(2):
                    pe.wait_ge(S("z"), 2 * p + j + 1)
                    if p >= 1 and j == 0:
                        pe.wait_ge(S("qkv_sb"), 2 * p)
                    last = mm(B[0][:, 128 * j:128 * j + 128], Z[:, p % 2, j, :], ident, start=True, stop=True,
                              is_transpose=True)
                last.then_inc(S("zT_ps"), 1)

            def front_qkv(p):
                pe.wait_ge(S("hT"), p + 1)
                if p == 0:
                    pe.wait_ge(s_w0, 16)
                else:
                    pe.wait_ge(S("qkv_sb"), 2 * p)
                for j in range(2):
                    last = mm(B[j][:, 0:3 * D], HT[:, p % 2, 128 * j:128 * j + 128], WQKV0[:, :],
                              start=True, stop=True)
                last.then_inc(S("qkv_ps"), 1)

            def mid_sum_heads(p, j):
                pe.wait_ge(S("p1d"), 2 * p + j + 1)
                pe.wait_ge(S("p1p"), 2 * p + j + 1)
                if p >= 1:
                    pe.wait_ge(S("x1"), 2 * (p - 1) + j + 1)
                for n in range(8):
                    last = mm(B[3 + j][:, 0:128], P1[:, j, 128 * n:128 * n + 128], ident,
                              start=(n == 0), stop=(n == 7), is_transpose=True)
                last.then_inc(S("tvT_ps"), 1)

            def mid_fold(p, j):
                pe.wait_ge(S("tvT"), 2 * p + j + 1)
                mm(B[3 + j][:, 128:192], TVT[:, j, :], fold, start=True, stop=True)\
                    .then_inc(S("tv_ps"), 1)

            def mid_sum_d(p, j):
                pe.wait_ge(S("p2d"), 2 * p + j + 1)
                pe.wait_ge(S("p2p"), 2 * p + j + 1)
                for n in range(8):
                    last = mm(B[3 + j][:, 192:320], P2[:, j, 128 * n:128 * n + 128], ident,
                              start=(n == 0), stop=(n == 7), is_transpose=True)
                last.then_inc(S("aT_ps"), 1)

            def mid_back(p, j):
                pe.wait_ge(S("aT"), 2 * p + j + 1)
                mm(B[3 + j][:, 320:448], AT[:, j, :], ident, start=True, stop=True,
                   is_transpose=True).then_inc(S("aB_ps"), 1)

            def back_T(p):
                for j in range(2):
                    pe.wait_ge(S("z2"), 2 * p + j + 1)
                    if p >= 1 and j == 0:
                        pe.wait_ge(S("x2"), p)
                    last = mm(B[2][:, 256 + 128 * j:384 + 128 * j], Z2[:, j, :], ident, start=True, stop=True,
                              is_transpose=True)
                last.then_inc(S("z2T_ps"), 1)

            def back_gu(p):
                pe.wait_ge(S("h2T"), p + 1)
                if p == 0:
                    pe.wait_ge(S("w0_cast"), 1)
                else:
                    pe.wait_ge(S("silu"), 2 * p)
                    pe.wait_ge(S("hid"), 2 * p)
                for n, w in enumerate((0, 1, 2, 5, 3, 4)):
                    last = mm(B[5 + n // 2][:, 256 * (n % 2):256 * (n % 2) + 256],
                              WGU0[:, 128 * w:128 * w + 128], H2T[:, :], start=True, stop=True)
                    if n % 2:
                        last.then_inc(S("gu_ps"), 1)

            def back_down(p):
                pe.wait_ge(S("hid"), 2 * (p + 1))
                if p == 0:
                    pe.wait_ge(S("wd0_ok"), 1)
                for j in range(2):
                    for n in range(C0):
                        last = mm(B[2][:, 256 + 128 * j:384 + 128 * j],
                                  HID[:, 256 * n + 128 * j:256 * n + 128 * j + 128], WD0[:, n, :],
                                  start=(n == 0), stop=(n == C0 - 1))
                last.then_inc(S("y_ps"), 1)

            for i in STEPS:
                n, f, m, b, _ = lead(i)
                if f is not None:
                    front_qkv(f)
                if m is not None:
                    mid_sum_heads(m, 0)
                if b is not None:
                    back_T(b)
                if m is not None:
                    mid_sum_heads(m, 1)
                    mid_fold(m, 0)
                    mid_fold(m, 1)
                if i == -1:
                    pe.wait_ge(S("wd0_scaled"), 1)
                    for c in range(C0):
                        last = mm(B[7][:, 128 * c:128 * c + 128], WD0g[:, 128 * c:128 * c + 128], ident,
                                  start=True, stop=True, is_transpose=True)
                    last.then_inc(S("wd0_ps"), 1)
                    pe.wait_ge(S("wd0_ok"), 1)
                if b is not None:
                    back_gu(b)
                if m is not None:
                    mid_sum_d(m, 0)
                    mid_sum_d(m, 1)
                if n is not None:
                    front(n)
                if m is not None:
                    mid_back(m, 0)
                    mid_back(m, 1)
                if b is not None:
                    back_down(b)
                if i == 0:
                    pe.wait_ge(S("w1_scaled"), 3)
                    pe.wait_ge(S("diag_gb"), 1)
                    for c in range(C1):
                        last = mm(B[5 + c // 4][:, 128 * (c % 4):128 * (c % 4) + 128],
                                  W1s[:, 0, 128 * c:128 * c + 128], ident, start=True, stop=True, is_transpose=True)
                    last.then_inc(S("prep_ps"), 1)
                    for c in range(C1):
                        mm(B[7][:, c:c + 1], W1[:, 0, 128 * c:128 * c + 128], MOD[:, 1, 0:1], start=True, stop=True)
                    mm(B[7][:, 128:256], ones, DG[:, :], start=True, stop=True).then_inc(S("prep_ps"), 1)
                if i == 0:
                    pe.wait_ge(S("prep_sb"), 2)
                    pe.wait_ge(S("gbb_sb"), 2)

            pe.wait_ge(S("x1"), T)
            pe.wait_ge(S("qkv_sb"), T)
            pe.wait_ge(S("one_c"), 1)
            for n, bank in enumerate((0, 1, 3, 4)):
                mm(B[bank][0:1, :], MOD[:, 1, 0:1], W1[:, 1 + n // 2, 512 * (n % 2):512 * (n % 2) + 512],
                   start=True, stop=True).then_inc(S("brow_ps"), 1)
            pe.wait_ge(S("z3"), T)
            pe.wait_ge(S("z3_ones"), 1)
            for t in range(T):
                last = mm(B[5][:, 0:D + 1], Z3[:, t, 0:D], Z3[:, t, :], start=(t == 0), stop=(t == T - 1))
            last.then_inc(S("g_all"), 1)

            def z3T(g):
                if g >= 2:
                    pe.wait_ge(S("z3T"), g - 1)
                for t in range(4 * g, 4 * g + 4):
                    last = mm(B[(2, 7)[g % 2]][:, 128 * (t % 4):128 * (t % 4) + 128], Z3[:, t, 0:D], ident,
                              start=True, stop=True, is_transpose=True)
                last.then_inc(S("z3T_ps"), 1)

            z3T(0)
            z3T(1)
            pe.wait_ge(S("gz"), 1)
            mm(B[6][0:1, 0:128], GZ[:, D:D + 1], ident, start=True, stop=True).then_inc(S("mrow_ps"), 1)
            pe.wait_ge(S("brow_sb"), 4)
            pe.wait_ge(S("mrow"), 1)
            pe.wait_ge(S("kv_zero"), 1)
            for n in range(2):
                cols = slice(512 * n, 512 * n + 512)
                mm(B[n][:, :], GZ[:, 0:D], W1s[:, 2, cols], start=True, stop=False)
                mm(B[n][:, :], MROW[0:1, :], BKVs[0:1, 1, cols], start=False, stop=True).then_inc(S("a_ps"), 1)
            for n in range(2):
                cols = slice(512 * n, 512 * n + 512)
                mm(B[3 + n][0:1, :], GZ[:, D:D + 1], W1s[:, 2, cols], start=True, stop=False)
                mm(B[3 + n][0:1, :], NTOK[0:1, 0:1], BKVs[0:1, 1, cols], start=False, stop=True)\
                    .then_inc(S("a_ps"), 1)
            z3T(2)
            z3T(3)
            pe.wait_ge(S("a_sb"), 2)
            pe.wait_ge(S("a_sb_d"), 2)
            for c in range(C1):
                cols = slice(128 * c, 128 * c + 128)
                o = B[5 + c // 4][:, 128 * (c % 4):128 * (c % 4) + 128]
                mm(o, A1[:, cols], W1s[:, 1, cols], start=True, stop=False)
                last = mm(o, A1b[0:1, cols], BKVs[0:1, 0, cols], start=False, stop=True)
                if c % 4 == 3:
                    last.then_inc(S("kv_ps"), 1)
            for c in range(C1):
                if c == 0:
                    pe.wait_ge(S("kv_sb_a"), 2)
                if c == 4:
                    pe.wait_ge(S("kv_sb_d"), 2)
                last = mm(B[c // 4][:, 128 * (c % 4):128 * (c % 4) + 128], KV[:, c, :], WO1[:, c, :],
                          start=True, stop=True)
                if c % 4 == 3:
                    last.then_inc(S("do_ps"), 1)
            for c in range(C1):
                if c == 0:
                    pe.wait_ge(S("do_sb_a"), 1)
                if c == 4:
                    pe.wait_ge(S("do_sb_d"), 1)
                last = mm(B[3][:, 0:D + 1], DO[:, c, :], WQT[:, c, :], start=(c == 0), stop=(c == C1 - 1))
            last.then_inc(S("mt_ps"), 1)
            pe.wait_ge(S("mt_step"), 3)
            mm(B[4][:, 0:128], MT[:, 0:128], ident, start=True, stop=True, is_transpose=True)
            mm(B[4][:, 128:256], ones, DG[:, :], start=True, stop=True).then_inc(S("mc_ps"), 1)

            def attend(g):
                if g == 0:
                    pe.wait_ge(S("mc"), 1)
                    pe.wait_ge(S("z3T"), 4)
                else:
                    if g >= 2:
                        pe.wait_ge(S("x3"), g - 1)
                for t in range(4 * g, 4 * g + 4):
                    last = mm(B[g % 2][:, 128 * (t % 4):128 * (t % 4) + 128], Z3T[:, 128 * t:128 * t + 128],
                              MC[:, 0:D], start=True, stop=True)
                last.then_inc(S("o_ps"), 1)

            def h4T(g):
                if g >= 2:
                    pe.wait_ge(S("h4T"), g - 1)
                pe.wait_ge(S("z4"), 4 * g + 4)
                for t in range(4 * g, 4 * g + 4):
                    last = mm(B[2 + g % 2][:, 128 * (t % 4):128 * (t % 4) + 128], Z4[:, t, :], ident,
                              start=True, stop=True, is_transpose=True)
                last.then_inc(S("h4T_ps"), 1)

            def logits(g):
                pe.wait_ge(S("h4T"), g + 1)
                for t in range(4 * g, 4 * g + 4):
                    last = mm(B[4][:, 9 * t:9 * t + 9], H4T[:, 128 * t:128 * t + 128], RT[:, :],
                              start=True, stop=True)
                last.then_inc(S("lg_ps"), 1)

            pe.wait_ge(s_we, 96)
            for g in range(6):
                if g < 4:
                    attend(g)
                if g >= 1 and g - 1 < 4:
                    h4T(g - 1)
                if g >= 2:
                    logits(g - 2)

            def shared_gu(n):
                g, f = n // 2, n % 2
                if n >= 2:
                    pe.wait_ge(S("ssilu"), n - 1)
                    pe.wait_ge(S("shid"), n - 1)
                if n == 1:
                    pe.wait_ge(S("x3"), 4)
                cols = slice(512 * g, 512 * g + 512)
                mm(B[(5, 7)[n % 2]][:, :], SGU[:, 128 * f:128 * f + 128], H4T[:, cols], start=True, stop=True)
                mm(B[(6, 0)[n % 2]][:, :], SGU[:, FE + 128 * f:FE + 128 * f + 128], H4T[:, cols],
                   start=True, stop=True).then_inc(S("sgu_ps"), 1)

            def shared_down(g):
                pe.wait_ge(S("shid"), 2 * g + 2)
                if g >= 2:
                    pe.wait_ge(S("x4"), 4 * (g - 1))
                for t in range(4):
                    for f in range(2):
                        last = mm(B[(1, 3)[g % 2]][:, 128 * t:128 * t + 128],
                                  HS[g % 2][:, 512 * f + 128 * t:512 * f + 128 * t + 128], WD1g[:, NE, f, :],
                                  start=(f == 0), stop=(f == 1))
                last.then_inc(S("sy_ps"), 1)

            def ranks():
                pe.wait_ge(S("picked"), 1)
                M = MH[:, :, :].rearrange("p t e -> p (t e)")
                for n in range(T + 1):
                    if n == 0:
                        mm(B[2][:, 0:8 * T + 8], tri_h, M, start=True, stop=False)
                    else:
                        last = mm(B[2][:, 8 * n:8 * T + 8], ones_h, M[:, 0:8 * (T + 1 - n)],
                                  start=False, stop=(n == T))
                last.then_inc(S("rank_ps"), 1)

            def places():
                pe.wait_ge(S("onehots"), 1)
                for n in range(2 * T):
                    last = mm(B[4][:, 0:2 * SLOTS], BH[:, n, :], AH[:, n, :], start=(n == 0), stop=(n == 2 * T - 1))
                last.then_inc(S("idx_ps"), 1)

            pe.wait_ge(S("wd1_scaled"), 1)
            shared_gu(0)
            shared_gu(1)
            shared_gu(2)
            shared_gu(3)
            shared_down(0)
            ranks()
            shared_gu(4)
            shared_down(1)
            shared_gu(5)
            shared_gu(6)
            shared_down(2)
            shared_gu(7)
            places()
            shared_down(3)

            def expert_x(j):
                pe.wait_ge(S(f"gathered{j % GATHERS}"), 16 * (j // GATHERS + 1))
                if j >= 2:
                    pe.wait_ge(S("xt"), j - 1)
                mm(B[j % 2][:, 0:128], GX[j % GATHERS], ident, start=True, stop=True, is_transpose=True)\
                    .then_inc(S("xt_ps"), 1)

            def expert_gu(j, e):
                pe.wait_ge(S("xt"), j + 1)
                if j >= 2:
                    pe.wait_ge(S("ehid"), j - 1)
                w = WGU1[:, :, :].rearrange("p e f -> p (e f)")
                mm(B[2 + j % 2][:, :], XT[j % 2], w[:, bass.ds(e * (2 * FE), 2 * FE)], start=True, stop=True)\
                    .then_inc(S("egu_ps"), 1)

            def expert_hT(j):
                pe.wait_ge(S("ehid"), j + 1)
                if j >= 2:
                    pe.wait_ge(S("ht"), j - 1)
                for f in range(2):
                    last = mm(B[4 + j % 2][:, 128 * f:128 * f + 128], HX[j % 2][:, 128 * f:128 * f + 128], ident,
                              start=True, stop=True, is_transpose=True)
                last.then_inc(S("ht_ps"), 1)

            def expert_down(j, e):
                pe.wait_ge(S("ht"), j + 1)
                if j >= 2:
                    pe.wait_ge(S("ey"), j - 1)
                w = WD1g[:, :, :, :].rearrange("p e f d -> p (e f d)")
                for f in range(2):
                    last = mm(B[6 + j % 2][:, 0:128], HXT[j % 2][:, 128 * f:128 * f + 128],
                              w[:, bass.ds(e * (2 * D) + f * D, D)], start=(f == 0), stop=(f == 1))
                last.then_inc(S("ey_ps"), 1)

            pe.wait_ge(S("idx"), 1)
            pe.wait_ge(S("x4"), T)
            held = {}
            for j in range(-2, SLOTS + 1):
                if j + 2 < SLOTS:
                    held[j + 2] = pe.value_load(EXI[0:1, j + 2:j + 3], min_val=0, max_val=NE - 1)
                    expert_x(j + 2)
                if 0 <= j - 1:
                    expert_down(j - 1, held.pop(j - 1))
                if 0 <= j + 1 < SLOTS:
                    expert_gu(j + 1, held[j + 1])
                if 0 <= j < SLOTS:
                    expert_hT(j)

        @blk.vector
        def _(dve):
            V = nc.vector
            V.memset(minus_half[:, :], -0.5).then_inc(S("half_set"), 1)
            V.memset(Z3[:, :, D:D + 1], 1.0).then_inc(S("z3_ones"), 1)
            for g in range(4):
                dve.wait_ge(S(f"x_in{g}"), 16)
                for t in range(4 * g, 4 * g + 4):
                    V.bn_stats(ST[:, t, :], X[:, t, :]).then_inc(S("st"), 1)
                dve.wait_ge(S("st"), 4 * g + 4)
                for t in range(4 * g, 4 * g + 4):
                    V.bn_aggr(MV[:, 0, t, :], ST[:, t, :]).then_inc(S("mv"), 1)
            dve.wait_ge(S("mod_sb"), 1)
            V.tensor_scalar(ONEC[:, :, :], MOD[:, :, 1:5:3], 1.0, None, ALU.add).then_inc(S("one_c"), 1)
            V.tensor_scalar(GA[:, :, :], MOD[:, :, 2:6:3], -1.0, None, ALU.mult).then_inc(S("gate_abs"), 1)
            V.tensor_scalar(GS[:, :, :], MOD[:, :, 2:6:3], 0.0, 2.0, ALU.is_ge, ALU.mult).then_inc(S("gate_sign"), 1)
            dve.wait_ge(S("gate_abs"), 1)
            V.tensor_tensor(GA[:, :, :], GA[:, :, :], MOD[:, :, 2:6:3], ALU.max).then_inc(S("gate_abs"), 1)
            dve.wait_ge(S("gate_sign"), 1)
            V.tensor_scalar(GS[:, :, :], GS[:, :, :], -1.0, None, ALU.add).then_inc(S("gate_sign"), 1)
            dve.wait_ge(S("gate_abs"), 2)
            V.tensor_scalar(GA[:, :, :], GA[:, :, :], 0.25, None, ALU.max).then_inc(S("gate_abs"), 1)
            dve.wait_ge(S("gate_abs"), 3)
            dve.wait_ge(S("gate_sign"), 2)
            V.tensor_tensor(GT[:, :, :], GA[:, :, :], GS[:, :, :], ALU.mult).then_inc(S("gate_ok"), 1)

            def norm(dst, t, k, done):
                V.tensor_scalar(dst, X[:, t, :], MV[:, k, t, 0:1], RS[:, k, t:t + 1], ALU.subtract, ALU.mult)\
                    .then_inc(S(done), 1)

            def front_z(p):
                dve.wait_ge(S("rs"), p // 2 + 1)
                if p >= 2:
                    dve.wait_ge(S("zT_ps"), p - 1)
                for j in range(2):
                    norm(Z[:, p % 2, j, :], 2 * p + j, 0, "z")

            def front_max(p):
                q = p % 2
                dve.wait_ge(S("qkv_sb"), 2 * (p + 1))
                if p >= 2:
                    dve.wait_ge(S("sub"), 2 * (p - 1))
                V.tensor_reduce(MX[:, q, 0:32].rearrange("p (t h) -> p t h", t=2), heads(QKV[:, q, :, 0:D]),
                                axis=AX.X, op=ALU.max).then_inc(S("mx"), 1)
                V.tensor_reduce(MX[:, q, 32:48].rearrange("p (t d) -> p t d", t=2),
                                QKV[:, q, :, D:2 * D].rearrange("p t (h d) -> p t d h", d=HD0),
                                axis=AX.X, op=ALU.max).then_inc(S("mx"), 1)

            def front_sum(p):
                q = p % 2
                dve.wait_ge(S("exp"), p + 1)
                V.tensor_reduce(SM[:, q, 0:32].rearrange("p (t h) -> p t h", t=2), heads(E0[:, q, :, 0:D]),
                                axis=AX.X, op=ALU.add).then_inc(S("sum"), 1)
                V.tensor_reduce(SM[:, q, 32:48].rearrange("p (t d) -> p t d", t=2),
                                E0[:, q, :, D:2 * D].rearrange("p t (h d) -> p t d h", d=HD0),
                                axis=AX.X, op=ALU.add).then_inc(S("sum"), 1)
                dve.wait_ge(S("sum"), 2 * (p + 1))
                if p >= 2:
                    dve.wait_ge(S("qn"), p - 1)
                V.reciprocal(RC[:, q, :], SM[:, q, :]).then_inc(S("rec"), 1)

            def mid_p1(p, j):
                if p >= 1:
                    dve.wait_ge(S("tvT_ps"), 2 * (p - 1) + j + 1)
                V.tensor_tensor(p1_out(j, 0, K1), p1_k(p % 2, j, 0, K1), p1_v(p % 2, j, 0, K1), ALU.mult)\
                    .then_inc(S("p1d"), 1)

            def mid_p2(p, j):
                dve.wait_ge(S("tv"), 2 * p + j + 1)
                if j == 0:
                    dve.wait_ge(S("qn"), p + 1)
                if p >= 1:
                    dve.wait_ge(S("aT_ps"), 2 * (p - 1) + j + 1)
                V.tensor_tensor(p2_out(j, 0, K2), p2_q(p % 2, j, 0, K2), p2_t(j, 0, K2), ALU.mult)\
                    .then_inc(S("p2d"), 1)

            def mid_x1(p, j):
                t = 2 * p + j
                dve.wait_ge(S("aB_ps"), t + 1)
                V.tensor_tensor(X[:, t, :], B[3 + j][:, 320:448], X[:, t, :], ALU.add)\
                    .then_inc(S("x1"), 1)

            def stats(p, k, ready, count, st, mv):
                dve.wait_ge(S(ready), count)
                for j in range(2):
                    t = 2 * p + j
                    V.bn_stats(ST[:, t, :], X[:, t, :]).then_inc(S(st), 1)
                for j in range(2):
                    t = 2 * p + j
                    dve.wait_ge(S(st), t + 1)
                    V.bn_aggr(MV[:, k, t, :], ST[:, t, :]).then_inc(S(mv), 1)

            def back_z2(p):
                dve.wait_ge(S("rs2"), p + 1)
                if p >= 1:
                    dve.wait_ge(S("z2T_ps"), p)
                for j in range(2):
                    norm(Z2[:, j, :], 2 * p + j, 1, "z2")

            def back_hid(p):
                dve.wait_ge(S("gu_ps"), 3 * (p + 1))
                dve.wait_ge(S("silu"), 2 * (p + 1))
                if p >= 1:
                    dve.wait_ge(S("y_ps"), p)
                V.tensor_tensor(HID[:, 0:512], SG[:, 0:512], B[7][:, :], ALU.mult).then_inc(S("hid"), 1)
                V.tensor_tensor(HID[:, 512:768], SG[:, 512:768], B[6][:, 256:512], ALU.mult).then_inc(S("hid"), 1)

            def back_x2(p):
                t = 2 * p
                dve.wait_ge(S("y_ps"), p + 1)
                V.tensor_tensor(X[:, t:t + 2, :], B[2][:, 256:512].rearrange("p (t d) -> p t d", t=2),
                                X[:, t:t + 2, :], ALU.add).then_inc(S("x2"), 1)

            def back_z3(p):
                dve.wait_ge(S("rs3"), p + 1)
                for j in range(2):
                    norm(Z3[:, 2 * p + j, 0:D], 2 * p + j, 2, "z3")

            for i in STEPS:
                n, f, m, b, c = lead(i)
                if m is not None:
                    mid_p1(m, 0)
                    mid_p1(m, 1)
                if c is not None:
                    back_x2(c)
                if b is not None:
                    back_z2(b)
                if c is not None:
                    stats(c, 2, "x2", c + 1, "st3", "mv3")
                if f is not None:
                    front_max(f)
                if m is not None:
                    mid_p2(m, 0)
                    mid_p2(m, 1)
                if c is not None:
                    back_z3(c)
                if f is not None:
                    front_sum(f)
                if b is not None:
                    back_hid(b)
                if n is not None:
                    front_z(n)
                if m is not None:
                    mid_x1(m, 0)
                    mid_x1(m, 1)
                    stats(m, 1, "x1", 2 * m + 2, "st2", "mv2")
                if i == 0:
                    dve.wait_ge(S("prep_ps"), 2)
                    dve.wait_ge(s_w1, 128)
                    V.tensor_tensor(WQT[:, :, D:D + 1], B[7][:, 0:C1].unsqueeze(2), BQC[:, :].unsqueeze(2), ALU.add)\
                        .then_inc(S("gbb_sb"), 1)
                    V.tensor_copy(GBB[:, :], B[7][:, 128:256]).then_inc(S("gbb_sb"), 1)
            dve.wait_ge(s_w1, 128)
            for n, bank in enumerate((0, 1, 3, 4)):
                cols = slice(512 * (n % 2), 512 * (n % 2) + 512)
                dve.wait_ge(S("brow_ps"), n + 1)
                V.tensor_tensor(BKVs[0:1, n // 2, cols], B[bank][0:1, :], BKV[0:1, n // 2, cols], ALU.add)\
                    .then_inc(S("brow_sb"), 1)
            dve.wait_ge(S("g_all"), 1)
            V.tensor_copy(GZ[:, :], B[5][:, 0:D + 1]).then_inc(S("gz"), 1)
            dve.wait_ge(S("mrow_ps"), 1)
            V.tensor_copy(MROW[0:1, :], B[6][0:1, 0:128]).then_inc(S("mrow"), 1)
            dve.wait_ge(S("a_ps"), 2)
            V.tensor_copy(A1[:, 512:1024], B[1][:, :]).then_inc(S("a_sb_d"), 1)
            dve.wait_ge(S("a_ps"), 4)
            V.tensor_copy(A1b[0:1, 512:1024], B[4][0:1, :]).then_inc(S("a_sb_d"), 1)
            dve.wait_ge(S("kv_ps"), 2)
            dve.wait_ge(S("kv_zero"), 1)
            for lo in (0, 64):
                V.tensor_copy(KV[lo:lo + 64, 4:8, lo:lo + 64],
                              B[6][lo:lo + 64, :].rearrange("p (c k) -> p c k", c=4)[:, :, lo:lo + 64])\
                    .then_inc(S("kv_sb_d"), 1)
            dve.wait_ge(S("do_ps"), 2)
            V.tensor_copy(DO[:, 4:8, :], B[1][:, :].rearrange("p (c d) -> p c d", c=4)).then_inc(S("do_sb_d"), 1)
            dve.wait_ge(S("mt_ps"), 1)
            V.tensor_scalar(MT[:, :], B[3][:, 0:D + 1], GT[:, 1, 0:1], SCALE1, ALU.mult, ALU.mult)\
                .then_inc(S("mt_step"), 1)
            dve.wait_ge(S("mt_step"), 1)
            dve.wait_ge(S("bog"), 1)
            V.tensor_tensor(MT[:, D:D + 1], MT[:, D:D + 1], BOG[:, :], ALU.add).then_inc(S("mt_step"), 1)
            dve.wait_ge(S("mt_step"), 2)
            V.tensor_scalar(DG[:, :], ident, MT[:, D:D + 1], None, ALU.mult).then_inc(S("mt_step"), 1)

            def attend(g):
                ts = slice(4 * g, 4 * g + 4)
                if g == 0:
                    dve.wait_ge(S("mc"), 1)
                V.tensor_tensor(X[:, ts, :], X[:, ts, :], MC[:, D:2 * D].unsqueeze(1).broadcast_to([128, 4, D]),
                                ALU.add).then_inc(S("x_cst"), 1)
                dve.wait_ge(S("x_cst"), g + 1)
                dve.wait_ge(S("o_ps"), g + 1)
                V.tensor_tensor(X[:, ts, :], B[g % 2][:, :].rearrange("p (t d) -> p t d", t=4), X[:, ts, :],
                                ALU.add).then_inc(S("x3"), 1)
                dve.wait_ge(S("x3"), g + 1)
                for t in range(4 * g, 4 * g + 4):
                    V.bn_stats(ST[:, t, :], X[:, t, :]).then_inc(S("st4"), 1)
                dve.wait_ge(S("st4"), 4 * g + 4)
                for t in range(4 * g, 4 * g + 4):
                    V.bn_aggr(MV[:, 3, t, :], ST[:, t, :]).then_inc(S("mv4"), 1)

            def last_norm(g):
                dve.wait_ge(S("rs4"), g + 1)
                for t in range(4 * g, 4 * g + 4):
                    norm(Z4[:, t, :], t, 3, "z4")

            for g in range(5):
                if g < 4:
                    attend(g)
                if g >= 1:
                    last_norm(g - 1)

            steps = [0]

            def link(ins):
                steps[0] += 1
                ins.then_inc(S("dve_step"), 1)
                dve.wait_ge(S("dve_step"), steps[0])

            def over_e(ap):
                return ap.unsqueeze(2).broadcast_to([128, T, NE])

            def shared_hid(n):
                dve.wait_ge(S("ssilu"), n + 1)
                if n >= 4:
                    dve.wait_ge(S("sy_ps"), n // 2 - 1)
                V.tensor_tensor(HS[n // 2 % 2][:, 512 * (n % 2):512 * (n % 2) + 512], SS[n % 2],
                                B[(6, 0)[n % 2]][:, :], ALU.mult).then_inc(S("shid"), 1)

            def shared_x4(g):
                dve.wait_ge(S("sy_ps"), g + 1)
                for t in range(4 * g, 4 * g + 4):
                    V.scalar_tensor_tensor(out=X[:, t, :], in0=B[(1, 3)[g % 2]][:, 128 * (t % 4):128 * (t % 4) + 128],
                                           scalar=GATE[:, t:t + 1], in1=X[:, t, :], op0=ALU.mult, op1=ALU.add)\
                        .then_inc(S("x4"), 1)

            dve.wait_ge(S("lg_ps"), 4)
            link(V.tensor_copy(LG[:, :, :], B[4][:, 0:9 * T].rearrange("p (t e) -> p t e", e=9)))
            link(V.tensor_reduce(RM[:, :], LG[:, :, 0:NE], axis=AX.X, op=ALU.max))
            V.tensor_tensor(PR[:, :, :], LG[:, :, 0:NE], over_e(RM[:, :]), ALU.subtract).then_inc(S("rt_sub"), 1)
            dve.wait_ge(S("rt_exp"), 1)
            link(V.tensor_reduce(RSUM[:, :], PX[:, :, :], axis=AX.X, op=ALU.add))
            link(V.reciprocal(RSUM[:, :], RSUM[:, :]))
            link(V.tensor_tensor(PR[:, :, :], PX[:, :, :], over_e(RSUM[:, :]), ALU.mult))
            for k in range(2):
                link(V.tensor_reduce(WK[:, k, :], PR[:, :, :], axis=AX.X, op=ALU.max))
                link(V.tensor_tensor(SCR[:, :, :], PR[:, :, :], over_e(WK[:, k, :]), ALU.is_equal))
                link(V.tensor_tensor(SCR[:, :, :], SCR[:, :, :], first_w.unsqueeze(1).broadcast_to([128, T, NE]),
                                     ALU.mult))
                link(V.tensor_reduce(RM[:, :], SCR[:, :, :], axis=AX.X, op=ALU.max))
                link(V.tensor_tensor(OH[:, k, :, :], SCR[:, :, :], over_e(RM[:, :]), ALU.is_equal))
                if k == 0:
                    link(V.scalar_tensor_tensor(out=PR[:, :, :], in0=OH[:, 0, :, :], scalar=-2.0, in1=PR[:, :, :],
                                                op0=ALU.mult, op1=ALU.add))
            V.tensor_tensor(MH[:, 0:T, :], OH[:, 0, :, :], OH[:, 1, :, :], ALU.add).then_inc(S("picked"), 1)
            dve.wait_ge(S("gate_e"), 1)
            link(V.tensor_scalar(GATE[:, :], GATE[:, :], 1.0, None, ALU.add))
            V.reciprocal(GATE[:, :], GATE[:, :]).then_inc(S("gate"), 1)
            for n in range(4):
                shared_hid(n)
            dve.wait_ge(S("gate"), 1)
            shared_x4(0)
            dve.wait_ge(S("rank_ps"), 1)
            link(V.tensor_copy(RK[:, :, :], B[2][:, 0:8 * T + 8].rearrange("p (t e) -> p t e", e=8)))
            link(V.tensor_scalar(NTI[:, :], RK[:, T, :], 127.0, None, ALU.add))
            link(V.tensor_scalar(NTI[:, :], NTI[:, :], 7, None, ALU.arith_shift_right))
            link(V.tensor_copy(NTF[:, :], NTI[:, :]))
            link(V.tensor_tensor(STT[:, :, :], before.rearrange("p (e f) -> p e f", e=8),
                                 NTF[:, :].unsqueeze(1).broadcast_to([128, NE, NE]), ALU.mult))
            link(V.tensor_reduce(START[:, :], STT[:, :, :], axis=AX.X, op=ALU.add))
            link(V.tensor_tensor(ENDT[:, :], START[:, :], NTF[:, :], ALU.add))
            link(V.scalar_tensor_tensor(out=RK[:, 0:T, :], in0=START[:, :].unsqueeze(1).broadcast_to([128, T, NE]),
                                        scalar=128.0, in1=RK[:, 0:T, :], op0=ALU.mult, op1=ALU.add))
            link(V.tensor_tensor(OH[:, :, :, :], OH[:, :, :, :],
                                 RK[:, 0:T, :].unsqueeze(1).broadcast_to([128, 2, T, NE]), ALU.mult))
            link(V.tensor_reduce(SLOT[:, :], OH[:, :, :, :].rearrange("p k t e -> p (k t) e"), axis=AX.X, op=ALU.add))
            link(V.tensor_copy(SLI[:, :], SLOT[:, :]))
            link(V.tensor_scalar(TLI[:, :], SLI[:, :], 7, None, ALU.arith_shift_right))
            link(V.tensor_scalar(RWI[:, :], SLI[:, :], 127, None, ALU.bitwise_and))
            link(V.tensor_copy(TLF[:, :], TLI[:, :]))
            link(V.tensor_copy(RWF[:, :], RWI[:, :]))
            link(V.tensor_tensor(BH, RWF[:, :].unsqueeze(2).broadcast_to([128, 2 * T, 128]),
                                 iota.unsqueeze(1).broadcast_to([128, 2 * T, 128]), ALU.is_equal))
            link(V.tensor_tensor(AH[:, :, SLOTS:2 * SLOTS], TLF[:, :].unsqueeze(2).broadcast_to([128, 2 * T, SLOTS]),
                                 slot_iota.unsqueeze(1).broadcast_to([128, 2 * T, SLOTS]), ALU.is_equal))
            for k in range(2):
                link(V.tensor_tensor(AH[:, T * k:T * k + T, 0:SLOTS], AH[:, T * k:T * k + T, SLOTS:2 * SLOTS],
                                     token_id.unsqueeze(2).broadcast_to([128, T, SLOTS]), ALU.mult))
            V.tensor_scalar(AH[:, T:2 * T, SLOTS:2 * SLOTS], AH[:, T:2 * T, SLOTS:2 * SLOTS], 2.0, None, ALU.mult)\
                .then_inc(S("onehots"), 1)
            link(V.tensor_tensor(GEQ[0:1, :, :], slot_iota[0:1, :].unsqueeze(2).broadcast_to([1, SLOTS, NE]),
                                 ENDT[0:1, :].unsqueeze(1).broadcast_to([1, SLOTS, NE]), ALU.is_ge))
            link(V.tensor_reduce(EXF[0:1, :], GEQ[0:1, :, :], axis=AX.X, op=ALU.add))
            link(V.tensor_scalar(EXI[0:1, :], EXF[0:1, :], NE - 1.0, None, ALU.min))
            for n in range(4, 6):
                shared_hid(n)
            shared_x4(1)
            dve.wait_ge(S("idx_ps"), 1)
            link(V.tensor_copy(IDX[:, :], B[4][:, 0:2 * SLOTS]))
            link(V.tensor_copy(GI[:, :], IDX[:, 0:SLOTS]))
            link(V.tensor_scalar(PADF[:, :], IDX[:, SLOTS:2 * SLOTS], 0.0, None, ALU.is_equal))
            link(V.tensor_tensor(PADF[:, :], PADF[:, :], pad_row, ALU.mult))
            link(V.scalar_tensor_tensor(out=DF[:, :], in0=IDX[:, SLOTS:2 * SLOTS], scalar=float(TOKENS),
                                        in1=IDX[:, 0:SLOTS], op0=ALU.mult, op1=ALU.add))
            link(V.tensor_scalar(DF[:, :], DF[:, :], -float(TOKENS), None, ALU.add))
            V.tensor_tensor(DI[:, :], DF[:, :], PADF[:, :], ALU.add).then_inc(S("idx"), 1)
            for n in range(6, 8):
                shared_hid(n)
            shared_x4(2)
            shared_x4(3)

            def expert_hid(j):
                dve.wait_ge(S("esilu"), j + 1)
                if j >= 2:
                    dve.wait_ge(S("ht_ps"), j - 1)
                V.tensor_tensor(HX[j % 2], SX[j % 2], B[2 + j % 2][:, FE:2 * FE], ALU.mult).then_inc(S("ehid"), 1)

            def expert_hT(j):
                dve.wait_ge(S("ht_ps"), j + 1)
                if j >= 2:
                    dve.wait_ge(S("ey_ps"), j - 1)
                V.tensor_copy(HXT[j % 2], B[4 + j % 2][:, 0:2 * 128]).then_inc(S("ht"), 1)

            def expert_y(j):
                dve.wait_ge(S("ey_ps"), j + 1)
                if j >= GATHERS:
                    dve.wait_ge(S(f"scattered{j % GATHERS}"), 16 * (j // GATHERS))
                V.tensor_copy(YX[j % GATHERS], B[6 + j % 2][:, 0:128]).then_inc(S("ey"), 1)

            for j in range(-2, SLOTS + 1):
                if 0 <= j - 1:
                    expert_y(j - 1)
                if 0 <= j < SLOTS:
                    expert_hT(j)
                if 0 <= j + 1 < SLOTS:
                    expert_hid(j + 1)

            for g in range(4):
                dve.wait_ge(S(f"y_in{g}"), 32)
                for k in range(2):
                    if k == 1:
                        dve.wait_ge(S("part"), 4 * g + 4)
                    for t in range(4 * g, 4 * g + 4):
                        V.scalar_tensor_tensor(out=X[:, t, :], in0=YB[g][:, k, t % 4, :], scalar=WK[:, k, t:t + 1],
                                               in1=X[:, t, :], op0=ALU.mult, op1=ALU.add)\
                            .then_inc(S("x5" if k else "part"), 1)

        @blk.gpsimd
        def _(pool):
            G = nc.gpsimd

            def rstd(k, a, b, mv, ve, rs, n):
                pool.wait_ge(S(mv), b)
                G.tensor_scalar(VE[:, k, a:b], MV[:, k, a:b, 1], EPS, None, ALU.add).then_inc(S(ve), 1)
                pool.wait_ge(S(ve), n + 1)
                G.tensor_tensor(RS[:, k, a:b], VE[:, k, a:b], minus_half[:, a:b], ALU.pow).then_inc(S(rs), 1)

            pool.wait_ge(S("half_set"), 1)
            for g in range(4):
                rstd(0, 4 * g, 4 * g + 4, "mv", "ve", "rs", g)
            pool.wait_ge(s_wi, 16)
            G.tensor_copy(WGU0[:, :], WGU0i[:, :]).then_inc(S("w0_cast"), 1)

            def layer1_weights():
                pool.wait_ge(s_w1, 128)
                pool.wait_ge(S("one_c"), 1)
                pool.wait_ge(S("gate_ok"), 1)
                for w in range(3):
                    G.tensor_scalar(W1s[:, w, :], W1[:, w, :], ONEC[:, 1, 0:1], None, ALU.mult)\
                        .then_inc(S("w1_scaled"), 1)
                pool.wait_ge(s_cf, 16)
                G.tensor_scalar(DG[:, :], ident, GT[:, 1, 1:2], None, ALU.mult).then_inc(S("diag_gb"), 1)
                G.tensor_scalar(BOG[:, :], BO[:, :], GT[:, 1, 0:1], None, ALU.mult).then_inc(S("bog"), 1)
                G.memset(KV[:, :, :], 0.0)
                G.memset(MH[:, :, :], 0.0)
                G.memset(NTOK[:, :], float(TOKENS)).then_inc(S("kv_zero"), 1)

            def front_sub(p):
                q = p % 2
                pool.wait_ge(S("mx"), 2 * (p + 1))
                if p >= 2:
                    pool.wait_ge(S("exp"), p - 1)
                G.tensor_tensor(heads(S0[:, q, :, 0:D]), heads(QKV[:, q, :, 0:D]),
                                MX[:, q, 0:32].rearrange("p (t h) -> p t h", t=2).unsqueeze(3)
                                .broadcast_to([128, 2, H0, HD0]), ALU.subtract).then_inc(S("sub"), 1)
                G.tensor_tensor(heads(S0[:, q, :, D:2 * D]), heads(QKV[:, q, :, D:2 * D]),
                                MX[:, q, 32:48].rearrange("p (t d) -> p t d", t=2).unsqueeze(2)
                                .broadcast_to([128, 2, H0, HD0]), ALU.subtract).then_inc(S("sub"), 1)

            def front_norm(p):
                q = p % 2
                pool.wait_ge(S("rec"), p + 1)
                if p >= 2:
                    pool.wait_ge(S("p2d"), 2 * (p - 1))
                G.tensor_tensor(heads(QH[:, q, :, :]), heads(E0[:, q, :, 0:D]),
                                RC[:, q, 0:32].rearrange("p (t h) -> p t h", t=2).unsqueeze(3)
                                .broadcast_to([128, 2, H0, HD0]), ALU.mult).then_inc(S("qh"), 1)
                pool.wait_ge(S("qh"), p + 1)
                G.tensor_tensor(heads(QN[:, q, :, :]), heads(QH[:, q, :, :]),
                                RC[:, q, 32:48].rearrange("p (t d) -> p t d", t=2).unsqueeze(2)
                                .broadcast_to([128, 2, H0, HD0]), ALU.mult).then_inc(S("qn"), 1)

            def mid_p1(p, j):
                pool.wait_ge(S("exp"), p + 1)
                if p >= 1:
                    pool.wait_ge(S("tvT_ps"), 2 * (p - 1) + j + 1)
                G.tensor_tensor(p1_out(j, K1, H0), p1_k(p % 2, j, K1, H0), p1_v(p % 2, j, K1, H0), ALU.mult)\
                    .then_inc(S("p1p"), 1)

            def mid_p2(p, j):
                pool.wait_ge(S("tv"), 2 * p + j + 1)
                if p >= 1:
                    pool.wait_ge(S("aT_ps"), 2 * (p - 1) + j + 1)
                if j == 0:
                    pool.wait_ge(S("qn"), p + 1)
                G.tensor_tensor(p2_out(j, K2, HD0), p2_q(p % 2, j, K2, HD0), p2_t(j, K2, HD0), ALU.mult)\
                    .then_inc(S("p2p"), 1)

            for i in STEPS:
                n, f, m, b, c = lead(i)
                if b is not None:
                    rstd(1, 2 * b, 2 * b + 2, "mv2", "ve2", "rs2", b)
                if m is not None:
                    mid_p1(m, 0)
                    mid_p1(m, 1)
                if c is not None:
                    rstd(2, 2 * c, 2 * c + 2, "mv3", "ve3", "rs3", c)
                if f is not None:
                    front_sub(f)
                if m is not None:
                    mid_p2(m, 0)
                    mid_p2(m, 1)
                if f is not None:
                    front_norm(f)
                if i == -1:
                    layer1_weights()
                if i == 0:
                    pool.wait_ge(s_we, 96)
                    pool.wait_ge(S("gbb_sb"), 2)
                    G.tensor_tensor(WD1g[:, :, :, :].rearrange("p e f d -> p (e f) d"),
                                    WD1[:, :, :, :].rearrange("p e f d -> p (e f) d"),
                                    GBB[:, :].unsqueeze(1).broadcast_to([128, 2 * (NE + 1), D]), ALU.mult)\
                        .then_inc(S("wd1_scaled"), 1)
            for g in range(4):
                rstd(3, 4 * g, 4 * g + 4, "mv4", "ve4", "rs4", g)

            def gather(j):
                if j >= GATHERS:
                    pool.wait_ge(S("xt_ps"), j - GATHERS + 1)
                G.indirect_dma_start(GX[j % GATHERS], None, z_dram.ap(),
                                     bass.IndirectOffsetOnAxis(GI[:, j:j + 1].bitcast(U32), 0))\
                    .then_inc(S(f"gathered{j % GATHERS}"), 16)

            def scatter(j):
                pool.wait_ge(S("ey"), j + 1)
                G.indirect_dma_start(y_dram.ap(), bass.IndirectOffsetOnAxis(DI[:, j:j + 1].bitcast(U32), 0),
                                     YX[j % GATHERS], None).then_inc(S(f"scattered{j % GATHERS}"), 16)

            pool.wait_ge(S("idx"), 1)
            pool.wait_ge(S("z_rows"), 64)
            for j in range(SLOTS + GATHERS - 1):
                if j < SLOTS:
                    gather(j)
                if j >= GATHERS - 1:
                    scatter(j - GATHERS + 1)


def laid_out(i):
    def c(a):
        return np.ascontiguousarray(a)
    i = {k: np.asarray(v) for k, v in i.items()}
    cf, _, ch = constants()
    n = NE
    return dict(
        x_in=c(i["L0_attn_input_seq_embs"].reshape(TOKENS, D)),
        wqkv0=c(np.concatenate([i["L0_attn_W_Q"].T, i["L0_attn_W_K"].T, i["L0_attn_W_V"].T], 1)),
        wgu0=c(np.concatenate([i["L0_ffn_w_gate"].T, i["L0_ffn_w_up"].T], 1)),
        wd0=c(i["L0_ffn_w_down"]),
        c0=c(i["L0_c"].reshape(D, 1)), wmod0=c(i["L0_wmod"]),
        wq1=c(i["L1_attn_Wq"]), wk1=c(i["L1_attn_Wk"]), wv1=c(i["L1_attn_Wv"]),
        bqc1=c(i["L1_attn_bq"].reshape(C1, 128).T), bk1=c(i["L1_attn_bk"].reshape(1, HW1)),
        bv1=c(i["L1_attn_bv"].reshape(1, HW1)), wo1=c(i["L1_attn_Wo"]),
        bo1=c(i["L1_attn_bo"].reshape(D, 1)),
        router=c(np.concatenate([i["L1_ffn_router_w"].T, i["L1_ffn_gate_w"].T], 1)),
        wgu1=c(np.concatenate([i["L1_ffn_w_gate"], i["L1_ffn_w_up"]], 2).transpose(1, 0, 2)),
        wd1=c(i["L1_ffn_w_down"].reshape(n, 2, 128, D).transpose(2, 0, 1, 3)),
        swgu1=c(np.concatenate([i["L1_ffn_sw_gate"], i["L1_ffn_sw_up"]], 1)),
        swd1=c(i["L1_ffn_sw_down"].reshape(2, 128, D).transpose(1, 0, 2)),
        c1=c(i["L1_c"].reshape(D, 1)), wmod1=c(i["L1_wmod"]),
        const_f=cf, const_h=ch,
    )


def kernel(**inputs):
    import concourse.bacc as _bacc
    from concourse.bass_utils import run_bass_kernel_spmd as _run

    arrays = laid_out(inputs)
    nc = _bacc.Bacc("TRN2", target_bir_lowering=False, num_devices=1)
    args = {name: nc.dram_tensor(name + "_dram", a.shape, mybir.dt.from_np(a.dtype), kind="ExternalInput").ap()
            for name, a in arrays.items()}
    out = nc.dram_tensor("out_dram", (TOKENS, D), F32, kind="ExternalOutput").ap()
    build(nc, out=out, **args)
    r = _run(nc, [{name + "_dram": a for name, a in arrays.items()}], core_ids=[0])
    return r.results[0]["out_dram"].reshape(1, TOKENS, D)
```

```python
import concourse.bass as bass
from concourse import mybir
from contextlib import ExitStack
import numpy as np

F32 = mybir.dt.float32
F16 = mybir.dt.float16
I32 = mybir.dt.int32
U32 = mybir.dt.uint32
ALU = mybir.AluOpType
ACT = mybir.ActivationFunctionType
AX = mybir.AxisListType

TOKENS, D = 2048, 128
T = TOKENS // 128
PAIRS = T // 2
H0, HD0 = 16, 8
HID0 = 384
C0 = HID0 // 128
HW1 = 1024
C1 = HW1 // 128
SCALE1 = 1.0 / 8.0
FE, NE = 256, 8
SLOTS = 2 * T + NE - 1
EPS = 1e-5
GATHERS = 9
SCATTERS = 4
MAGIC = 1.5 * 2.0 ** 23
FILL = (12, 12, 12, 12, 40, 50)
WARM = 5


def constants():
    p = np.arange(128)
    ident = np.eye(128, dtype=np.float32)
    fold = np.concatenate([np.eye(64), np.eye(64)], 0).astype(np.float32)
    iota128 = np.tile(p.astype(np.float32), (128, 1))
    slot = np.tile(np.arange(SLOTS, dtype=np.float32), (128, 1))
    token = (np.arange(T)[None, :] * 128 + p[:, None]).astype(np.float32)
    first = np.tile(np.arange(8, 0, -1, dtype=np.float32), (128, 1))
    before = np.tile(np.tril(np.ones((8, 8)), -1).astype(np.float32).reshape(1, 64), (128, 1))
    pad_row = (2 * TOKENS + 128 * np.arange(SLOTS)[None, :] + p[:, None]).astype(np.float32)
    ones = np.ones((128, 128), np.float32)
    parts = dict(ident=ident, fold=fold, slot=slot, token=token, first=first,
                 before=before, pad=pad_row, ones=ones)
    at, cols = {}, 0
    for name, a in parts.items():
        at[name] = (cols, cols + a.shape[1])
        cols += a.shape[1]
    tri = (p[:, None] < p[None, :]).astype(np.float16)
    half = np.concatenate([tri, np.ones((128, 128), np.float16), iota128.astype(np.float16)], 1)
    return np.concatenate(list(parts.values()), 1), at, half


def build(nc, x_in, wqkv0, wgu0, wd0, c0, wmod0, wq1, wk1, wv1, bqc1, bk1, bv1, wo1, bo1,
          router, wgu1, wd1, swgu1, swd1, c1, wmod1, const_f, const_h, out):
    _, at, _ = constants()
    z_dram = nc.dram_tensor("z_rows", [TOKENS, D], F32)
    y_dram = nc.dram_tensor("y_rows", [2 * TOKENS + 128 * SLOTS, D], F32)
    ctx = ExitStack()
    with ctx:
        def sb(name, shape, dt=F32):
            return ctx.enter_context(nc.sbuf_tensor(name, shape, dt))

        def ps(name, shape=(128, 512), dt=F32):
            return ctx.enter_context(nc.psum_tensor(name, list(shape), dt))

        def sem(name):
            return ctx.enter_context(nc.semaphore(name))

        ncf = max(b for _, b in at.values())
        CF = sb("CF", [128, ncf])
        CH = sb("CH", [128, 384], F16)

        def cf(name):
            a, b = at[name]
            return CF[:, a:b]
        ident, fold, slot_iota = cf("ident"), cf("fold"), cf("slot")
        token_id, first_w, before, pad_row, ones = cf("token"), cf("first"), cf("before"), cf("pad"), cf("ones")
        tri_h, ones_h, iota_h = CH[:, 0:128], CH[:, 128:256], CH[:, 256:384]
        minus_half = sb("minus_half", [128, T])
        X = sb("X", [128, T, D])
        WQKV0 = sb("WQKV0", [128, 3 * D])
        WGU0i = sb("WGU0i", [128, 2 * HID0], I32)
        WGU0 = sb("WGU0", [128, 2 * HID0])
        WD0i = sb("WD0i", [128, HID0], I32)
        WD0g = sb("WD0g", [128, HID0])
        WD0 = sb("WD0", [128, C0, D])
        CM = sb("CM", [128, 2])
        SC = sb("SC", [128, 2])
        WM = sb("WM", [128, 2, 6 * D])
        MOD = sb("MOD", [128, 2, 6])
        ONEC = sb("ONEC", [128, 2, 2])
        GT = sb("GT", [128, 2, 2])
        GA = sb("GA", [128, 2, 2])
        GS = sb("GS", [128, 2, 2])
        W1 = sb("W1", [128, 3, HW1])
        W1s = sb("W1s", [128, 3, HW1])
        WQT = sb("WQT", [128, C1, D + 1])
        WO1 = sb("WO1", [128, C1, D])
        BQC = sb("BQC", [128, C1])
        BKV = sb("BKV", [1, 2, HW1])
        BKVs = sb("BKVs", [1, 2, HW1])
        BO = sb("BO", [128, 1])
        RT = sb("RT", [128, NE + 1])
        WGU1 = sb("WGU1", [128, NE, 2 * FE])
        WD1 = sb("WD1", [128, NE + 1, 2, D])
        WD1g = sb("WD1g", [128, NE + 1, 2, D])
        SGU = sb("SGU", [128, 2 * FE])
        DG = sb("DG", [128, 128])
        GBB = sb("GBB", [128, D])

        ST = sb("ST", [128, T, 6])
        MV = sb("MV", [128, 4, T, 2])
        VE = sb("VE", [128, 4, T])
        NM = sb("NM", [128, T])
        RS = sb("RS", [128, 4, T])
        Z = sb("Z", [128, 2, 2, D])
        HT = sb("HT", [128, 2, 256])
        QKV = sb("QKV", [128, 2, 2, 3 * D])
        MX = sb("MX", [128, 2, 48])
        S0 = sb("S0", [128, 2, 2, 2 * D])
        E0 = sb("E0", [128, 2, 2, 2 * D])
        SM = sb("SM", [128, 2, 48])
        RC = sb("RC", [128, 2, 48])
        QH = sb("QH", [128, 2, 2, D])
        QN = sb("QN", [128, 2, 2, D])
        P1 = sb("P1", [128, 2, 1024])
        P2 = sb("P2", [128, 2, 1024])
        WARMUP = P2[:, 1, 0:512]
        TVT = sb("TVT", [128, 2, 128])
        TV = sb("TV", [128, 2, 64])
        AT = sb("AT", [128, 2, 128])
        Z2 = sb("Z2", [128, 2, D])
        H2T = sb("H2T", [128, 256])
        SG = sb("SG", [128, C0 * 256])
        HID = sb("HID", [128, C0 * 256])
        Z3 = sb("Z3", [128, T, D + 1])
        Z3T = sb("Z3T", [128, TOKENS])
        GZ = sb("GZ", [128, D + 1])
        MROW = sb("MROW", [1, 128])
        NBV = BKV[0:1, 1, :]
        A1 = sb("A1", [128, HW1])
        A1b = sb("A1b", [1, HW1])
        KV = sb("KV", [128, C1, 128])
        DO = sb("DO", [128, C1, 128])
        MT = sb("MT", [128, D + 1])
        MC = sb("MC", [128, D])
        BOG = sb("BOG", [128, 1])
        Z4 = Z3[:, :, 0:D]
        H4T = Z3T
        LG = sb("LG", [128, T, NE + 1])
        GATE = sb("GATE", [128, T])
        SS = [QKV[:, 0, :, :].rearrange("p t c -> p (t c)")[:, 0:512], QKV[:, 1, :, :].rearrange("p t c -> p (t c)")[:, 0:512]]
        HS = [S0[:, :, :, :].rearrange("p a b c -> p (a b c)"), E0[:, :, :, :].rearrange("p a b c -> p (a b c)")]
        PR = sb("PR", [128, T, NE])
        PX = sb("PX", [128, T, NE])
        L2 = SG[:, 0:T * NE].rearrange("p (t e) -> p t e", e=NE)
        TOP = sb("TOP", [128, 2, T])
        RM = sb("RM", [128, T])
        RSUM = sb("RSUM", [128, T])
        WK = sb("WK", [128, 2, T])
        OH = sb("OH", [128, 2, T, NE])
        SCR = SG[:, T * NE:2 * T * NE].rearrange("p (t e) -> p t e", e=NE)
        MH = sb("MH", [128, T + 1, NE], F16)
        OHR = SG[:, 2 * T * NE:4 * T * NE].rearrange("p (k t e) -> p k t e", k=2, e=NE)
        OHS = SG[:, 4 * T * NE:6 * T * NE].rearrange("p (k t e) -> p k t e", k=2, e=NE)
        NTF = sb("NTF", [128, NE])
        STT = HID[:, 512:512 + NE * NE].rearrange("p (e f) -> p e f", e=NE)
        START = sb("START", [128, NE])
        ENDT = sb("ENDT", [128, NE])
        RANK = sb("RANK", [128, 2 * T])
        RTILE = sb("RTILE", [128, 2 * T])
        FIRST = sb("FIRST", [128, 2 * T])
        ROW = sb("ROW", [128, 2 * T], F16)
        TILE = sb("TILE", [128, 2 * T], F16)
        BH = P1[:, :, :].rearrange("p a b -> p (a b)").bitcast(F16).rearrange("p (k r) -> p k r", r=128)
        AH = P2[:, :, :].rearrange("p a b -> p (a b)").bitcast(F16)[:, 0:2 * T * 2 * SLOTS]\
            .rearrange("p (k c) -> p k c", c=2 * SLOTS)
        IDX = sb("IDX", [128, 2, 2, SLOTS])
        GI = sb("GI", [128, SLOTS], I32)
        PADF = sb("PADF", [128, SLOTS])
        DF = sb("DF", [128, SLOTS])
        ANY = sb("ANY", [128, SLOTS])
        DI = sb("DI", [128, SLOTS], I32)
        GEQ = HID[0:1, 0:SLOTS * NE].rearrange("p (s e) -> p s e", e=NE)
        EXF = sb("EXF", [1, SLOTS])
        EXI = sb("EXI", [1, SLOTS], I32)
        W1f = W1[:, :, :].rearrange("p a b -> p (a b)")
        WMf = WM[:, :, :].rearrange("p l m -> p (l m)")
        GX = [WMf[:, 128 * b:128 * b + 128] for b in range(GATHERS)]
        YX = [W1f[:, 768 + 128 * b:896 + 128 * b] for b in range(SCATTERS)]
        XT = [W1f[:, c:c + 128] for c in (1536, 1664, 2816)]
        SX = [W1f[:, 1792 + 256 * b:2048 + 256 * b] for b in range(2)]
        HX = [W1f[:, 2304 + 256 * b:2560 + 256 * b] for b in range(2)]
        HXT = [A1[:, 256 * b:256 * b + 256] for b in range(2)]
        YB = [a.rearrange("p (k t d) -> p k t d", k=2, t=4) for a in
              (W1s[:, 0, :], W1s[:, 1, :], W1s[:, 2, :], WO1[:, :, :].rearrange("p c d -> p (c d)"))]

        B = [ps(f"bank{i}") for i in range(8)]

        s_cf, s_x, s_w0, s_wi, s_c, s_w1, s_we = (sem(n) for n in
            ("const_in", "x_in", "w0_in", "w0int_in", "c_in", "w1_in", "we_in"))
        s = {}

        def S(name):
            if name not in s:
                s[name] = sem(name)
            return s[name]

        parts = [("gu", 2), ("gu", 3), ("down", 0)] + [("gu", 4), ("gu", 5), ("down", 1), ("gu", 6), ("gu", 7), ("down", 2),
                                              ("down", 3)]
        SHARED_AT = {3 * n + 2: part for n, part in enumerate(parts)}
        blk = ctx.enter_context(nc.Block())

        xv = x_in.rearrange("(t p) d -> p t d", p=128)
        outv = out.rearrange("(t p) d -> p t d", p=128)

        @blk.sync
        def _(sp):
            sp.dma_start(X[:, 0:4, :], xv[:, 0:4, :]).then_inc(S("x_in0"), 16)
            sp.dma_start(CF[:, :], const_f).then_inc(s_cf, 16)
            sp.dma_start(WQKV0[:, :], wqkv0).then_inc(s_w0, 16)
            for g in range(1, 4):
                sp.dma_start(X[:, 4 * g:4 * g + 4, :], xv[:, 4 * g:4 * g + 4, :]).then_inc(S(f"x_in{g}"), 16)
            sp.dma_start(WGU0i[:, :], wgu0).then_inc(s_wi, 16)
            for w, src in enumerate((wq1, wk1, wv1)):
                sp.dma_start(W1[:, w, :], src).then_inc(s_w1, 16)
            sp.dma_start(WO1[:, :, :], wo1.rearrange("(c p) d -> p c d", p=128)).then_inc(s_w1, 16)
            sp.dma_start(BQC[:, :], bqc1).then_inc(s_w1, 16)
            sp.dma_start(BKV[0:1, 0, :], bk1).then_inc(s_w1, 16)
            sp.dma_start(BKV[0:1, 1, :], bv1).then_inc(s_w1, 16)
            sp.dma_start(BO[:, :], bo1).then_inc(s_w1, 16)
            sp.dma_start(CH[:, :], const_h).then_inc(s_we, 16)
            sp.dma_start(RT[:, :], router).then_inc(s_we, 16)
            sp.dma_start(SGU[:, :], swgu1).then_inc(s_we, 16)
            sp.dma_start(WGU1[:, :, :], wgu1).then_inc(s_we, 16)
            sp.dma_start(WD1[:, 0:NE, :, :], wd1).then_inc(s_we, 16)
            sp.dma_start(WD1[:, NE, :, :], swd1).then_inc(s_we, 16)
            zv = z_dram.ap().rearrange("(t p) d -> p t d", p=128)
            for g in range(4):
                sp.wait_ge(S("z4a"), 3 * g + 3)
                sp.wait_ge(S("z4d"), g + 1)
                sp.dma_start(zv[:, 4 * g:4 * g + 4, :], Z4[:, 4 * g:4 * g + 4, :]).then_inc(S("z_rows"), 16)
            for b in range(SCATTERS):
                sp.wait_ge(S(f"scattered{b}"), 16 * len(range(b, SLOTS, SCATTERS)))
            yv = y_dram.ap()[0:2 * TOKENS, :].rearrange("(k t p) d -> p k t d", p=128, k=2)
            for g in range(4):
                for k in range(2):
                    sp.dma_start(YB[g][:, k, :, :], yv[:, k, 4 * g:4 * g + 4, :]).then_inc(S(f"y_in{g}"), 16)
            for g in range(4):
                sp.wait_ge(S("x5"), 4 * g + 4)
                sp.dma_start(outv[:, 4 * g:4 * g + 4, :], X[:, 4 * g:4 * g + 4, :]).then_inc(S("out"), 16)
            sp.wait_ge(S("out"), 64)

        def lead(i):
            return [i + k if 0 <= i + k < PAIRS else None for k in (3, 2, 1, 0, -1, -2)]

        STEPS = range(-3, PAIRS + 2)

        OUT = (1, 5, 6, 0)
        LB = (4, 7)
        BROW = (1, 3, 4, 5)

        def heads(ap):
            return ap.rearrange("p t (h d) -> p t h d", d=HD0)

        def p1_out(j, a, b):
            return P1[:, j, 64 * a:64 * b].rearrange("p (h d e) -> p h d e", d=HD0, e=HD0)

        def p1_k(q, j, a, b):
            e = E0[:, q, j, D + HD0 * a:D + HD0 * b].rearrange("p (h d) -> p h d", d=HD0)
            return e.unsqueeze(3).broadcast_to([128, b - a, HD0, HD0])

        def p1_v(q, j, a, b):
            v = QKV[:, q, j, 2 * D + HD0 * a:2 * D + HD0 * b].rearrange("p (h e) -> p h e", e=HD0)
            return v.unsqueeze(2).broadcast_to([128, b - a, HD0, HD0])

        def p2_out(j, a, b):
            return P2[:, j, 128 * a:128 * b].rearrange("p (d h e) -> p d h e", h=H0, e=HD0)

        def p2_q(q, j, a, b):
            v = QN[:, q, j, :].rearrange("p (h d) -> p d h", d=HD0)[:, a:b, :]
            return v.unsqueeze(3).broadcast_to([128, b - a, H0, HD0])

        def p2_t(j, a, b):
            v = TV[:, j, :].rearrange("p (d e) -> p d e", e=HD0)[:, a:b, :]
            return v.unsqueeze(2).broadcast_to([128, b - a, H0, HD0])

        K1, K2 = 11, 5

        @blk.scalar
        def _(act):
            act.dma_start(CM[:, 0:1], c0).then_inc(s_c, 16)
            act.dma_start(CM[:, 1:2], c1).then_inc(s_c, 16)
            act.dma_start(WM[:, 0, :], wmod0).then_inc(S("wmod_in0"), 16)
            act.dma_start(WM[:, 1, :], wmod1).then_inc(S("wmod_in1"), 16)
            act.dma_start(WD0i[:, :], wd0).then_inc(S("wd0_in"), 16)
            act.wait_ge(s_c, 32)
            nc.scalar.activation(SC[:, :], CM[:, :], ACT.Silu).then_inc(S("silu_c"), 1)
            act.wait_ge(S("mod_ps"), 1)
            nc.scalar.activation(MOD[:, :, :], B[5][:, 0:12].rearrange("p (l m) -> p l m", l=2), ACT.Copy)\
                .then_inc(S("mod_sb"), 1)

            def front_hT(p):
                act.wait_ge(S("zT_ps"), p + 1)
                if p == 0:
                    act.wait_ge(S("one_c"), 1)
                    act.wait_ge(S("mod_sb"), 1)
                nc.scalar.activation(HT[:, p % 2, :], B[0][:, 0:256], ACT.Identity, bias=MOD[:, 0, 0:1],
                                     scale=ONEC[:, 0, 0:1]).then_inc(S("hT"), 1)

            def front_qkv(p):
                act.wait_ge(S("qkv_ps"), p + 1)
                if p >= 2:
                    act.wait_ge(S("p1d"), 2 * (p - 1))
                    act.wait_ge(S("p1p"), 2 * (p - 1))
                for j in range(2):
                    nc.scalar.activation(QKV[:, p % 2, j, :], B[j][:, 0:3 * D], ACT.Copy).then_inc(S("qkv_sb"), 1)

            def front_exp(p):
                act.wait_ge(S("sub"), 2 * (p + 1))
                nc.scalar.activation(E0[:, p % 2, :, :], S0[:, p % 2, :, :], ACT.Exp).then_inc(S("exp"), 1)

            def mid_tvT(p, j):
                act.wait_ge(S("tvT_ps"), 2 * p + j + 1)
                nc.scalar.activation(TVT[:, j, :], B[3 + j][:, 0:128], ACT.Copy).then_inc(S("tvT"), 1)

            def mid_tv(p, j):
                act.wait_ge(S("tv_ps"), 2 * p + j + 1)
                if p >= 1:
                    act.wait_ge(S("p2p"), 2 * p - 1 + j)
                    act.wait_ge(S("p2d"), 2 * p - 1 + j)
                nc.scalar.activation(TV[:, j, :], B[3 + j][:, 128:192], ACT.Copy)\
                    .then_inc(S("tv"), 1)

            def mid_aT(p, j):
                act.wait_ge(S("aT_ps"), 2 * p + j + 1)
                if p == 0 and j == 0:
                    act.wait_ge(S("gate_ok"), 1)
                nc.scalar.activation(AT[:, j, :], B[3 + j][:, 192:320], ACT.Identity,
                                     scale=GT[:, 0, 0:1]).then_inc(S("aT"), 1)

            def back_h2T(p):
                act.wait_ge(S("z2T_ps"), p + 1)
                nc.scalar.activation(H2T[:, :], B[1][:, 0:256], ACT.Identity, bias=MOD[:, 0, 3:4],
                                     scale=ONEC[:, 0, 1:2]).then_inc(S("h2T"), 1)

            def back_silu(p):
                act.wait_ge(S("gu_ps"), 3 * p + 1)
                if p >= 1:
                    act.wait_ge(S("hid"), 2 * p)
                nc.scalar.activation(SG[:, 0:512], B[5][:, :], ACT.Silu, scale=1.0 / 127.0).then_inc(S("silu"), 1)
                act.wait_ge(S("gu_ps"), 3 * p + 2)
                nc.scalar.activation(SG[:, 512:768], B[6][:, 0:256], ACT.Silu, scale=1.0 / 127.0)\
                    .then_inc(S("silu"), 1)

            def w1_scale(w):
                nc.scalar.activation(W1s[:, w, :], W1[:, w, :], ACT.Copy, scale=ONEC[:, 1, 0:1])\
                    .then_inc(S("w1_scaled"), 1)

            for i in STEPS:
                n, f, a, m, b, _ = lead(i)
                if f is not None:
                    front_qkv(f)
                if m is not None:
                    mid_aT(m, 0)
                    mid_aT(m, 1)
                if f is not None:
                    front_exp(f)
                if i == 0:
                    act.wait_ge(S("wd0_ps"), 1)
                    nc.scalar.activation(WD0[:, :, :], B[7][:, 0:384].rearrange("p (c d) -> p c d", c=C0),
                                         ACT.Copy, scale=1.0 / (127.0 * 127.0)).then_inc(S("wd0_ok"), 1)
                    for w in (1, 2):
                        w1_scale(w)
                if b is not None:
                    back_silu(b)
                if a is not None:
                    mid_tvT(a, 0)
                    mid_tvT(a, 1)
                    mid_tv(a, 0)
                    mid_tv(a, 1)
                if m is not None:
                    back_h2T(m)
                if n is not None:
                    front_hT(n)
                if i == -1:
                    act.wait_ge(S("gate_ok"), 1)
                    act.wait_ge(S("wd0_in"), 16)
                    nc.scalar.activation(WD0g[:, :], WD0i[:, :], ACT.Identity, scale=GT[:, 0, 1:2])\
                        .then_inc(S("wd0_scaled"), 1)
                    act.wait_ge(s_w1, 128)
                    w1_scale(0)
                if i == 0:
                    act.wait_ge(S("prep_ps"), 1)
                    for h in range(2):
                        nc.scalar.activation(WQT[:, 4 * h:4 * h + 4, 0:128],
                                             B[5 + h][:, :].rearrange("p (c d) -> p c d", c=4), ACT.Copy)\
                            .then_inc(S("prep_sb"), 1)

            for g in range(4):
                act.wait_ge(S("z3T_ps"), g + 1)
                nc.scalar.activation(Z3T[:, 512 * g:512 * g + 512], B[6 + g % 2][:, :], ACT.Copy)\
                    .then_inc(S("z3T"), 1)
                if g == 1:
                    act.wait_ge(S("a_ps"), 3)
                    nc.scalar.activation(A1[:, 0:512], B[0][:, :], ACT.Copy).then_inc(S("a_sb"), 1)
            act.wait_ge(S("kv_zero"), 2)
            act.wait_ge(S("kv_ps"), 1)
            for lo in (0, 64):
                nc.scalar.activation(KV[lo:lo + 64, 0:4, lo:lo + 64],
                                     B[5][lo:lo + 64, :].rearrange("p (c k) -> p c k", c=4)[:, :, lo:lo + 64],
                                     ACT.Copy).then_inc(S("kv_sb_a"), 1)
            act.wait_ge(S("do_ps"), 1)
            nc.scalar.activation(DO[:, 0:4, :], B[0][:, :].rearrange("p (c d) -> p c d", c=4), ACT.Copy)\
                .then_inc(S("do_sb_a"), 1)
            act.wait_ge(S("mc_ps"), 1)
            nc.scalar.activation(MC[:, :], B[4][:, 0:128], ACT.Copy).then_inc(S("mc"), 1)
            for g in range(5):
                if g < 4:
                    act.wait_ge(S("nm4"), g + 1)
                    for t in range(4 * g, 4 * g + 3):
                        nc.scalar.activation(Z4[:, t, :], X[:, t, :], ACT.Identity, bias=NM[:, t:t + 1],
                                             scale=RS[:, 3, t:t + 1]).then_inc(S("z4a"), 1)
                if g >= 1:
                    act.wait_ge(S("h4T_ps"), g)
                    nc.scalar.activation(H4T[:, 512 * g - 512:512 * g], B[2 + (g - 1) % 2][:, :], ACT.Identity,
                                         bias=MOD[:, 1, 3:4], scale=ONEC[:, 1, 1:2]).then_inc(S("h4T"), 1)

            def shared_silu(n):
                act.wait_ge(S("sgu_ps"), n + 1)
                if n >= 2:
                    act.wait_ge(S("shid"), n - 1)
                nc.scalar.activation(SS[n % 2], B[6][:, :], ACT.Silu).then_inc(S("ssilu"), 1)

            act.wait_ge(S("rt_sub"), 1)
            nc.scalar.activation(PX[:, :, :], PR[:, :, :], ACT.Exp).then_inc(S("rt_exp"), 1)
            nc.scalar.activation(GATE[:, :], LG[:, :, NE], ACT.Exp, scale=-1.0).then_inc(S("gate_e"), 1)
            act.wait_ge(S("wk_sub"), 1)
            nc.scalar.activation(WK[:, 1, :], WK[:, 1, :], ACT.Exp).then_inc(S("wk_exp"), 1)
            for n in range(2):
                shared_silu(n)

            def expert_x(j):
                act.wait_ge(S("xt_ps"), j + 1)
                if j >= 3:
                    act.wait_ge(S("egu_ps"), j - 2)
                nc.scalar.activation(XT[j % 3], B[0][:, 0:128], ACT.Identity, bias=MOD[:, 1, 3:4],
                                     scale=ONEC[:, 1, 1:2]).then_inc(S("xt"), 1)

            def expert_silu(j):
                act.wait_ge(S("egu_ps"), j + 1)
                if j >= 2:
                    act.wait_ge(S("ehid"), j - 1)
                nc.scalar.activation(SX[j % 2], B[2 + j % 2][:, 0:FE], ACT.Silu).then_inc(S("esilu"), 1)

            for j in range(-3, SLOTS):
                if 0 <= j + 1 < SLOTS:
                    expert_silu(j + 1)
                if j + 3 < SLOTS:
                    expert_x(j + 3)
                if j in SHARED_AT and SHARED_AT[j][0] == "gu":
                    shared_silu(SHARED_AT[j][1])

        @blk.tensor
        def _(pe):
            mm = nc.tensor.matmul

            def front(p):
                for j in range(2):
                    pe.wait_ge(S("z"), 2 * p + j + 1)
                    if p >= 1 and j == 0:
                        pe.wait_ge(S("qkv_sb"), 2 * p)
                    last = mm(B[0][:, 128 * j:128 * j + 128], Z[:, p % 2, j, :], ident, start=True, stop=True,
                              is_transpose=True)
                last.then_inc(S("zT_ps"), 1)

            pe.wait_ge(S("warm"), 1)
            for n in range(WARM):
                mm(B[7][:, :], WARMUP[:, 0:128], WARMUP[:, :], start=True, stop=True)
            pe.wait_ge(s_cf, 16)
            front(0)
            pe.wait_ge(S("silu_c"), 1)
            for l in range(2):
                pe.wait_ge(S(f"wmod_in{l}"), 16)
                for m in range(6):
                    last = mm(B[5][:, 6 * l + m:6 * l + m + 1], WM[:, l, D * m:D * m + D], SC[:, l:l + 1],
                              start=True, stop=True)
            last.then_inc(S("mod_ps"), 1)

            def front_qkv(p):
                pe.wait_ge(S("hT"), p + 1)
                if p == 0:
                    pe.wait_ge(s_w0, 16)
                else:
                    pe.wait_ge(S("qkv_sb"), 2 * p)
                if p >= 3:
                    pe.wait_ge(S("h2T"), p - 2)
                for j in range(2):
                    last = mm(B[j][:, 0:3 * D], HT[:, p % 2, 128 * j:128 * j + 128], WQKV0[:, :],
                              start=True, stop=True)
                last.then_inc(S("qkv_ps"), 1)

            def mid_sum_heads(p, j):
                pe.wait_ge(S("p1d"), 2 * p + j + 1)
                pe.wait_ge(S("p1p"), 2 * p + j + 1)
                if p >= 1:
                    pe.wait_ge(S("x1"), 2 * (p - 1) + j + 1)
                for n in range(8):
                    last = mm(B[3 + j][:, 0:128], P1[:, j, 128 * n:128 * n + 128], ident,
                              start=(n == 0), stop=(n == 7), is_transpose=True)
                last.then_inc(S("tvT_ps"), 1)

            def mid_fold(p, j):
                pe.wait_ge(S("tvT"), 2 * p + j + 1)
                mm(B[3 + j][:, 128:192], TVT[:, j, :], fold, start=True, stop=True)\
                    .then_inc(S("tv_ps"), 1)

            def mid_sum_d(p, j):
                pe.wait_ge(S("p2d"), 2 * p + j + 1)
                pe.wait_ge(S("p2p"), 2 * p + j + 1)
                for n in range(8):
                    last = mm(B[3 + j][:, 192:320], P2[:, j, 128 * n:128 * n + 128], ident,
                              start=(n == 0), stop=(n == 7), is_transpose=True)
                last.then_inc(S("aT_ps"), 1)

            def mid_back(p, j):
                pe.wait_ge(S("aT"), 2 * p + j + 1)
                mm(B[3 + j][:, 320:448], AT[:, j, :], ident, start=True, stop=True,
                   is_transpose=True).then_inc(S("aB_ps"), 1)

            def back_T(p):
                for j in range(2):
                    pe.wait_ge(S("z2"), 2 * p + j + 1)
                    if j == 0:
                        pe.wait_ge(S("qkv_sb"), min(2 * (p + 3), T))
                    last = mm(B[1][:, 128 * j:128 * j + 128], Z2[:, j, :], ident, start=True, stop=True,
                              is_transpose=True)
                last.then_inc(S("z2T_ps"), 1)

            def back_gu(p, part):
                if part == 0:
                    pe.wait_ge(S("h2T"), p + 1)
                    if p == 0:
                        pe.wait_ge(S("w0_cast"), 1)
                    else:
                        pe.wait_ge(S("silu"), 2 * p)
                        pe.wait_ge(S("hid"), 2 * p)
                for n in (2 * part, 2 * part + 1):
                    w = (0, 1, 2, 5, 3, 4)[n]
                    last = mm(B[5 + n // 2][:, 256 * (n % 2):256 * (n % 2) + 256],
                              WGU0[:, 128 * w:128 * w + 128], H2T[:, :], start=True, stop=True)
                    if n % 2:
                        last.then_inc(S("gu_ps"), 1)

            def back_down(p):
                pe.wait_ge(S("hid"), 2 * (p + 1))
                if p == 0:
                    pe.wait_ge(S("wd0_ok"), 1)
                else:
                    pe.wait_ge(S("x2"), p)
                for j in range(2):
                    for n in range(C0):
                        last = mm(B[2][:, 256 + 128 * j:384 + 128 * j],
                                  HID[:, 256 * n + 128 * j:256 * n + 128 * j + 128], WD0[:, n, :],
                                  start=(n == 0), stop=(n == C0 - 1))
                last.then_inc(S("y_ps"), 1)

            def sum_tokens(a, b):
                if a == 0:
                    pe.wait_ge(S("qkv_sb"), T)
                    pe.wait_ge(S("z3_ones"), 1)
                pe.wait_ge(S("z3"), b)
                for t in range(a, b):
                    last = mm(B[0][:, 0:D + 1], Z3[:, t, 0:D], Z3[:, t, :], start=(t == 0), stop=(t == T - 1))
                if b == T:
                    last.then_inc(S("g_all"), 1)

            def bias_rows(a, b):
                if a == 0:
                    pe.wait_ge(S("x1"), T)
                    pe.wait_ge(S("h2T"), PAIRS)
                else:
                    pe.wait_ge(S("silu"), T)
                for n in range(a, b):
                    mm(B[BROW[n]][0:1, :], MOD[:, 1, 0:1], W1[:, 1 + n // 2, 512 * (n % 2):512 * (n % 2) + 512],
                       start=True, stop=True).then_inc(S("brow_ps"), 1)

            def z3T(g):
                if g >= 2:
                    pe.wait_ge(S("z3T"), g - 1)
                else:
                    pe.wait_ge(S("hid"), T)
                for t in range(4 * g, 4 * g + 4):
                    last = mm(B[6 + g % 2][:, 128 * (t % 4):128 * (t % 4) + 128], Z3[:, t, 0:D], ident,
                              start=True, stop=True, is_transpose=True)
                last.then_inc(S("z3T_ps"), 1)

            for i in STEPS:
                n, f, a, m, b, _ = lead(i)
                if f is not None:
                    front_qkv(f)
                if m is not None:
                    mid_sum_d(m, 0)
                    mid_sum_d(m, 1)
                if i == 0:
                    pe.wait_ge(S("wd0_scaled"), 1)
                    for c in range(C0):
                        last = mm(B[7][:, 128 * c:128 * c + 128], WD0g[:, 128 * c:128 * c + 128], ident,
                                  start=True, stop=True, is_transpose=True)
                    last.then_inc(S("wd0_ps"), 1)
                if i == PAIRS:
                    sum_tokens(0, 2 * (PAIRS - 2))
                if i == 1:
                    pe.wait_ge(S("prep_sb"), 2)
                if b is not None:
                    back_gu(b, 0)
                if m is not None:
                    mid_back(m, 0)
                if b is not None:
                    back_gu(b, 1)
                if m is not None:
                    mid_back(m, 1)
                if i == 0:
                    pe.wait_ge(S("w1_scaled"), 1)
                    for c in range(C1):
                        last = mm(B[5 + c // 4][:, 128 * (c % 4):128 * (c % 4) + 128],
                                  W1s[:, 0, 128 * c:128 * c + 128], ident, start=True, stop=True, is_transpose=True)
                    last.then_inc(S("prep_ps"), 1)
                if i == 1:
                    pe.wait_ge(S("gbb_sb"), 2)
                if b is not None:
                    back_gu(b, 2)
                if i == PAIRS:
                    bias_rows(0, 3)
                    sum_tokens(2 * (PAIRS - 2), 2 * (PAIRS - 1))
                if a is not None:
                    mid_sum_heads(a, 0)
                    mid_sum_heads(a, 1)
                    mid_fold(a, 0)
                    mid_fold(a, 1)
                if m is not None:
                    back_T(m)
                if n is not None and n > 0:
                    front(n)
                if b is not None:
                    back_down(b)
                if i == 0:
                    pe.wait_ge(S("wd0_ok"), 1)
                    pe.wait_ge(S("diag_gb"), 1)
                    for c in range(C1):
                        mm(B[7][:, c:c + 1], W1[:, 0, 128 * c:128 * c + 128], MOD[:, 1, 0:1], start=True, stop=True)
                    mm(B[7][:, 128:256], ones, DG[:, :], start=True, stop=True).then_inc(S("prep_ps"), 1)

            bias_rows(3, 4)
            z3T(0)
            z3T(1)
            sum_tokens(2 * (PAIRS - 1), T)

            pe.wait_ge(S("gz"), 1)
            mm(B[2][0:1, 0:128], GZ[:, D:D + 1], ident, start=True, stop=True).then_inc(S("mrow_ps"), 1)
            pe.wait_ge(S("brow_sb"), 4)
            for n in range(2):
                mm(B[3 + n][0:1, :], GZ[:, D:D + 1], W1s[:, 2, 512 * n:512 * n + 512], start=True, stop=True)\
                    .then_inc(S("a_ps"), 1)
            pe.wait_ge(S("mrow"), 1)
            for n in range(2):
                cols = slice(512 * n, 512 * n + 512)
                mm(B[n][:, :], GZ[:, 0:D], W1s[:, 2, cols], start=True, stop=False)
                mm(B[n][:, :], MROW[0:1, :], BKVs[0:1, 1, cols], start=False, stop=True).then_inc(S("a_ps"), 1)
            z3T(2)
            z3T(3)
            pe.wait_ge(S("a_sb"), 1)
            pe.wait_ge(S("a_sb_d"), 2)
            for c in range(C1):
                if c == 4:
                    pe.wait_ge(S("a_sb_d"), 3)
                cols = slice(128 * c, 128 * c + 128)
                o = B[(5, 2)[c // 4]][:, 128 * (c % 4):128 * (c % 4) + 128]
                mm(o, A1[:, cols], W1s[:, 1, cols], start=True, stop=False)
                last = mm(o, A1b[0:1, cols], BKVs[0:1, 0, cols], start=False, stop=True)
                if c % 4 == 3:
                    last.then_inc(S("kv_ps"), 1)
            for c in range(C1):
                if c == 0:
                    pe.wait_ge(S("kv_sb_a"), 2)
                if c == 4:
                    pe.wait_ge(S("kv_sb_d"), 2)
                last = mm(B[c // 4][:, 128 * (c % 4):128 * (c % 4) + 128], KV[:, c, :], WO1[:, c, :],
                          start=True, stop=True)
                if c % 4 == 3:
                    last.then_inc(S("do_ps"), 1)
            for c in range(C1):
                if c == 0:
                    pe.wait_ge(S("do_sb_a"), 1)
                if c == 4:
                    pe.wait_ge(S("do_sb_d"), 1)
                last = mm(B[3][:, 0:D + 1], DO[:, c, :], WQT[:, c, :], start=(c == 0), stop=(c == C1 - 1))
            last.then_inc(S("mt_ps"), 1)
            pe.wait_ge(S("mt_step"), 2)
            mm(B[4][:, 0:128], MT[:, 0:128], ident, start=True, stop=True, is_transpose=True)\
                .then_inc(S("mc_ps"), 1)

            def attend(g):
                if g == 0:
                    pe.wait_ge(S("mt_step"), 3)
                for t in range(4):
                    mm(B[OUT[g]][:, 128 * t:128 * t + 128], ones, DG[:, :], start=True, stop=False)
                    if g == 0 and t == 0:
                        pe.wait_ge(S("mc"), 1)
                        pe.wait_ge(S("z3T"), 4)
                    last = mm(B[OUT[g]][:, 128 * t:128 * t + 128], Z3T[:, 512 * g + 128 * t:512 * g + 128 * t + 128],
                              MC[:, :], start=False, stop=True)
                last.then_inc(S("o_ps"), 1)

            def h4T(g):
                if g >= 2:
                    pe.wait_ge(S("h4T"), g - 1)
                pe.wait_ge(S("z4a"), 3 * g + 3)
                pe.wait_ge(S("z4d"), g + 1)
                for t in range(4 * g, 4 * g + 4):
                    last = mm(B[2 + g % 2][:, 128 * (t % 4):128 * (t % 4) + 128], Z4[:, t, :], ident,
                              start=True, stop=True, is_transpose=True)
                last.then_inc(S("h4T_ps"), 1)

            def logits(g):
                pe.wait_ge(S("h4T"), g + 1)
                for t in range(4 * g, 4 * g + 4):
                    last = mm(B[LB[g // 2]][:, 9 * t:9 * t + 9], H4T[:, 128 * t:128 * t + 128], RT[:, :],
                              start=True, stop=True)
                last.then_inc(S("lg_ps"), 1)

            def shared_gu(n):
                g, f = n // 2, n % 2
                if n == 0:
                    pe.wait_ge(S("x3"), 4)
                    pe.wait_ge(S("picked"), 4)
                else:
                    pe.wait_ge(S("ssilu"), n)
                    pe.wait_ge(S("shid"), n)
                cols = slice(512 * g, 512 * g + 512)
                mm(B[6][:, :], SGU[:, 128 * f:128 * f + 128], H4T[:, cols], start=True, stop=True)
                mm(B[7][:, :], SGU[:, FE + 128 * f:FE + 128 * f + 128], H4T[:, cols],
                   start=True, stop=True).then_inc(S("sgu_ps"), 1)

            def shared_down(g):
                pe.wait_ge(S("shid"), 2 * g + 2)
                if g >= 1:
                    pe.wait_ge(S("x4"), 4 * g)
                for t in range(4):
                    for f in range(2):
                        last = mm(B[1][:, 128 * t:128 * t + 128],
                                  HS[g % 2][:, 512 * f + 128 * t:512 * f + 128 * t + 128], WD1g[:, NE, f, :],
                                  start=(f == 0), stop=(f == 1))
                last.then_inc(S("sy_ps"), 1)

            pe.wait_ge(s_we, 96)
            pe.wait_ge(S("wd1_scaled"), NE + 1)
            for g in range(4):
                attend(g)
            def stay_warm(n):
                for _ in range(n):
                    mm(B[1][:, 0:128], ones_h, iota_h, start=True, stop=True)

            for g in range(5):
                if g < 4:
                    h4T(g)
                if g >= 1:
                    logits(g - 1)
                stay_warm(FILL[g])

            def ranks():
                pe.wait_ge(S("picked"), 4)
                M = MH[:, :, :].rearrange("p t e -> p (t e)")
                for n in range(T + 1):
                    if n == 0:
                        mm(B[2][:, 0:8 * T + 8], tri_h, M, start=True, stop=False)
                    else:
                        last = mm(B[2][:, 8 * n:8 * T + 8], ones_h, M[:, 0:8 * (T + 1 - n)],
                                  start=False, stop=(n == T))
                last.then_inc(S("rank_ps"), 1)

            def places():
                pe.wait_ge(S("token_hot"), 1)
                for n in range(2 * T):
                    k = n // T
                    if n == T:
                        pe.wait_ge(S("token_hot"), 2)
                    if n % 8 == 0:
                        pe.wait_ge(S("row_hot"), n // 8 + 1)
                    last = mm(B[4][:, 2 * SLOTS * k:2 * SLOTS * k + 2 * SLOTS], BH[:, n, :], AH[:, n, :],
                              start=(n % T == 0), stop=(n % T == T - 1))
                last.then_inc(S("idx_ps"), 1)

            ranks()
            shared_gu(0)
            stay_warm(FILL[5])
            places()
            shared_gu(1)

            def expert_x(j):
                pe.wait_ge(S(f"gathered{j % GATHERS}"), 16 * (j // GATHERS + 1))
                if j >= 1:
                    pe.wait_ge(S("xt"), j)
                mm(B[0][:, 0:128], GX[j % GATHERS], ident, start=True, stop=True, is_transpose=True)\
                    .then_inc(S("xt_ps"), 1)

            def expert_gu(j, e):
                pe.wait_ge(S("xt"), j + 1)
                if j >= 2:
                    pe.wait_ge(S("ehid"), j - 1)
                w = WGU1[:, :, :].rearrange("p e f -> p (e f)")
                mm(B[2 + j % 2][:, :], XT[j % 3], w[:, bass.ds(e * (2 * FE), 2 * FE)], start=True, stop=True)\
                    .then_inc(S("egu_ps"), 1)

            def expert_hT(j):
                pe.wait_ge(S("ehid"), j + 1)
                if j >= 1:
                    pe.wait_ge(S("ht"), j)
                for f in range(2):
                    last = mm(B[4][:, 128 * f:128 * f + 128], HX[j % 2][:, 128 * f:128 * f + 128], ident,
                              start=True, stop=True, is_transpose=True)
                last.then_inc(S("ht_ps"), 1)

            def expert_down(j, e):
                pe.wait_ge(S("ht"), j + 1)
                if j >= 1:
                    pe.wait_ge(S("ey"), j)
                w = WD1g[:, :, :, :].rearrange("p e f d -> p (e f d)")
                for f in range(2):
                    last = mm(B[5][:, 0:128], HXT[j % 2][:, 128 * f:128 * f + 128],
                              w[:, bass.ds(e * (2 * D) + f * D, D)], start=(f == 0), stop=(f == 1))
                last.then_inc(S("ey_ps"), 1)

            pe.wait_ge(S("idx"), 1)
            held = {}
            for j in range(-3, SLOTS + 1):
                if 0 <= j + 1 < SLOTS:
                    expert_gu(j + 1, held[j + 1])
                if j + 3 < SLOTS:
                    held[j + 3] = pe.value_load(EXI[0:1, j + 3:j + 4], min_val=0, max_val=NE - 1)
                    expert_x(j + 3)
                if 0 <= j - 1:
                    expert_down(j - 1, held.pop(j - 1))
                if 0 <= j < SLOTS:
                    expert_hT(j)
                if j in SHARED_AT:
                    kind, n = SHARED_AT[j]
                    if kind == "gu":
                        shared_gu(n)
                    else:
                        shared_down(n)

        @blk.vector
        def _(dve):
            V = nc.vector
            steps = [0]

            def link(ins):
                steps[0] += 1
                ins.then_inc(S("dve_step"), 1)
                dve.wait_ge(S("dve_step"), steps[0])

            V.memset(WARMUP[:, :], 0.0).then_inc(S("warm"), 1)
            V.memset(minus_half[:, :], -0.5).then_inc(S("half_set"), 1)
            V.memset(Z3[:, :, D:D + 1], 1.0).then_inc(S("z3_ones"), 1)
            def norm(dst, t, k, done):
                V.tensor_scalar(dst, X[:, t, :], MV[:, k, t, 0:1], RS[:, k, t:t + 1], ALU.subtract, ALU.mult)\
                    .then_inc(S(done), 1)

            stated = [0]

            def bn(tiles):
                for t in tiles:
                    V.bn_stats(ST[:, t, :], X[:, t, :]).then_inc(S("st"), 1)
                stated[0] += len(tiles)
                dve.wait_ge(S("st"), stated[0])

            def front_z(p):
                dve.wait_ge(S("rs"), p // 2 + 1)
                if p >= 2:
                    dve.wait_ge(S("zT_ps"), p - 1)
                for j in range(2):
                    norm(Z[:, p % 2, j, :], 2 * p + j, 0, "z")

            for g in range(4):
                dve.wait_ge(S(f"x_in{g}"), 16)
                bn(range(4 * g, 4 * g + 4))
                for t in range(4 * g, 4 * g + 4):
                    V.bn_aggr(MV[:, 0, t, :], ST[:, t, :]).then_inc(S("mv"), 1)
                if g == 1:
                    front_z(0)
            dve.wait_ge(S("mod_sb"), 1)
            V.tensor_scalar(ONEC[:, :, :], MOD[:, :, 1:5:3], 1.0, None, ALU.add).then_inc(S("one_c"), 1)
            link(V.tensor_scalar(GS[:, :, :], MOD[:, :, 2:6:3], 0.0, 2.0, ALU.is_ge, ALU.mult))
            link(V.tensor_scalar(GS[:, :, :], GS[:, :, :], -1.0, None, ALU.add))
            link(V.tensor_scalar(GA[:, :, :], MOD[:, :, 2:6:3], -1.0, None, ALU.mult))
            link(V.tensor_tensor(GA[:, :, :], GA[:, :, :], MOD[:, :, 2:6:3], ALU.max))
            link(V.tensor_scalar(GA[:, :, :], GA[:, :, :], 0.25, None, ALU.max))
            V.tensor_tensor(GT[:, :, :], GA[:, :, :], GS[:, :, :], ALU.mult).then_inc(S("gate_ok"), 1)

            def front_max(p):
                q = p % 2
                dve.wait_ge(S("qkv_sb"), 2 * (p + 1))
                if p >= 2:
                    dve.wait_ge(S("sub"), 2 * (p - 1))
                V.tensor_reduce(MX[:, q, 0:32].rearrange("p (t h) -> p t h", t=2), heads(QKV[:, q, :, 0:D]),
                                axis=AX.X, op=ALU.max).then_inc(S("mx"), 1)
                V.tensor_reduce(MX[:, q, 32:48].rearrange("p (t d) -> p t d", t=2),
                                QKV[:, q, :, D:2 * D].rearrange("p t (h d) -> p t d h", d=HD0),
                                axis=AX.X, op=ALU.max).then_inc(S("mx"), 1)

            def front_sum(p):
                q = p % 2
                dve.wait_ge(S("exp"), p + 1)
                V.tensor_reduce(SM[:, q, 0:32].rearrange("p (t h) -> p t h", t=2), heads(E0[:, q, :, 0:D]),
                                axis=AX.X, op=ALU.add).then_inc(S("sum"), 1)
                V.tensor_reduce(SM[:, q, 32:48].rearrange("p (t d) -> p t d", t=2),
                                E0[:, q, :, D:2 * D].rearrange("p t (h d) -> p t d h", d=HD0),
                                axis=AX.X, op=ALU.add).then_inc(S("sum"), 1)
                dve.wait_ge(S("sum"), 2 * (p + 1))
                if p >= 2:
                    dve.wait_ge(S("qn"), p - 1)
                V.reciprocal(RC[:, q, :], SM[:, q, :]).then_inc(S("rec"), 1)

            def mid_p1(p, j):
                if p >= 1:
                    dve.wait_ge(S("tvT_ps"), 2 * (p - 1) + j + 1)
                V.tensor_tensor(p1_out(j, 0, K1), p1_k(p % 2, j, 0, K1), p1_v(p % 2, j, 0, K1), ALU.mult)\
                    .then_inc(S("p1d"), 1)

            def mid_p2(p, j):
                dve.wait_ge(S("tv"), 2 * p + j + 1)
                if j == 0:
                    dve.wait_ge(S("qn"), p + 1)
                if p >= 1:
                    dve.wait_ge(S("aT_ps"), 2 * (p - 1) + j + 1)
                V.tensor_tensor(p2_out(j, 0, K2), p2_q(p % 2, j, 0, K2), p2_t(j, 0, K2), ALU.mult)\
                    .then_inc(S("p2d"), 1)

            def mid_x1(p, j):
                t = 2 * p + j
                dve.wait_ge(S("aB_ps"), t + 1)
                V.tensor_tensor(X[:, t, :], B[3 + j][:, 320:448], X[:, t, :], ALU.add)\
                    .then_inc(S("x1"), 1)

            def stats(p, k, ready, count, mv):
                dve.wait_ge(S(ready), count)
                bn(range(2 * p, 2 * p + 2))
                for j in range(2):
                    t = 2 * p + j
                    V.bn_aggr(MV[:, k, t, :], ST[:, t, :]).then_inc(S(mv), 1)

            def back_z2(p):
                dve.wait_ge(S("rs2"), p + 1)
                if p >= 1:
                    dve.wait_ge(S("z2T_ps"), p)
                for j in range(2):
                    norm(Z2[:, j, :], 2 * p + j, 1, "z2")

            def back_hid(p):
                dve.wait_ge(S("gu_ps"), 3 * (p + 1))
                dve.wait_ge(S("silu"), 2 * (p + 1))
                if p >= 1:
                    dve.wait_ge(S("y_ps"), p)
                V.tensor_tensor(HID[:, 0:512], SG[:, 0:512], B[7][:, :], ALU.mult).then_inc(S("hid"), 1)
                V.tensor_tensor(HID[:, 512:768], SG[:, 512:768], B[6][:, 256:512], ALU.mult).then_inc(S("hid"), 1)

            def back_x2(p):
                t = 2 * p
                dve.wait_ge(S("y_ps"), p + 1)
                V.tensor_tensor(X[:, t:t + 2, :], B[2][:, 256:512].rearrange("p (t d) -> p t d", t=2),
                                X[:, t:t + 2, :], ALU.add).then_inc(S("x2"), 1)

            def bias_rows():
                dve.wait_ge(s_w1, 128)
                for n, bank in enumerate(BROW):
                    cols = slice(512 * (n % 2), 512 * (n % 2) + 512)
                    dve.wait_ge(S("brow_ps"), n + 1)
                    V.tensor_tensor(BKVs[0:1, n // 2, cols], B[bank][0:1, :], BKV[0:1, n // 2, cols], ALU.add)\
                        .then_inc(S("brow_sb"), 1)
                dve.wait_ge(S("brow_sb"), 4)
                V.tensor_scalar(NBV[0:1, :], BKVs[0:1, 1, :], float(TOKENS), None, ALU.mult).then_inc(S("nbv"), 1)

            def back_z3(p):
                dve.wait_ge(S("rs3"), p + 1)
                for j in range(2):
                    norm(Z3[:, 2 * p + j, 0:D], 2 * p + j, 2, "z3")

            for i in STEPS:
                n, f, a, m, b, c = lead(i)
                if m is not None:
                    mid_p2(m, 0)
                    mid_p2(m, 1)
                if a is not None:
                    mid_p1(a, 0)
                    mid_p1(a, 1)
                if i == 1:
                    dve.wait_ge(S("prep_ps"), 2)
                    dve.wait_ge(s_w1, 128)
                    V.tensor_tensor(WQT[:, :, D:D + 1], B[7][:, 0:C1].unsqueeze(2), BQC[:, :].unsqueeze(2), ALU.add)\
                        .then_inc(S("gbb_sb"), 1)
                    V.tensor_copy(GBB[:, :], B[7][:, 128:256]).then_inc(S("gbb_sb"), 1)
                if f is not None:
                    front_max(f)
                if c is not None:
                    back_x2(c)
                    stats(c, 2, "x2", c + 1, "mv3")
                if m is not None:
                    mid_x1(m, 0)
                    mid_x1(m, 1)
                    stats(m, 1, "x1", 2 * m + 2, "mv2")
                if n is not None and n > 0:
                    front_z(n)
                if c is not None:
                    back_z3(c)
                if m is not None:
                    back_z2(m)
                if b is not None:
                    back_hid(b)
                if i == PAIRS:
                    bias_rows()
                if f is not None:
                    front_sum(f)
            dve.wait_ge(S("g_all"), 1)
            V.tensor_copy(GZ[:, :], B[0][:, 0:D + 1]).then_inc(S("gz"), 1)
            dve.wait_ge(S("mrow_ps"), 1)
            V.tensor_copy(MROW[0:1, :], B[2][0:1, 0:128]).then_inc(S("mrow"), 1)
            dve.wait_ge(S("nbv"), 1)
            for n in range(2):
                cols = slice(512 * n, 512 * n + 512)
                dve.wait_ge(S("a_ps"), n + 1)
                V.tensor_tensor(A1b[0:1, cols], B[3 + n][0:1, :], NBV[0:1, cols], ALU.add).then_inc(S("a_sb_d"), 1)
            dve.wait_ge(S("a_ps"), 4)
            V.tensor_copy(A1[:, 512:1024], B[1][:, :]).then_inc(S("a_sb_d"), 1)
            dve.wait_ge(S("kv_ps"), 2)
            dve.wait_ge(S("kv_zero"), 2)
            for lo in (0, 64):
                V.tensor_copy(KV[lo:lo + 64, 4:8, lo:lo + 64],
                              B[2][lo:lo + 64, :].rearrange("p (c k) -> p c k", c=4)[:, :, lo:lo + 64])\
                    .then_inc(S("kv_sb_d"), 1)
            dve.wait_ge(S("do_ps"), 2)
            V.tensor_copy(DO[:, 4:8, :], B[1][:, :].rearrange("p (c d) -> p c d", c=4)).then_inc(S("do_sb_d"), 1)
            dve.wait_ge(S("mt_ps"), 1)
            V.tensor_scalar(MT[:, :], B[3][:, 0:D + 1], GT[:, 1, 0:1], SCALE1, ALU.mult, ALU.mult)\
                .then_inc(S("mt_step"), 1)
            dve.wait_ge(S("mt_step"), 1)
            dve.wait_ge(S("bog"), 1)
            V.tensor_tensor(MT[:, D:D + 1], MT[:, D:D + 1], BOG[:, :], ALU.add).then_inc(S("mt_step"), 1)
            dve.wait_ge(S("mt_step"), 2)
            V.tensor_scalar(DG[:, :], ident, MT[:, D:D + 1], None, ALU.mult).then_inc(S("mt_step"), 1)

            def attend(g):
                ts = slice(4 * g, 4 * g + 4)
                dve.wait_ge(S("o_ps"), g + 1)
                V.tensor_tensor(X[:, ts, :], B[OUT[g]][:, :].rearrange("p (t d) -> p t d", t=4), X[:, ts, :],
                                ALU.add).then_inc(S("x3"), 1)
                dve.wait_ge(S("x3"), g + 1)
                bn(range(4 * g, 4 * g + 4))
                for t in range(4 * g, 4 * g + 4):
                    V.bn_aggr(MV[:, 3, t, :], ST[:, t, :]).then_inc(S("mv4"), 1)

            def last_norm(g):
                ts = slice(4 * g, 4 * g + 4)
                dve.wait_ge(S("rs4"), g + 1)
                V.scalar_tensor_tensor(out=NM[:, ts], in0=MV[:, 3, ts, 0], scalar=-1.0, in1=RS[:, 3, ts],
                                       op0=ALU.mult, op1=ALU.mult).then_inc(S("nm4"), 1)
                norm(Z4[:, 4 * g + 3, :], 4 * g + 3, 3, "z4d")

            for g in range(5):
                if g < 4:
                    attend(g)
                if g >= 1:
                    last_norm(g - 1)

            def over_e(ap):
                return ap.unsqueeze(2).broadcast_to([128, T, NE])

            def shared_hid(n):
                dve.wait_ge(S("ssilu"), n + 1)
                if n >= 4:
                    dve.wait_ge(S("sy_ps"), n // 2 - 1)
                V.tensor_tensor(HS[n // 2 % 2][:, 512 * (n % 2):512 * (n % 2) + 512], SS[n % 2], B[7][:, :], ALU.mult)\
                    .then_inc(S("shid"), 1)

            def shared_x4(g):
                dve.wait_ge(S("sy_ps"), g + 1)
                for t in range(4 * g, 4 * g + 4):
                    V.scalar_tensor_tensor(out=X[:, t, :], in0=B[1][:, 128 * (t % 4):128 * (t % 4) + 128],
                                           scalar=GATE[:, t:t + 1], in1=X[:, t, :], op0=ALU.mult, op1=ALU.add)\
                        .then_inc(S("x4"), 1)

            def do(ins):
                steps[0] += 1
                ins.then_inc(S("dve_step"), 1)
                return steps[0]

            def after(n):
                dve.wait_ge(S("dve_step"), n)

            def pick(groups):
                dve.wait_ge(S("lg_ps"), max(groups) + 1)
                done = {}

                def both(make):
                    for g in groups:
                        if g in done:
                            after(done[g])
                        done[g] = do(make(slice(4 * g, 4 * g + 4)))

                def over(ap):
                    return ap.unsqueeze(2).broadcast_to([128, 4, NE])

                w = first_w.unsqueeze(1).broadcast_to([128, 4, NE])
                both(lambda ts: V.tensor_copy(LG[:, ts, :], B[LB[ts.start // 8]][:, 9 * ts.start:9 * ts.stop]
                                              .rearrange("p (t e) -> p t e", e=9)))
                for k in range(2):
                    L = (LG[:, :, 0:NE], L2)[k]
                    both(lambda ts: V.tensor_reduce(TOP[:, k, ts], L[:, ts, :], axis=AX.X, op=ALU.max))
                    both(lambda ts: V.tensor_tensor(SCR[:, ts, :], L[:, ts, :], over(TOP[:, k, ts]), ALU.is_equal))
                    both(lambda ts: V.tensor_tensor(SCR[:, ts, :], SCR[:, ts, :], w, ALU.mult))
                    both(lambda ts: V.tensor_reduce(RM[:, ts], SCR[:, ts, :], axis=AX.X, op=ALU.max))
                    both(lambda ts: V.tensor_tensor(OH[:, k, ts, :], SCR[:, ts, :], over(RM[:, ts]), ALU.is_equal))
                    if k == 0:
                        both(lambda ts: V.scalar_tensor_tensor(out=L2[:, ts, :], in0=OH[:, 0, ts, :], scalar=-1e30,
                                                               in1=LG[:, ts, 0:NE], op0=ALU.mult, op1=ALU.add))
                for g in groups:
                    ts = slice(4 * g, 4 * g + 4)
                    after(done[g])
                    V.tensor_tensor(MH[:, ts, :], OH[:, 0, ts, :], OH[:, 1, ts, :], ALU.add)\
                        .then_inc(S("picked"), 1)

            pick((0, 1))
            pick((2, 3))
            V.tensor_tensor(PR[:, :, :], LG[:, :, 0:NE], over_e(TOP[:, 0, :]), ALU.subtract).then_inc(S("rt_sub"), 1)
            V.tensor_tensor(WK[:, 1, :], TOP[:, 1, :], TOP[:, 0, :], ALU.subtract).then_inc(S("wk_sub"), 1)

            dve.wait_ge(S("rank_ps"), 1)
            tiles = do(V.tensor_scalar(NTF[:, :], B[2][:, 8 * T:8 * T + 8], 1.0 / 128, 63.5 / 128, ALU.mult, ALU.add))
            sel = do(V.tensor_tensor(OHR[:, :, :, :], OH[:, :, :, :], B[2][:, 0:8 * T]
                                     .rearrange("p (t e) -> p t e", e=8).unsqueeze(1)
                                     .broadcast_to([128, 2, T, NE]), ALU.mult))
            after(tiles)
            tiles = do(V.tensor_scalar(NTF[:, :], NTF[:, :], MAGIC, -MAGIC, ALU.add, ALU.add))
            after(sel)
            rank = do(V.tensor_reduce(RANK[:, :], OHR[:, :, :, :].rearrange("p k t e -> p (k t) e"),
                                      axis=AX.X, op=ALU.add))
            after(tiles)
            start = do(V.tensor_tensor(STT[:, :, :], before.rearrange("p (e f) -> p e f", e=8),
                                       NTF[:, :].unsqueeze(1).broadcast_to([128, NE, NE]), ALU.mult))
            after(rank)
            row = do(V.tensor_scalar(RTILE[:, :], RANK[:, :], 1.0 / 128, -63.5 / 128, ALU.mult, ALU.add))
            after(start)
            start = do(V.tensor_reduce(START[:, :], STT[:, :, :], axis=AX.X, op=ALU.add))
            after(row)
            row = do(V.tensor_scalar(RTILE[:, :], RTILE[:, :], MAGIC, -MAGIC, ALU.add, ALU.add))
            after(start)
            sel = do(V.tensor_tensor(OHS[:, :, :, :], OH[:, :, :, :], START[:, :].unsqueeze(1).unsqueeze(1)
                                     .broadcast_to([128, 2, T, NE]), ALU.mult))
            after(row)
            row = do(V.scalar_tensor_tensor(out=ROW[:, :], in0=RTILE[:, :], scalar=-128.0, in1=RANK[:, :],
                                            op0=ALU.mult, op1=ALU.add))
            after(sel)
            tile = do(V.tensor_reduce(FIRST[:, :], OHS[:, :, :, :].rearrange("p k t e -> p (k t) e"),
                                      axis=AX.X, op=ALU.add))
            end = do(V.tensor_tensor(ENDT[:, :], START[:, :], NTF[:, :], ALU.add))
            after(tile)
            tile = do(V.tensor_tensor(TILE[:, :], FIRST[:, :], RTILE[:, :], ALU.add))
            after(tile)
            for k in range(2):
                V.tensor_tensor(AH[:, T * k:T * k + T, SLOTS:2 * SLOTS],
                                TILE[:, T * k:T * k + T].unsqueeze(2).broadcast_to([128, T, SLOTS]),
                                iota_h[:, 0:SLOTS].unsqueeze(1).broadcast_to([128, T, SLOTS]), ALU.is_equal)\
                    .then_inc(S("tile_hot"), 1)
            for n in range(0, 2 * T, 8):
                V.tensor_tensor(BH[:, n:n + 8, :], iota_h.unsqueeze(1).broadcast_to([128, 8, 128]),
                                ROW[:, n:n + 8].unsqueeze(2).broadcast_to([128, 8, 128]), ALU.is_equal)\
                    .then_inc(S("row_hot"), 1)
            shared_hid(0)
            dve.wait_ge(S("idx_ps"), 1)
            link(V.tensor_copy(IDX[:, :, :, :], B[4][:, 0:4 * SLOTS].rearrange("p (k w s) -> p k w s", k=2, w=2)))
            V.tensor_tensor(GI[:, :], IDX[:, 0, 0, :], IDX[:, 1, 0, :], ALU.add).then_inc(S("gather_idx"), 1)
            after(end)
            link(V.tensor_tensor(GEQ[0:1, :, :], slot_iota[0:1, :].unsqueeze(2).broadcast_to([1, SLOTS, NE]),
                                 ENDT[0:1, :].unsqueeze(1).broadcast_to([1, SLOTS, NE]), ALU.is_ge))
            link(V.tensor_reduce(EXF[0:1, :], GEQ[0:1, :, :], axis=AX.X, op=ALU.add))
            link(V.tensor_scalar(EXI[0:1, :], EXF[0:1, :], NE - 1.0, None, ALU.min))
            a = do(V.tensor_tensor(ANY[:, :], IDX[:, 0, 1, :], IDX[:, 1, 1, :], ALU.add))
            d = do(V.scalar_tensor_tensor(out=DF[:, :], in0=IDX[:, 1, 1, :], scalar=float(TOKENS),
                                          in1=IDX[:, 1, 0, :], op0=ALU.mult, op1=ALU.add))
            after(a)
            do(V.scalar_tensor_tensor(out=PADF[:, :], in0=ANY[:, :], scalar=0.0, in1=pad_row,
                                      op0=ALU.is_equal, op1=ALU.mult))
            after(d)
            d = do(V.tensor_tensor(DF[:, :], DF[:, :], IDX[:, 0, 0, :], ALU.add))
            after(d)
            V.tensor_tensor(DI[:, :], DF[:, :], PADF[:, :], ALU.add).then_inc(S("idx"), 1)
            dve.wait_ge(S("rt_exp"), 1)
            s1 = do(V.tensor_reduce(RSUM[:, :], PX[:, :, :], axis=AX.X, op=ALU.add))
            dve.wait_ge(S("gate_e"), 1)
            s2 = do(V.tensor_scalar(GATE[:, :], GATE[:, :], 1.0, None, ALU.add))
            after(s1)
            s1 = do(V.reciprocal(WK[:, 0, :], RSUM[:, :]))
            after(s2)
            V.reciprocal(GATE[:, :], GATE[:, :]).then_inc(S("gate"), 1)
            dve.wait_ge(S("wk_exp"), 1)
            after(s1)
            link(V.tensor_tensor(WK[:, 1, :], WK[:, 1, :], WK[:, 0, :], ALU.mult))
            dve.wait_ge(S("gate"), 1)
            shared_hid(1)


            def expert_hid(j):
                dve.wait_ge(S("esilu"), j + 1)
                if j >= 2:
                    dve.wait_ge(S("ht_ps"), j - 1)
                V.tensor_tensor(HX[j % 2], SX[j % 2], B[2 + j % 2][:, FE:2 * FE], ALU.mult).then_inc(S("ehid"), 1)

            def expert_hT(j):
                dve.wait_ge(S("ht_ps"), j + 1)
                if j >= 2:
                    dve.wait_ge(S("ey_ps"), j - 1)
                V.tensor_copy(HXT[j % 2], B[4][:, 0:2 * 128]).then_inc(S("ht"), 1)

            def expert_y(j):
                dve.wait_ge(S("ey_ps"), j + 1)
                if j >= SCATTERS:
                    dve.wait_ge(S(f"scattered{j % SCATTERS}"), 16 * (j // SCATTERS))
                V.tensor_copy(YX[j % SCATTERS], B[5][:, 0:128]).then_inc(S("ey"), 1)

            for j in range(-3, SLOTS + 1):
                if 0 <= j - 1:
                    expert_y(j - 1)
                if 0 <= j < SLOTS:
                    expert_hT(j)
                if 0 <= j + 1 < SLOTS:
                    expert_hid(j + 1)
                if j in SHARED_AT:
                    kind, n = SHARED_AT[j]
                    if kind == "gu":
                        shared_hid(n)
                    else:
                        shared_x4(n)

            for g in range(4):
                dve.wait_ge(S(f"y_in{g}"), 32)
                for k in range(2):
                    if k == 1:
                        dve.wait_ge(S("part"), 4 * g + 4)
                    for t in range(4 * g, 4 * g + 4):
                        V.scalar_tensor_tensor(out=X[:, t, :], in0=YB[g][:, k, t % 4, :], scalar=WK[:, k, t:t + 1],
                                               in1=X[:, t, :], op0=ALU.mult, op1=ALU.add)\
                            .then_inc(S("x5" if k else "part"), 1)

        @blk.gpsimd
        def _(pool):
            G = nc.gpsimd

            added = [0]

            def rstd(k, a, b, mv, rs):
                pool.wait_ge(S(mv), b)
                G.tensor_scalar(VE[:, k, a:b], MV[:, k, a:b, 1], EPS, None, ALU.add).then_inc(S("var_eps"), 1)
                added[0] += 1
                pool.wait_ge(S("var_eps"), added[0])
                G.tensor_tensor(RS[:, k, a:b], VE[:, k, a:b], minus_half[:, a:b], ALU.pow).then_inc(S(rs), 1)

            pool.wait_ge(S("half_set"), 1)
            for g in range(4):
                rstd(0, 4 * g, 4 * g + 4, "mv", "rs")
            pool.wait_ge(s_wi, 16)
            G.tensor_copy(WGU0[:, :], WGU0i[:, :]).then_inc(S("w0_cast"), 1)

            def layer1_weights():
                pool.wait_ge(s_w1, 128)
                pool.wait_ge(S("one_c"), 1)
                pool.wait_ge(S("gate_ok"), 1)
                pool.wait_ge(s_cf, 16)
                G.tensor_scalar(DG[:, :], ident, GT[:, 1, 1:2], None, ALU.mult).then_inc(S("diag_gb"), 1)
                G.tensor_scalar(BOG[:, :], BO[:, :], GT[:, 1, 0:1], None, ALU.mult).then_inc(S("bog"), 1)
                G.memset(MH[:, :, :], 0.0).then_inc(S("kv_zero"), 1)
                G.memset(KV[:, :, :], 0.0).then_inc(S("kv_zero"), 1)

            def front_sub(p):
                q = p % 2
                pool.wait_ge(S("mx"), 2 * (p + 1))
                if p >= 2:
                    pool.wait_ge(S("exp"), p - 1)
                G.tensor_tensor(heads(S0[:, q, :, 0:D]), heads(QKV[:, q, :, 0:D]),
                                MX[:, q, 0:32].rearrange("p (t h) -> p t h", t=2).unsqueeze(3)
                                .broadcast_to([128, 2, H0, HD0]), ALU.subtract).then_inc(S("sub"), 1)
                G.tensor_tensor(heads(S0[:, q, :, D:2 * D]), heads(QKV[:, q, :, D:2 * D]),
                                MX[:, q, 32:48].rearrange("p (t d) -> p t d", t=2).unsqueeze(2)
                                .broadcast_to([128, 2, H0, HD0]), ALU.subtract).then_inc(S("sub"), 1)

            def front_norm(p):
                q = p % 2
                pool.wait_ge(S("rec"), p + 1)
                if p >= 2:
                    pool.wait_ge(S("p2d"), 2 * (p - 1))
                G.tensor_tensor(heads(QH[:, q, :, :]), heads(E0[:, q, :, 0:D]),
                                RC[:, q, 0:32].rearrange("p (t h) -> p t h", t=2).unsqueeze(3)
                                .broadcast_to([128, 2, H0, HD0]), ALU.mult).then_inc(S("qh"), 1)
                pool.wait_ge(S("qh"), p + 1)
                G.tensor_tensor(heads(QN[:, q, :, :]), heads(QH[:, q, :, :]),
                                RC[:, q, 32:48].rearrange("p (t d) -> p t d", t=2).unsqueeze(2)
                                .broadcast_to([128, 2, H0, HD0]), ALU.mult).then_inc(S("qn"), 1)

            def mid_p1(p, j):
                pool.wait_ge(S("exp"), p + 1)
                if p >= 1:
                    pool.wait_ge(S("tvT_ps"), 2 * (p - 1) + j + 1)
                G.tensor_tensor(p1_out(j, K1, H0), p1_k(p % 2, j, K1, H0), p1_v(p % 2, j, K1, H0), ALU.mult)\
                    .then_inc(S("p1p"), 1)

            def mid_p2(p, j):
                pool.wait_ge(S("tv"), 2 * p + j + 1)
                if p >= 1:
                    pool.wait_ge(S("aT_ps"), 2 * (p - 1) + j + 1)
                if j == 0:
                    pool.wait_ge(S("qn"), p + 1)
                G.tensor_tensor(p2_out(j, K2, HD0), p2_q(p % 2, j, K2, HD0), p2_t(j, K2, HD0), ALU.mult)\
                    .then_inc(S("p2p"), 1)

            for i in STEPS:
                n, f, a, m, b, c = lead(i)
                if m is not None:
                    mid_p2(m, 0)
                    mid_p2(m, 1)
                if a is not None:
                    mid_p1(a, 0)
                    mid_p1(a, 1)
                if f is not None:
                    front_sub(f)
                if c is not None:
                    rstd(2, 2 * c, 2 * c + 2, "mv3", "rs3")
                if m is not None:
                    rstd(1, 2 * m, 2 * m + 2, "mv2", "rs2")
                if a is not None:
                    front_norm(a)
                if i == -1:
                    layer1_weights()
                if 1 <= i <= NE + 1:
                    e = (i - 2) % (NE + 1)
                    if i == 1:
                        pool.wait_ge(s_we, 96)
                        pool.wait_ge(S("gbb_sb"), 2)
                    G.tensor_tensor(WD1g[:, e, :, :], WD1[:, e, :, :],
                                    GBB[:, :].unsqueeze(1).broadcast_to([128, 2, D]), ALU.mult)\
                        .then_inc(S("wd1_scaled"), 1)
            for g in range(4):
                rstd(3, 4 * g, 4 * g + 4, "mv4", "rs4")

            def tokens_hot():
                for k in range(2):
                    pool.wait_ge(S("tile_hot"), k + 1)
                    G.tensor_tensor(AH[:, T * k:T * k + T, 0:SLOTS], AH[:, T * k:T * k + T, SLOTS:2 * SLOTS],
                                    token_id.unsqueeze(2).broadcast_to([128, T, SLOTS]), ALU.mult)\
                        .then_inc(S("token_hot"), 1)

            def gather(j):
                if j >= GATHERS:
                    pool.wait_ge(S("xt_ps"), j - GATHERS + 1)
                G.indirect_dma_start(GX[j % GATHERS], None, z_dram.ap(),
                                     bass.IndirectOffsetOnAxis(GI[:, j:j + 1].bitcast(U32), 0))\
                    .then_inc(S(f"gathered{j % GATHERS}"), 16)

            def scatter(j):
                if j == 0:
                    pool.wait_ge(S("idx"), 1)
                pool.wait_ge(S("ey"), j + 1)
                G.indirect_dma_start(y_dram.ap(), bass.IndirectOffsetOnAxis(DI[:, j:j + 1].bitcast(U32), 0),
                                     YX[j % SCATTERS], None).then_inc(S(f"scattered{j % SCATTERS}"), 16)

            tokens_hot()
            pool.wait_ge(S("gather_idx"), 1)
            pool.wait_ge(S("z_rows"), 64)
            for j in range(SLOTS + GATHERS - 1):
                if j < SLOTS:
                    gather(j)
                if j >= GATHERS - 1:
                    scatter(j - GATHERS + 1)


def laid_out(i):
    def c(a):
        return np.ascontiguousarray(a)
    i = {k: np.asarray(v) for k, v in i.items()}
    cf, _, ch = constants()
    n = NE
    return dict(
        x_in=c(i["L0_attn_input_seq_embs"].reshape(TOKENS, D)),
        wqkv0=c(np.concatenate([i["L0_attn_W_Q"].T, i["L0_attn_W_K"].T, i["L0_attn_W_V"].T], 1)),
        wgu0=c(np.concatenate([i["L0_ffn_w_gate"].T, i["L0_ffn_w_up"].T], 1)),
        wd0=c(i["L0_ffn_w_down"]),
        c0=c(i["L0_c"].reshape(D, 1)), wmod0=c(i["L0_wmod"]),
        wq1=c(i["L1_attn_Wq"]), wk1=c(i["L1_attn_Wk"]), wv1=c(i["L1_attn_Wv"]),
        bqc1=c(i["L1_attn_bq"].reshape(C1, 128).T), bk1=c(i["L1_attn_bk"].reshape(1, HW1)),
        bv1=c(i["L1_attn_bv"].reshape(1, HW1)), wo1=c(i["L1_attn_Wo"]),
        bo1=c(i["L1_attn_bo"].reshape(D, 1)),
        router=c(np.concatenate([i["L1_ffn_router_w"].T, i["L1_ffn_gate_w"].T], 1)),
        wgu1=c(np.concatenate([i["L1_ffn_w_gate"], i["L1_ffn_w_up"]], 2).transpose(1, 0, 2)),
        wd1=c(i["L1_ffn_w_down"].reshape(n, 2, 128, D).transpose(2, 0, 1, 3)),
        swgu1=c(np.concatenate([i["L1_ffn_sw_gate"], i["L1_ffn_sw_up"]], 1)),
        swd1=c(i["L1_ffn_sw_down"].reshape(2, 128, D).transpose(1, 0, 2)),
        c1=c(i["L1_c"].reshape(D, 1)), wmod1=c(i["L1_wmod"]),
        const_f=cf, const_h=ch,
    )


def kernel(**inputs):
    import concourse.bacc as _bacc
    from concourse.bass_utils import run_bass_kernel_spmd as _run

    arrays = laid_out(inputs)
    nc = _bacc.Bacc("TRN2", target_bir_lowering=False, num_devices=1)
    args = {name: nc.dram_tensor(name + "_dram", a.shape, mybir.dt.from_np(a.dtype), kind="ExternalInput").ap()
            for name, a in arrays.items()}
    out = nc.dram_tensor("out_dram", (TOKENS, D), F32, kind="ExternalOutput").ap()
    build(nc, out=out, **args)
    r = _run(nc, [{name + "_dram": a for name, a in arrays.items()}], core_ids=[0])
    return r.results[0]["out_dram"].reshape(1, TOKENS, D)
```

```python
import concourse.bass as bass
from concourse import mybir
from contextlib import ExitStack
import numpy as np

F32 = mybir.dt.float32
F16 = mybir.dt.float16
I32 = mybir.dt.int32
U32 = mybir.dt.uint32
ALU = mybir.AluOpType
ACT = mybir.ActivationFunctionType
AX = mybir.AxisListType

TOKENS, D = 2048, 128
T = TOKENS // 128
PAIRS = T // 2
H0, HD0 = 16, 8
HID0 = 384
C0 = HID0 // 128
HW1 = 1024
C1 = HW1 // 128
SCALE1 = 1.0 / 8.0
FE, NE = 256, 8
SLOTS = 2 * T + NE - 1
EPS = 1e-5
GATHERS = 9
SCATTERS = 4
MAGIC = 1.5 * 2.0 ** 23
WARM = 5
FILL = (20, 4)


def constants():
    p = np.arange(128)
    ident = np.eye(128, dtype=np.float32)
    fold = np.concatenate([np.eye(64), np.eye(64)], 0).astype(np.float32)
    iota128 = np.tile(p.astype(np.float32), (128, 1))
    slot = np.tile(np.arange(SLOTS, dtype=np.float32), (128, 1))
    token = (np.arange(T)[None, :] * 128 + p[:, None]).astype(np.float32)
    first = np.tile(np.arange(8, 0, -1, dtype=np.float32), (128, 1))
    before = np.tile(np.tril(np.ones((8, 8)), -1).astype(np.float32).reshape(1, 64), (128, 1))
    pad_row = (2 * TOKENS + 128 * np.arange(SLOTS)[None, :] + p[:, None]).astype(np.float32)
    ones = np.ones((128, 128), np.float32)
    parts = dict(ident=ident, fold=fold, slot=slot, token=token, first=first,
                 before=before, pad=pad_row, ones=ones)
    at, cols = {}, 0
    for name, a in parts.items():
        at[name] = (cols, cols + a.shape[1])
        cols += a.shape[1]
    tri = (p[:, None] < p[None, :]).astype(np.float16)
    half = np.concatenate([tri, np.ones((128, 128), np.float16), iota128.astype(np.float16)], 1)
    return np.concatenate(list(parts.values()), 1), at, half


def build(nc, x_in, wqkv0, wgu0, wd0, c0, wmod0, wq1, wk1, wv1, bqc1, bvc1, bk1, bv1, wo1, bo1,
          router, wgu1, wd1, swgu1, swd1, c1, wmod1, const_f, const_h, out):
    _, at, _ = constants()
    z_dram = nc.dram_tensor("z_rows", [TOKENS, D + 2], F32)
    y_dram = nc.dram_tensor("y_rows", [2 * TOKENS + 128 * SLOTS, D], F32)
    ctx = ExitStack()
    with ctx:
        def sb(name, shape, dt=F32):
            return ctx.enter_context(nc.sbuf_tensor(name, shape, dt))

        def ps(name, shape=(128, 512), dt=F32):
            return ctx.enter_context(nc.psum_tensor(name, list(shape), dt))

        def sem(name):
            return ctx.enter_context(nc.semaphore(name))

        ncf = max(b for _, b in at.values())
        CF = sb("CF", [128, ncf])
        CH = sb("CH", [128, 384], F16)

        def cf(name):
            a, b = at[name]
            return CF[:, a:b]
        ident, fold, slot_iota = cf("ident"), cf("fold"), cf("slot")
        token_id, first_w, before, pad_row, ones = cf("token"), cf("first"), cf("before"), cf("pad"), cf("ones")
        tri_h, ones_h, iota_h = CH[:, 0:128], CH[:, 128:256], CH[:, 256:384]
        minus_half = sb("minus_half", [128, T])
        X = sb("X", [128, T, D])
        WQKV0 = sb("WQKV0", [128, 3 * D])
        WGU0i = sb("WGU0i", [128, 2 * HID0], I32)
        WGU0 = sb("WGU0", [128, 2 * HID0])
        WD0i = sb("WD0i", [128, HID0], I32)
        WD0g = sb("WD0g", [128, HID0])
        WD0 = sb("WD0", [128, C0, D])
        CM = sb("CM", [128, 2])
        SC = sb("SC", [128, 2])
        WM = sb("WM", [128, 2, 6 * D])
        MOD = sb("MOD", [128, 2, 6])
        ONEC = sb("ONEC", [128, 2, 2])
        GT = sb("GT", [128, 2, 2])
        GA = sb("GA", [128, 2, 2])
        GS = sb("GS", [128, 2, 2])
        W1 = sb("W1", [128, 3, HW1])
        W1s = sb("W1s", [128, 3, HW1])
        WQT = sb("WQT", [128, C1, D + 1])
        WO1 = sb("WO1", [128, C1, D])
        BQC = sb("BQC", [128, C1])
        BVC = sb("BVC", [128, C1])
        BKV = sb("BKV", [128, 2, HW1])
        BKVs = sb("BKVs", [128, 2, HW1])
        BO = sb("BO", [128, 1])
        RT = sb("RT", [128, NE + 1])
        WGU1 = sb("WGU1", [128, NE, 2 * FE])
        WD1 = sb("WD1", [128, NE + 1, 2, D])
        WD1g = sb("WD1g", [128, NE + 1, 2, D])
        SGU = sb("SGU", [128, 2 * FE])
        DG = sb("DG", [128, 128])
        GBB = sb("GBB", [128, D])

        ST = sb("ST", [128, T, 6])
        MV = sb("MV", [128, 4, T, 2])
        VE = sb("VE", [128, 4, T])
        NM = sb("NM", [128, T])
        RS = sb("RS", [128, 4, T])
        Z = sb("Z", [128, 2, 2, D])
        HT = sb("HT", [128, 2, 256])
        QKV = sb("QKV", [128, 2, 2, 3 * D])
        MX = sb("MX", [128, 2, 48])
        S0 = sb("S0", [128, 2, 2, 2 * D])
        E0 = sb("E0", [128, 2, 2, 2 * D])
        SM = sb("SM", [128, 2, 48])
        RC = sb("RC", [128, 2, 48])
        QH = sb("QH", [128, 2, 2, D])
        QN = sb("QN", [128, 2, 2, D])
        P1 = sb("P1", [128, 2, 1024])
        P2 = sb("P2", [128, 2, 1024])
        WARMUP = P2[:, 1, 0:512]
        TVT = sb("TVT", [128, 2, 128])
        TV = sb("TV", [128, 2, 64])
        AT = sb("AT", [128, 2, 128])
        Z2 = sb("Z2", [128, 2, D])
        H2T = sb("H2T", [128, 256])
        SG = sb("SG", [128, C0 * 256])
        HID = sb("HID", [128, C0 * 256])
        Z3 = sb("Z3", [128, T, D + 2])
        Z3T = sb("Z3T", [128, TOKENS])
        GZ = sb("GZ", [128, D + 1])
        NBVC = sb("NBVC", [128, C1])
        A1 = sb("A1", [128, HW1])
        AB = sb("AB", [128, C1])
        VSK = BKV[:, 0, :]
        KV = sb("KV", [128, C1, 128])
        DO = sb("DO", [128, C1, 128])
        MT = sb("MT", [128, D + 1])
        MC = sb("MC", [128, D])
        BOG = sb("BOG", [128, 1])
        Z4 = Z3[:, :, 0:D]
        H4T = Z3T
        LG = sb("LG", [128, T, NE + 1])
        GATE = sb("GATE", [128, T])
        SS = [QKV[:, b, :, :].rearrange("p t c -> p (t c)")[:, 0:512] for b in range(2)]
        US = [QH[:, :, :, :].rearrange("p a b c -> p (a b c)"), QN[:, :, :, :].rearrange("p a b c -> p (a b c)")]
        HS = [S0[:, :, :, :].rearrange("p a b c -> p (a b c)"), E0[:, :, :, :].rearrange("p a b c -> p (a b c)")]
        PR = sb("PR", [128, T, NE])
        PX = sb("PX", [128, T, NE])
        L2 = SG[:, 0:T * NE].rearrange("p (t e) -> p t e", e=NE)
        TOP = sb("TOP", [128, 2, T])
        RM = sb("RM", [128, T])
        RSUM = sb("RSUM", [128, T])
        WK = [Z3[:, :, D], Z3[:, :, D + 1]]
        WROW = sb("WROW", [128, 2, 2])
        OH = sb("OH", [128, 2, T, NE])
        SCR = SG[:, T * NE:2 * T * NE].rearrange("p (t e) -> p t e", e=NE)
        MH = sb("MH", [128, T + 1, NE], F16)
        OHR = SG[:, 2 * T * NE:4 * T * NE].rearrange("p (k t e) -> p k t e", k=2, e=NE)
        OHS = SG[:, 4 * T * NE:6 * T * NE].rearrange("p (k t e) -> p k t e", k=2, e=NE)
        NTF = sb("NTF", [128, NE])
        STT = HID[:, 512:512 + NE * NE].rearrange("p (e f) -> p e f", e=NE)
        START = sb("START", [128, NE])
        ENDT = sb("ENDT", [128, NE])
        RANK = sb("RANK", [128, 2 * T])
        RTILE = sb("RTILE", [128, 2 * T])
        FIRST = sb("FIRST", [128, 2 * T])
        ROW = sb("ROW", [128, 2 * T], F16)
        TILE = sb("TILE", [128, 2 * T], F16)
        BH = P1[:, :, :].rearrange("p a b -> p (a b)").bitcast(F16).rearrange("p (k r) -> p k r", r=128)
        AH = P2[:, :, :].rearrange("p a b -> p (a b)").bitcast(F16)[:, 0:2 * T * 2 * SLOTS]\
            .rearrange("p (k c) -> p k c", c=2 * SLOTS)
        IDX = sb("IDX", [128, 2, 2, SLOTS])
        KROW = [IDX[:, k, 1, :] for k in range(2)]
        GI = sb("GI", [128, SLOTS], I32)
        PADF = sb("PADF", [128, SLOTS])
        DF = sb("DF", [128, SLOTS])
        ANY = sb("ANY", [128, SLOTS])
        DI = sb("DI", [128, SLOTS], I32)
        GEQ = HID[0:1, 0:SLOTS * NE].rearrange("p (s e) -> p s e", e=NE)
        EXF = sb("EXF", [1, SLOTS])
        EXI = sb("EXI", [1, SLOTS], I32)
        W1f = W1[:, :, :].rearrange("p a b -> p (a b)")
        WMf = WM[:, :, :].rearrange("p l m -> p (l m)")
        GX = [WMf[:, (D + 2) * b:(D + 2) * (b + 1)] for b in range(GATHERS)]
        YX = [W1f[:, 768 + 128 * b:896 + 128 * b] for b in range(SCATTERS)]
        XT = [W1f[:, c:c + 128] for c in (1536, 1664, 2816)]
        SX = [W1f[:, 1792 + 256 * b:2048 + 256 * b] for b in range(2)]
        HX = [W1f[:, 2304 + 256 * b:2560 + 256 * b] for b in range(2)]
        HXT = [A1[:, 256 * b:256 * b + 256] for b in range(2)]
        YB = [a.rearrange("p (k t d) -> p k t d", k=2, t=4) for a in
              (W1s[:, 0, :], W1s[:, 1, :], W1s[:, 2, :], WO1[:, :, :].rearrange("p c d -> p (c d)"))]

        B = [ps(f"bank{i}") for i in range(8)]

        s_cf, s_w0, s_wi, s_c, s_w1, s_we = (sem(n) for n in
            ("const_in", "w0_in", "w0int_in", "c_in", "w1_in", "we_in"))
        s = {}

        def S(name):
            if name not in s:
                s[name] = sem(name)
            return s[name]

        parts = [("gu", 5), ("down", 1), ("gu", 6), ("gu", 7), ("down", 2), ("down", 3)]
        SHARED_AT = {4 * n + 2: part for n, part in enumerate(parts)}
        blk = ctx.enter_context(nc.Block())

        xv = x_in.rearrange("(t p) d -> p t d", p=128)
        outv = out.rearrange("(t p) d -> p t d", p=128)

        NORMA, NORMD = (4, 4, 0, 2), (0, 0, 4, 2)
        Z4A = [sum(NORMA[:g + 1]) for g in range(4)]
        Z4D = [sum(NORMD[:g + 1]) for g in range(4)]

        @blk.sync
        def _(sp):
            sp.dma_start(X[:, 0:4, :], xv[:, 0:4, :]).then_inc(S("x_in0"), 16)
            sp.dma_start(CF[:, :], const_f).then_inc(s_cf, 16)
            sp.dma_start(WQKV0[:, :], wqkv0).then_inc(s_w0, 16)
            for g in range(1, 4):
                sp.dma_start(X[:, 4 * g:4 * g + 4, :], xv[:, 4 * g:4 * g + 4, :]).then_inc(S(f"x_in{g}"), 16)
            sp.dma_start(WGU0i[:, :], wgu0).then_inc(s_wi, 16)
            for w, src in enumerate((wq1, wk1, wv1)):
                sp.dma_start(W1[:, w, :], src).then_inc(s_w1, 16)
            sp.dma_start(WO1[:, :, :], wo1.rearrange("(c p) d -> p c d", p=128)).then_inc(s_w1, 16)
            sp.dma_start(BQC[:, :], bqc1).then_inc(s_w1, 16)
            sp.dma_start(BVC[:, :], bvc1).then_inc(s_w1, 16)
            sp.dma_start(BKV[:, 0, :], bk1.broadcast_to([128, HW1])).then_inc(s_w1, 16)
            sp.dma_start(BKV[:, 1, :], bv1.broadcast_to([128, HW1])).then_inc(s_w1, 16)
            sp.dma_start(BO[:, :], bo1).then_inc(s_w1, 16)
            sp.dma_start(CH[:, :], const_h).then_inc(s_we, 16)
            sp.dma_start(RT[:, :], router).then_inc(s_we, 16)
            sp.dma_start(SGU[:, :], swgu1).then_inc(s_we, 16)
            sp.dma_start(WGU1[:, :, :], wgu1).then_inc(s_we, 16)
            sp.dma_start(WD1[:, 0:NE, :, :], wd1).then_inc(s_we, 16)
            sp.dma_start(WD1[:, NE, :, :], swd1).then_inc(s_we, 16)
            zv = z_dram.ap().rearrange("(t p) d -> p t d", p=128)
            sp.wait_ge(S("z4a"), Z4A[3])
            sp.wait_ge(S("z4d"), Z4D[3])
            sp.wait_ge(S("weights"), 2)
            for g in range(4):
                sp.dma_start(zv[:, 4 * g:4 * g + 4, :], Z3[:, 4 * g:4 * g + 4, :]).then_inc(S("z_rows"), 16)
            for b in range(SCATTERS):
                sp.wait_ge(S(f"scattered{b}"), 16 * len(range(b, SLOTS, SCATTERS)))
            yv = y_dram.ap()[0:2 * TOKENS, :].rearrange("(k t p) d -> p k t d", p=128, k=2)
            for g in (3, 0, 1, 2):
                for k in range(2):
                    sp.dma_start(YB[g][:, k, :, :], yv[:, k, 4 * g:4 * g + 4, :]).then_inc(S(f"y_in{g}"), 16)
            for g in (0, 1, 3, 2):
                if g < 3:
                    sp.wait_ge(S("x5"), 2 * g + 2)
                else:
                    sp.wait_ge(S("x5p"), 2)
                sp.dma_start(outv[:, 4 * g:4 * g + 4, :], X[:, 4 * g:4 * g + 4, :]).then_inc(S("out"), 16)
            sp.wait_ge(S("out"), 64)

        def lead(i):
            return [i + k if 0 <= i + k < PAIRS else None for k in (3, 2, 1, 0, -1, -2)]

        STEPS = range(-3, PAIRS + 2)

        def yb(p):
            return 3 if p == PAIRS - 1 else 2

        OUT = (1, 5, 6, 0)
        UB = (5, 3, 7, 5) + (7,) * 4
        LB = (4, 7)

        def heads(ap):
            return ap.rearrange("p t (h d) -> p t h d", d=HD0)

        def p1_out(j, a, b):
            return P1[:, j, 64 * a:64 * b].rearrange("p (h d e) -> p h d e", d=HD0, e=HD0)

        def p1_k(q, j, a, b):
            e = E0[:, q, j, D + HD0 * a:D + HD0 * b].rearrange("p (h d) -> p h d", d=HD0)
            return e.unsqueeze(3).broadcast_to([128, b - a, HD0, HD0])

        def p1_v(q, j, a, b):
            v = QKV[:, q, j, 2 * D + HD0 * a:2 * D + HD0 * b].rearrange("p (h e) -> p h e", e=HD0)
            return v.unsqueeze(2).broadcast_to([128, b - a, HD0, HD0])

        def p2_out(j, a, b):
            return P2[:, j, 128 * a:128 * b].rearrange("p (d h e) -> p d h e", h=H0, e=HD0)

        def p2_q(q, j, a, b):
            v = QN[:, q, j, :].rearrange("p (h d) -> p d h", d=HD0)[:, a:b, :]
            return v.unsqueeze(3).broadcast_to([128, b - a, H0, HD0])

        def p2_t(j, a, b):
            v = TV[:, j, :].rearrange("p (d e) -> p d e", e=HD0)[:, a:b, :]
            return v.unsqueeze(2).broadcast_to([128, b - a, H0, HD0])

        K1, K2 = 11, 5

        @blk.scalar
        def _(act):
            act.dma_start(CM[:, 0:1], c0).then_inc(s_c, 16)
            act.dma_start(CM[:, 1:2], c1).then_inc(s_c, 16)
            act.dma_start(WM[:, 0, :], wmod0).then_inc(S("wmod_in0"), 16)
            act.dma_start(WM[:, 1, :], wmod1).then_inc(S("wmod_in1"), 16)
            act.dma_start(WD0i[:, :], wd0).then_inc(S("wd0_in"), 16)
            act.wait_ge(s_c, 32)
            nc.scalar.activation(SC[:, :], CM[:, :], ACT.Silu).then_inc(S("silu_c"), 1)
            act.wait_ge(S("mod_ps"), 1)
            nc.scalar.activation(MOD[:, :, :], B[5][:, 0:12].rearrange("p (l m) -> p l m", l=2), ACT.Copy)\
                .then_inc(S("mod_sb"), 1)

            def front_hT(p):
                act.wait_ge(S("zT_ps"), p + 1)
                if p == 0:
                    act.wait_ge(S("one_c"), 1)
                    act.wait_ge(S("mod_sb"), 1)
                nc.scalar.activation(HT[:, p % 2, :], B[0][:, 0:256], ACT.Identity, bias=MOD[:, 0, 0:1],
                                     scale=ONEC[:, 0, 0:1]).then_inc(S("hT"), 1)

            def front_qkv(p):
                act.wait_ge(S("qkv_ps"), p + 1)
                if p >= 2:
                    act.wait_ge(S("p1d"), 2 * (p - 1))
                    act.wait_ge(S("p1p"), 2 * (p - 1))
                for j in range(2):
                    nc.scalar.activation(QKV[:, p % 2, j, :], B[j][:, 0:3 * D], ACT.Copy).then_inc(S("qkv_sb"), 1)

            def front_exp(p):
                act.wait_ge(S("sub"), 2 * (p + 1))
                nc.scalar.activation(E0[:, p % 2, :, :], S0[:, p % 2, :, :], ACT.Exp).then_inc(S("exp"), 1)

            def mid_tvT(p, j):
                act.wait_ge(S("tvT_ps"), 2 * p + j + 1)
                nc.scalar.activation(TVT[:, j, :], B[3 + j][:, 0:128], ACT.Copy).then_inc(S("tvT"), 1)

            def mid_tv(p, j):
                act.wait_ge(S("tv_ps"), 2 * p + j + 1)
                if p >= 1:
                    act.wait_ge(S("p2p"), 2 * p - 1 + j)
                    act.wait_ge(S("p2d"), 2 * p - 1 + j)
                nc.scalar.activation(TV[:, j, :], B[3 + j][:, 128:192], ACT.Copy)\
                    .then_inc(S("tv"), 1)

            def mid_aT(p, j):
                act.wait_ge(S("aT_ps"), 2 * p + j + 1)
                if p == 0 and j == 0:
                    act.wait_ge(S("gate_ok"), 1)
                nc.scalar.activation(AT[:, j, :], B[3 + j][:, 192:320], ACT.Identity,
                                     scale=GT[:, 0, 0:1]).then_inc(S("aT"), 1)

            def back_h2T(p):
                act.wait_ge(S("z2T_ps"), p + 1)
                nc.scalar.activation(H2T[:, :], B[1][:, 0:256], ACT.Identity, bias=MOD[:, 0, 3:4],
                                     scale=ONEC[:, 0, 1:2]).then_inc(S("h2T"), 1)

            def back_silu(p):
                act.wait_ge(S("gu_ps"), 3 * p + 1)
                if p >= 1:
                    act.wait_ge(S("hid"), 2 * p)
                nc.scalar.activation(SG[:, 0:512], B[5][:, :], ACT.Silu, scale=1.0 / 127.0).then_inc(S("silu"), 1)
                act.wait_ge(S("gu_ps"), 3 * p + 2)
                nc.scalar.activation(SG[:, 512:768], B[6][:, 0:256], ACT.Silu, scale=1.0 / 127.0)\
                    .then_inc(S("silu"), 1)

            def w1_scale(w):
                nc.scalar.activation(W1s[:, w, :], W1[:, w, :], ACT.Copy, scale=ONEC[:, 1, 0:1])\
                    .then_inc(S("w1_scaled"), 1)

            for i in STEPS:
                n, f, a, m, b, _ = lead(i)
                if f is not None:
                    front_qkv(f)
                if m is not None:
                    mid_aT(m, 0)
                    mid_aT(m, 1)
                if f is not None:
                    front_exp(f)
                if i == 0:
                    act.wait_ge(S("wd0_ps"), 1)
                    nc.scalar.activation(WD0[:, :, :], B[7][:, 0:384].rearrange("p (c d) -> p c d", c=C0),
                                         ACT.Copy, scale=1.0 / (127.0 * 127.0)).then_inc(S("wd0_ok"), 1)
                    for w in (1, 2):
                        w1_scale(w)
                if b is not None:
                    back_silu(b)
                if a is not None:
                    mid_tvT(a, 0)
                    mid_tvT(a, 1)
                    mid_tv(a, 0)
                    mid_tv(a, 1)
                if m is not None:
                    back_h2T(m)
                if n is not None:
                    front_hT(n)
                if i == -1:
                    act.wait_ge(S("gate_ok"), 1)
                    act.wait_ge(S("wd0_in"), 16)
                    nc.scalar.activation(WD0g[:, :], WD0i[:, :], ACT.Identity, scale=GT[:, 0, 1:2])\
                        .then_inc(S("wd0_scaled"), 1)
                    act.wait_ge(s_w1, 144)
                    w1_scale(0)
                if i == 0:
                    act.wait_ge(S("prep_ps"), 1)
                    for h in range(2):
                        nc.scalar.activation(WQT[:, 4 * h:4 * h + 4, 0:128],
                                             B[5 + h][:, :].rearrange("p (c d) -> p c d", c=4), ACT.Copy)\
                            .then_inc(S("prep_sb"), 1)

            for g in range(4):
                act.wait_ge(S("z3T_ps"), g + 1)
                nc.scalar.activation(Z3T[:, 512 * g:512 * g + 512], B[6 + g % 2][:, :], ACT.Copy)\
                    .then_inc(S("z3T"), 1)
            act.wait_ge(S("do_ps"), 1)
            nc.scalar.activation(DO[:, 0:4, :], B[0][:, :].rearrange("p (c d) -> p c d", c=4), ACT.Copy)\
                .then_inc(S("do_sb_a"), 1)
            act.wait_ge(S("mc_ps"), 1)
            nc.scalar.activation(MC[:, :], B[4][:, 0:128], ACT.Copy).then_inc(S("mc"), 1)
            for g in range(5):
                if g < 4 and NORMA[g]:
                    act.wait_ge(S("nm4"), 2 * g + 2)
                    for t in range(4 * g, 4 * g + NORMA[g]):
                        nc.scalar.activation(Z4[:, t, :], X[:, t, :], ACT.Identity, bias=NM[:, t:t + 1],
                                             scale=RS[:, 3, t:t + 1]).then_inc(S("z4a"), 1)
                if g in (1, 2, 4):
                    act.wait_ge(S("h4T_ps"), g)
                    nc.scalar.activation(H4T[:, 512 * g - 512:512 * g], B[2 + (g - 1) % 2][:, :], ACT.Identity,
                                         bias=MOD[:, 1, 3:4], scale=ONEC[:, 1, 1:2]).then_inc(S("h4T"), 1)

            def shared_silu(n):
                act.wait_ge(S("sgu_ps"), n + 1)
                if n >= 2:
                    act.wait_ge(S("shid"), n - 1)
                nc.scalar.activation(SS[n % 2], B[6][:, :], ACT.Silu).then_inc(S("ssilu"), 1)
                if n < 2:
                    nc.scalar.activation(US[n % 2], B[UB[n]][:, :], ACT.Copy).then_inc(S("u_sb"), 1)

            shared_silu(0)
            act.wait_ge(S("rt_sub"), 2)
            nc.scalar.activation(PX[:, :, :], PR[:, :, :], ACT.Exp).then_inc(S("rt_exp"), 1)
            nc.scalar.activation(WK[1], WK[1], ACT.Exp).then_inc(S("rt_exp"), 1)
            nc.scalar.activation(GATE[:, :], LG[:, :, NE], ACT.Exp, scale=-1.0).then_inc(S("rt_exp"), 1)
            shared_silu(1)
            shared_silu(2)
            act.wait_ge(S("row"), 1)
            last_hot = slice(2 * T - 8, 2 * T)
            for n in range(2 * T - 8, 2 * T):
                nc.scalar.activation(BH[:, n, :], iota_h, ACT.Square, bias=ROW[:, n:n + 1], scale=-1.0)\
                    .then_inc(S("row_hot_act"), 1)
            act.wait_ge(S("row_hot_act"), 8)
            nc.scalar.activation(BH[:, last_hot, :], BH[:, last_hot, :], ACT.Relu, bias=1.0, scale=-1.0)\
                .then_inc(S("row_hot_act"), 1)
            for n in range(3, 5):
                shared_silu(n)

            def expert_x(j):
                act.wait_ge(S("xt_ps"), j + 1)
                if j >= 3:
                    act.wait_ge(S("egu_ps"), j - 2)
                nc.scalar.activation(XT[j % 3], B[0][:, 0:128], ACT.Identity, bias=MOD[:, 1, 3:4],
                                     scale=ONEC[:, 1, 1:2]).then_inc(S("xt"), 1)

            def expert_silu(j):
                act.wait_ge(S("egu_ps"), j + 1)
                if j >= 2:
                    act.wait_ge(S("ehid"), j - 1)
                nc.scalar.activation(SX[j % 2], B[2 + j % 2][:, 0:FE], ACT.Silu).then_inc(S("esilu"), 1)

            for j in range(-3, SLOTS):
                if 0 <= j + 1 < SLOTS:
                    expert_silu(j + 1)
                if j + 3 < SLOTS:
                    expert_x(j + 3)
                if j in SHARED_AT and SHARED_AT[j][0] == "gu":
                    shared_silu(SHARED_AT[j][1])

        @blk.tensor
        def _(pe):
            mm = nc.tensor.matmul

            def front(p):
                for j in range(2):
                    pe.wait_ge(S("z"), 2 * p + j + 1)
                    if p >= 1 and j == 0:
                        pe.wait_ge(S("qkv_sb"), 2 * p)
                    last = mm(B[0][:, 128 * j:128 * j + 128], Z[:, p % 2, j, :], ident, start=True, stop=True,
                              is_transpose=True)
                last.then_inc(S("zT_ps"), 1)

            pe.wait_ge(S("constants_set"), 1)
            for n in range(WARM):
                mm(B[7][:, :], WARMUP[:, 0:128], WARMUP[:, :], start=True, stop=True)
            pe.wait_ge(s_cf, 16)
            front(0)
            pe.wait_ge(S("silu_c"), 1)
            for l in range(2):
                pe.wait_ge(S(f"wmod_in{l}"), 16)
                for m in range(6):
                    last = mm(B[5][:, 6 * l + m:6 * l + m + 1], WM[:, l, D * m:D * m + D], SC[:, l:l + 1],
                              start=True, stop=True)
            last.then_inc(S("mod_ps"), 1)

            def front_qkv(p):
                pe.wait_ge(S("hT"), p + 1)
                if p == 0:
                    pe.wait_ge(s_w0, 16)
                else:
                    pe.wait_ge(S("qkv_sb"), 2 * p)
                if p >= 3:
                    pe.wait_ge(S("h2T"), p - 2)
                for j in range(2):
                    last = mm(B[j][:, 0:3 * D], HT[:, p % 2, 128 * j:128 * j + 128], WQKV0[:, :],
                              start=True, stop=True)
                last.then_inc(S("qkv_ps"), 1)

            def mid_sum_heads(p, j):
                pe.wait_ge(S("p1d"), 2 * p + j + 1)
                pe.wait_ge(S("p1p"), 2 * p + j + 1)
                if p >= 1:
                    pe.wait_ge(S("x1"), 2 * (p - 1) + j + 1)
                for n in range(8):
                    last = mm(B[3 + j][:, 0:128], P1[:, j, 128 * n:128 * n + 128], ident,
                              start=(n == 0), stop=(n == 7), is_transpose=True)
                last.then_inc(S("tvT_ps"), 1)

            def mid_fold(p, j):
                pe.wait_ge(S("tvT"), 2 * p + j + 1)
                mm(B[3 + j][:, 128:192], TVT[:, j, :], fold, start=True, stop=True)\
                    .then_inc(S("tv_ps"), 1)

            def mid_sum_d(p, j):
                pe.wait_ge(S("p2d"), 2 * p + j + 1)
                pe.wait_ge(S("p2p"), 2 * p + j + 1)
                for n in range(8):
                    last = mm(B[3 + j][:, 192:320], P2[:, j, 128 * n:128 * n + 128], ident,
                              start=(n == 0), stop=(n == 7), is_transpose=True)
                last.then_inc(S("aT_ps"), 1)

            def mid_back(p, j):
                pe.wait_ge(S("aT"), 2 * p + j + 1)
                mm(B[3 + j][:, 320:448], AT[:, j, :], ident, start=True, stop=True,
                   is_transpose=True).then_inc(S("aB_ps"), 1)

            def back_T(p):
                for j in range(2):
                    pe.wait_ge(S("z2"), 2 * p + j + 1)
                    if j == 0:
                        pe.wait_ge(S("qkv_sb"), min(2 * (p + 3), T))
                    last = mm(B[1][:, 128 * j:128 * j + 128], Z2[:, j, :], ident, start=True, stop=True,
                              is_transpose=True)
                last.then_inc(S("z2T_ps"), 1)

            def back_gu(p, part):
                if part == 0:
                    pe.wait_ge(S("h2T"), p + 1)
                    if p == 0:
                        pe.wait_ge(S("w0_cast"), 1)
                    else:
                        pe.wait_ge(S("silu"), 2 * p)
                        pe.wait_ge(S("hid"), 2 * p)
                for n in (2 * part, 2 * part + 1):
                    w = (0, 1, 2, 5, 3, 4)[n]
                    last = mm(B[5 + n // 2][:, 256 * (n % 2):256 * (n % 2) + 256],
                              WGU0[:, 128 * w:128 * w + 128], H2T[:, :], start=True, stop=True)
                    if n % 2:
                        last.then_inc(S("gu_ps"), 1)

            def back_down(p):
                pe.wait_ge(S("hid"), 2 * (p + 1))
                if p == 0:
                    pe.wait_ge(S("wd0_ok"), 1)
                elif p < PAIRS - 1:
                    pe.wait_ge(S("x2"), p)
                for j in range(2):
                    for n in range(C0):
                        last = mm(B[yb(p)][:, 256 + 128 * j:384 + 128 * j],
                                  HID[:, 256 * n + 128 * j:256 * n + 128 * j + 128], WD0[:, n, :],
                                  start=(n == 0), stop=(n == C0 - 1))
                last.then_inc(S("y_ps"), 1)

            def sum_tokens(a, b):
                if a == 0:
                    pe.wait_ge(S("brow_sb"), 4)
                    pe.wait_ge(S("constants_set"), 3)
                pe.wait_ge(S("z3"), b)
                for t in range(a, b):
                    last = mm(B[0][:, 0:D + 1], Z3[:, t, 0:D], Z3[:, t, 0:D + 1], start=(t == 0), stop=(t == T - 1))
                if b == T:
                    last.then_inc(S("g_all"), 1)

            def bias_row(n):
                if n == 0:
                    pe.wait_ge(S("qkv_sb"), T)
                else:
                    pe.wait_ge(S("brow_sb"), n)
                mm(B[0][:, :], MOD[:, 1, 0:1].broadcast_to([128, 128]),
                   W1[:, 1 + n // 2, 512 * (n % 2):512 * (n % 2) + 512], start=True, stop=True)\
                    .then_inc(S("brow_ps"), 1)

            def z3T(g):
                if g >= 2:
                    pe.wait_ge(S("z3T"), g - 1)
                else:
                    pe.wait_ge(S("hid"), T)
                for t in range(4 * g, 4 * g + 4):
                    last = mm(B[6 + g % 2][:, 128 * (t % 4):128 * (t % 4) + 128], Z3[:, t, 0:D], ident,
                              start=True, stop=True, is_transpose=True)
                last.then_inc(S("z3T_ps"), 1)

            def stay_warm(n, bank):
                for _ in range(n):
                    mm(B[bank][:, 0:128], ones_h, iota_h, start=True, stop=True)

            for i in STEPS:
                n, f, a, m, b, _ = lead(i)
                if f is not None:
                    front_qkv(f)
                if m is not None:
                    mid_sum_d(m, 0)
                    mid_sum_d(m, 1)
                if i == 0:
                    pe.wait_ge(S("wd0_scaled"), 1)
                    for c in range(C0):
                        last = mm(B[7][:, 128 * c:128 * c + 128], WD0g[:, 128 * c:128 * c + 128], ident,
                                  start=True, stop=True, is_transpose=True)
                    last.then_inc(S("wd0_ps"), 1)
                if PAIRS - 2 <= i < PAIRS:
                    bias_row(2 * (i - PAIRS + 2))
                if i == 1:
                    pe.wait_ge(S("prep_sb"), 2)
                if b is not None:
                    back_gu(b, 0)
                if m is not None:
                    mid_back(m, 0)
                if b is not None:
                    back_gu(b, 1)
                if m is not None:
                    mid_back(m, 1)
                if i == 0:
                    pe.wait_ge(S("w1_scaled"), 1)
                    for c in range(C1):
                        last = mm(B[5 + c // 4][:, 128 * (c % 4):128 * (c % 4) + 128],
                                  W1s[:, 0, 128 * c:128 * c + 128], ident, start=True, stop=True, is_transpose=True)
                    last.then_inc(S("prep_ps"), 1)
                if i == 1:
                    pe.wait_ge(S("gbb_sb"), 3)
                if b is not None:
                    back_gu(b, 2)
                if a is not None:
                    mid_sum_heads(a, 0)
                    mid_sum_heads(a, 1)
                    mid_fold(a, 0)
                    mid_fold(a, 1)
                if m is not None:
                    back_T(m)
                if i == PAIRS - 2:
                    bias_row(1)
                if n is not None and n > 0:
                    front(n)
                if i == PAIRS:
                    bias_row(3)
                if b is not None:
                    back_down(b)
                if i == PAIRS:
                    sum_tokens(0, 2 * (PAIRS - 2))
                if i == 0:
                    pe.wait_ge(S("wd0_ok"), 1)
                    pe.wait_ge(S("diag_gb"), 1)
                    for c in range(C1):
                        mm(B[7][:, c:c + 1], W1[:, 0, 128 * c:128 * c + 128], MOD[:, 1, 0:1], start=True, stop=True)
                    for c in range(C1):
                        mm(B[7][:, C1 + c:C1 + c + 1], W1[:, 2, 128 * c:128 * c + 128], MOD[:, 1, 0:1],
                           start=True, stop=True)
                    mm(B[7][:, 128:256], ones, DG[:, :], start=True, stop=True).then_inc(S("prep_ps"), 1)

            z3T(0)
            sum_tokens(2 * (PAIRS - 2), T)
            z3T(1)
            z3T(2)

            pe.wait_ge(S("gz"), 1)
            pe.wait_ge(S("x2"), PAIRS)
            for c in range(C1):
                last = mm(B[2][:, c:c + 1], W1s[:, 2, 128 * c:128 * c + 128], GZ[:, D:D + 1], start=True, stop=True)
            last.then_inc(S("ab_ps"), 1)
            pe.wait_ge(S("h2T"), PAIRS)
            for n in range(2):
                mm(B[n][:, :], GZ[:, 0:D], W1s[:, 2, 512 * n:512 * n + 512], start=True, stop=True)\
                    .then_inc(S("a_ps"), 1)
            z3T(3)
            pe.wait_ge(S("silu"), T)
            for c in range(C1):
                if c % 4 == 0:
                    pe.wait_ge(S("a_sb"), c // 4 + 1)
                if c == 4:
                    pe.wait_ge(S("ab"), 1)
                cols = slice(128 * c, 128 * c + 128)
                last = mm(B[(5, 2)[c // 4]][:, 128 * (c % 4):128 * (c % 4) + 128], A1[:, cols], W1s[:, 1, cols],
                          start=True, stop=True)
                if c % 4 == 3:
                    last.then_inc(S("kv_ps"), 1)
            for c in range(C1):
                if c == 0:
                    pe.wait_ge(S("kv_sb"), 2)
                if c == 4:
                    pe.wait_ge(S("kv_sb"), 4)
                last = mm(B[c // 4][:, 128 * (c % 4):128 * (c % 4) + 128], KV[:, c, :], WO1[:, c, :],
                          start=True, stop=True)
                if c % 4 == 3:
                    last.then_inc(S("do_ps"), 1)
            for c in range(C1):
                if c == 0:
                    pe.wait_ge(S("do_sb_a"), 1)
                if c == 4:
                    pe.wait_ge(S("do_sb_d"), 1)
                last = mm(B[3][:, 0:D + 1], DO[:, c, :], WQT[:, c, :], start=(c == 0), stop=(c == C1 - 1))
            last.then_inc(S("mt_ps"), 1)
            pe.wait_ge(S("mt_step"), 2)
            mm(B[4][:, 0:128], MT[:, 0:128], ident, start=True, stop=True, is_transpose=True)\
                .then_inc(S("mc_ps"), 1)

            def attend(g):
                if g == 0:
                    pe.wait_ge(S("mt_step"), 3)
                for t in range(4):
                    mm(B[OUT[g]][:, 128 * t:128 * t + 128], ones, DG[:, :], start=True, stop=False)
                    if g == 0 and t == 0:
                        pe.wait_ge(S("mc"), 1)
                        pe.wait_ge(S("z3T"), 4)
                    last = mm(B[OUT[g]][:, 128 * t:128 * t + 128], Z3T[:, 512 * g + 128 * t:512 * g + 128 * t + 128],
                              MC[:, :], start=False, stop=True)
                last.then_inc(S("o_ps"), 1)

            def h4T(g):
                if g >= 2:
                    pe.wait_ge(S("h4T"), g - 1)
                pe.wait_ge(S("z4a"), Z4A[g])
                if Z4D[g]:
                    pe.wait_ge(S("z4d"), Z4D[g])
                for t in range(4 * g, 4 * g + 4):
                    last = mm(B[2 + g % 2][:, 128 * (t % 4):128 * (t % 4) + 128], Z4[:, t, :], ident,
                              start=True, stop=True, is_transpose=True)
                last.then_inc(S("h4T_ps"), 1)

            def logits(g):
                if g == 2:
                    pe.wait_ge(S("h4T_d"), 1)
                else:
                    pe.wait_ge(S("h4T"), min(g + 1, 3))
                for t in range(4 * g, 4 * g + 4):
                    last = mm(B[LB[g // 2]][:, 9 * t:9 * t + 9], H4T[:, 128 * t:128 * t + 128], RT[:, :],
                              start=True, stop=True)
                last.then_inc(S("lg_ps"), 1)

            def shared_gu(n, halves=(0, 1)):
                g, f = n // 2, n % 2
                cols = slice(512 * g, 512 * g + 512)
                if 0 in halves:
                    if n == 0:
                        pe.wait_ge(S("x3"), 3)
                    else:
                        pe.wait_ge(S("ssilu"), n)
                    mm(B[6][:, :], SGU[:, 128 * f:128 * f + 128], H4T[:, cols], start=True, stop=True)
                if 1 in halves:
                    if n == 2:
                        pe.wait_ge(S("picked"), 2)
                    if n == 3:
                        pe.wait_ge(S("u_sb"), 1)
                    if n >= 4:
                        pe.wait_ge(S("shid"), n)
                    mm(B[UB[n]][:, :], SGU[:, FE + 128 * f:FE + 128 * f + 128], H4T[:, cols],
                       start=True, stop=True).then_inc(S("sgu_ps"), 1)

            def shared_down(g):
                pe.wait_ge(S("shid"), 2 * g + 2)
                if g >= 1:
                    pe.wait_ge(S("x4"), 4 * g)
                for t in range(4):
                    for f in range(2):
                        last = mm(B[1][:, 128 * t:128 * t + 128],
                                  HS[g % 2][:, 512 * f + 128 * t:512 * f + 128 * t + 128], WD1g[:, NE, f, :],
                                  start=(f == 0), stop=(f == 1))
                last.then_inc(S("sy_ps"), 1)

            pe.wait_ge(s_we, 96)
            pe.wait_ge(S("wd1_scaled"), NE + 1)
            for g in range(4):
                attend(g)
            for g in range(5):
                if g < 4:
                    h4T(g)
                if g >= 1:
                    logits(g - 1)
                if g < len(FILL):
                    stay_warm(FILL[g], 1)

            def ranks():
                pe.wait_ge(S("picked"), 2)
                M = MH[:, :, :].rearrange("p t e -> p (t e)")
                for n in range(T + 1):
                    if n == 0:
                        mm(B[2][:, 0:8 * T + 8], tri_h, M, start=True, stop=False)
                    else:
                        last = mm(B[2][:, 8 * n:8 * T + 8], ones_h, M[:, 0:8 * (T + 1 - n)],
                                  start=False, stop=(n == T))
                last.then_inc(S("rank_ps"), 1)

            def places():
                pe.wait_ge(S("token_hot"), 1)
                for n in range(2 * T):
                    k = n // T
                    if n == T:
                        pe.wait_ge(S("token_hot"), 2)
                    if n == 2 * T - 8:
                        pe.wait_ge(S("row_hot_act"), 9)
                    elif n % 8 == 0:
                        pe.wait_ge(S("row_hot"), n // 8 + 1)
                    last = mm(B[4][:, 2 * SLOTS * k:2 * SLOTS * k + 2 * SLOTS], BH[:, n, :], AH[:, n, :],
                              start=(n % T == 0), stop=(n % T == T - 1))
                last.then_inc(S("idx_ps"), 1)

            shared_gu(0)
            shared_gu(1, (0,))
            ranks()
            shared_gu(1, (1,))
            shared_gu(2)
            shared_gu(3)
            places()
            shared_down(0)
            shared_gu(4)

            def expert_x(j):
                pe.wait_ge(S(f"gathered{j % GATHERS}"), 16 * (j // GATHERS + 1))
                if j >= 1:
                    pe.wait_ge(S("xt"), j)
                mm(B[0][:, 0:128], GX[j % GATHERS][:, 0:D], ident, start=True, stop=True, is_transpose=True)\
                    .then_inc(S("xt_ps"), 1)

            def expert_gu(j, e):
                pe.wait_ge(S("xt"), j + 1)
                if j >= 2:
                    pe.wait_ge(S("ehid"), j - 1)
                w = WGU1[:, :, :].rearrange("p e f -> p (e f)")
                mm(B[2 + j % 2][:, :], XT[j % 3], w[:, bass.ds(e * (2 * FE), 2 * FE)], start=True, stop=True)\
                    .then_inc(S("egu_ps"), 1)

            def expert_hT(j):
                pe.wait_ge(S("ehid"), j + 1)
                if j >= 1:
                    pe.wait_ge(S("ht"), j)
                for f in range(2):
                    last = mm(B[4][:, 128 * f:128 * f + 128], HX[j % 2][:, 128 * f:128 * f + 128], ident,
                              start=True, stop=True, is_transpose=True)
                last.then_inc(S("ht_ps"), 1)

            def expert_down(j, e):
                pe.wait_ge(S("ht"), j + 1)
                if j >= 1:
                    pe.wait_ge(S("ey"), j)
                w = WD1g[:, :, :, :].rearrange("p e f d -> p (e f d)")
                for f in range(2):
                    last = mm(B[5][:, 0:128], HXT[j % 2][:, 128 * f:128 * f + 128],
                              w[:, bass.ds(e * (2 * D) + f * D, D)], start=(f == 0), stop=(f == 1))
                last.then_inc(S("ey_ps"), 1)

            pe.wait_ge(S("idx"), 1)
            held = {}
            for j in range(-3, SLOTS + 1):
                if 0 <= j + 1 < SLOTS:
                    expert_gu(j + 1, held[j + 1])
                if j + 3 < SLOTS:
                    held[j + 3] = pe.value_load(EXI[0:1, j + 3:j + 4], min_val=0, max_val=NE - 1)
                    expert_x(j + 3)
                if 0 <= j - 1:
                    expert_down(j - 1, held.pop(j - 1))
                if 0 <= j < SLOTS:
                    expert_hT(j)
                if j in SHARED_AT:
                    kind, n = SHARED_AT[j]
                    if kind == "gu":
                        shared_gu(n)
                    else:
                        shared_down(n)

        @blk.vector
        def _(dve):
            V = nc.vector
            steps = [0]

            def link(ins):
                steps[0] += 1
                ins.then_inc(S("dve_step"), 1)
                dve.wait_ge(S("dve_step"), steps[0])

            V.memset(WARMUP[:, :], 0.0).then_inc(S("constants_set"), 1)
            V.memset(minus_half[:, :], -0.5).then_inc(S("constants_set"), 1)
            V.memset(Z3[:, :, D:D + 1], 1.0).then_inc(S("constants_set"), 1)
            def norm(dst, t, k, done):
                V.tensor_scalar(dst, X[:, t, :], MV[:, k, t, 0:1], RS[:, k, t:t + 1], ALU.subtract, ALU.mult)\
                    .then_inc(S(done), 1)

            stated = [0]

            def bn(tiles):
                for t in tiles:
                    V.bn_stats(ST[:, t, :], X[:, t, :]).then_inc(S("st"), 1)
                stated[0] += len(tiles)
                dve.wait_ge(S("st"), stated[0])

            def front_z(p):
                dve.wait_ge(S("rs"), p // 2 + 1)
                if p >= 2:
                    dve.wait_ge(S("zT_ps"), p - 1)
                for j in range(2):
                    norm(Z[:, p % 2, j, :], 2 * p + j, 0, "z")

            for g in range(4):
                dve.wait_ge(S(f"x_in{g}"), 16)
                bn(range(4 * g, 4 * g + 4))
                for t in range(4 * g, 4 * g + 4):
                    V.bn_aggr(MV[:, 0, t, :], ST[:, t, :]).then_inc(S("mv"), 1)
                if g == 1:
                    front_z(0)
            dve.wait_ge(S("mod_sb"), 1)
            V.tensor_scalar(ONEC[:, :, :], MOD[:, :, 1:5:3], 1.0, None, ALU.add).then_inc(S("one_c"), 1)
            link(V.tensor_scalar(GS[:, :, :], MOD[:, :, 2:6:3], 0.0, 2.0, ALU.is_ge, ALU.mult))
            link(V.tensor_scalar(GS[:, :, :], GS[:, :, :], -1.0, None, ALU.add))
            link(V.tensor_scalar(GA[:, :, :], MOD[:, :, 2:6:3], -1.0, None, ALU.mult))
            link(V.tensor_tensor(GA[:, :, :], GA[:, :, :], MOD[:, :, 2:6:3], ALU.max))
            link(V.tensor_scalar(GA[:, :, :], GA[:, :, :], 0.25, None, ALU.max))
            V.tensor_tensor(GT[:, :, :], GA[:, :, :], GS[:, :, :], ALU.mult).then_inc(S("gate_ok"), 1)

            def front_max(p):
                q = p % 2
                dve.wait_ge(S("qkv_sb"), 2 * (p + 1))
                if p >= 2:
                    dve.wait_ge(S("sub"), 2 * (p - 1))
                V.tensor_reduce(MX[:, q, 0:32].rearrange("p (t h) -> p t h", t=2), heads(QKV[:, q, :, 0:D]),
                                axis=AX.X, op=ALU.max).then_inc(S("mx"), 1)
                V.tensor_reduce(MX[:, q, 32:48].rearrange("p (t d) -> p t d", t=2),
                                QKV[:, q, :, D:2 * D].rearrange("p t (h d) -> p t d h", d=HD0),
                                axis=AX.X, op=ALU.max).then_inc(S("mx"), 1)

            def front_sum(p):
                q = p % 2
                dve.wait_ge(S("exp"), p + 1)
                V.tensor_reduce(SM[:, q, 0:32].rearrange("p (t h) -> p t h", t=2), heads(E0[:, q, :, 0:D]),
                                axis=AX.X, op=ALU.add).then_inc(S("sum"), 1)
                V.tensor_reduce(SM[:, q, 32:48].rearrange("p (t d) -> p t d", t=2),
                                E0[:, q, :, D:2 * D].rearrange("p t (h d) -> p t d h", d=HD0),
                                axis=AX.X, op=ALU.add).then_inc(S("sum"), 1)
                dve.wait_ge(S("sum"), 2 * (p + 1))
                if p >= 2:
                    dve.wait_ge(S("qn"), p - 1)
                V.reciprocal(RC[:, q, :], SM[:, q, :]).then_inc(S("rec"), 1)

            def mid_p1(p, j):
                if p >= 1:
                    dve.wait_ge(S("tvT_ps"), 2 * (p - 1) + j + 1)
                V.tensor_tensor(p1_out(j, 0, K1), p1_k(p % 2, j, 0, K1), p1_v(p % 2, j, 0, K1), ALU.mult)\
                    .then_inc(S("p1d"), 1)

            def mid_p2(p, j):
                dve.wait_ge(S("tv"), 2 * p + j + 1)
                if j == 0:
                    dve.wait_ge(S("qn"), p + 1)
                if p >= 1:
                    dve.wait_ge(S("aT_ps"), 2 * (p - 1) + j + 1)
                V.tensor_tensor(p2_out(j, 0, K2), p2_q(p % 2, j, 0, K2), p2_t(j, 0, K2), ALU.mult)\
                    .then_inc(S("p2d"), 1)

            def mid_x1(p, j):
                t = 2 * p + j
                dve.wait_ge(S("aB_ps"), t + 1)
                V.tensor_tensor(X[:, t, :], B[3 + j][:, 320:448], X[:, t, :], ALU.add)\
                    .then_inc(S("x1"), 1)

            def stats(p, k, ready, count, mv):
                dve.wait_ge(S(ready), count)
                bn(range(2 * p, 2 * p + 2))
                for j in range(2):
                    t = 2 * p + j
                    V.bn_aggr(MV[:, k, t, :], ST[:, t, :]).then_inc(S(mv), 1)

            def back_z2(p):
                dve.wait_ge(S("rs2"), p + 1)
                if p >= 1:
                    dve.wait_ge(S("z2T_ps"), p)
                for j in range(2):
                    norm(Z2[:, j, :], 2 * p + j, 1, "z2")

            def back_hid(p):
                dve.wait_ge(S("gu_ps"), 3 * (p + 1))
                dve.wait_ge(S("silu"), 2 * (p + 1))
                if p >= 1:
                    dve.wait_ge(S("y_ps"), p)
                V.tensor_tensor(HID[:, 0:512], SG[:, 0:512], B[7][:, :], ALU.mult).then_inc(S("hid"), 1)
                V.tensor_tensor(HID[:, 512:768], SG[:, 512:768], B[6][:, 256:512], ALU.mult).then_inc(S("hid"), 1)

            def back_x2(p):
                t = 2 * p
                dve.wait_ge(S("y_ps"), p + 1)
                V.tensor_tensor(X[:, t:t + 2, :], B[yb(p)][:, 256:512].rearrange("p (t d) -> p t d", t=2),
                                X[:, t:t + 2, :], ALU.add).then_inc(S("x2"), 1)

            def bias_row(n):
                if n == 0:
                    dve.wait_ge(s_w1, 144)
                cols = slice(512 * (n % 2), 512 * (n % 2) + 512)
                dve.wait_ge(S("brow_ps"), n + 1)
                V.tensor_tensor(BKVs[:, n // 2, cols], B[0][:, :], BKV[:, n // 2, cols], ALU.add)\
                    .then_inc(S("brow_sb"), 1)

            def back_z3(p):
                dve.wait_ge(S("rs3"), p + 1)
                for j in range(2):
                    norm(Z3[:, 2 * p + j, 0:D], 2 * p + j, 2, "z3")

            for i in STEPS:
                n, f, a, m, b, c = lead(i)
                if m is not None:
                    mid_p2(m, 0)
                    mid_p2(m, 1)
                if a is not None:
                    mid_p1(a, 0)
                    mid_p1(a, 1)
                if i == 1:
                    dve.wait_ge(S("prep_ps"), 2)
                    dve.wait_ge(s_w1, 144)
                    V.tensor_tensor(WQT[:, :, D:D + 1], B[7][:, 0:C1].unsqueeze(2), BQC[:, :].unsqueeze(2), ALU.add)\
                        .then_inc(S("gbb_sb"), 1)
                    V.tensor_copy(GBB[:, :], B[7][:, 128:256]).then_inc(S("gbb_sb"), 1)
                    V.tensor_tensor(NBVC[:, :], B[7][:, C1:2 * C1], BVC[:, :], ALU.add).then_inc(S("gbb_sb"), 1)
                    dve.wait_ge(S("gbb_sb"), 3)
                    link(V.tensor_scalar(NBVC[:, :], NBVC[:, :], float(TOKENS), None, ALU.mult))
                if f is not None:
                    front_max(f)
                if PAIRS - 2 <= i < PAIRS:
                    bias_row(2 * (i - PAIRS + 2))
                if c is not None:
                    back_x2(c)
                    stats(c, 2, "x2", c + 1, "mv3")
                if m is not None:
                    mid_x1(m, 0)
                    mid_x1(m, 1)
                    stats(m, 1, "x1", 2 * m + 2, "mv2")
                if n is not None and n > 0:
                    front_z(n)
                if c is not None:
                    back_z3(c)
                if i == PAIRS - 1:
                    back_hid(b)
                if m is not None:
                    back_z2(m)
                if b is not None and i != PAIRS - 1:
                    back_hid(b)
                if i == PAIRS - 2:
                    bias_row(1)
                if i == PAIRS:
                    bias_row(3)
                if f is not None:
                    front_sum(f)
            dve.wait_ge(S("g_all"), 1)
            V.tensor_copy(GZ[:, :], B[0][:, 0:D + 1]).then_inc(S("gz"), 1)
            dve.wait_ge(S("ab_ps"), 1)
            V.tensor_tensor(AB[:, :], B[2][:, 0:C1], NBVC[:, :], ALU.add).then_inc(S("ab"), 1)
            dve.wait_ge(S("gz"), 1)
            for n in range(2):
                cols = slice(512 * n, 512 * n + 512)
                dve.wait_ge(S("a_ps"), n + 1)
                V.scalar_tensor_tensor(out=A1[:, cols], in0=BKVs[:, 1, cols], scalar=GZ[:, D:D + 1], in1=B[n][:, :],
                                       op0=ALU.mult, op1=ALU.add).then_inc(S("a_sb"), 1)
            dve.wait_ge(S("kv_zero"), 2)
            for h in range(2):
                dve.wait_ge(S("kv_ps"), h + 1)
                dve.wait_ge(S("vsk"), h + 1)
                for lo in (0, 64):
                    V.tensor_tensor(KV[lo:lo + 64, 4 * h:4 * h + 4, lo:lo + 64],
                                    B[(5, 2)[h]][lo:lo + 64, :].rearrange("p (c k) -> p c k", c=4)[:, :, lo:lo + 64],
                                    VSK[lo:lo + 64, 512 * h:512 * h + 512].rearrange("p (c k) -> p c k", c=4)
                                    [:, :, lo:lo + 64], ALU.add).then_inc(S("kv_sb"), 1)
            dve.wait_ge(S("do_ps"), 2)
            V.tensor_copy(DO[:, 4:8, :], B[1][:, :].rearrange("p (c d) -> p c d", c=4)).then_inc(S("do_sb_d"), 1)
            dve.wait_ge(S("mt_ps"), 1)
            V.tensor_scalar(MT[:, :], B[3][:, 0:D + 1], GT[:, 1, 0:1], SCALE1, ALU.mult, ALU.mult)\
                .then_inc(S("mt_step"), 1)
            dve.wait_ge(S("mt_step"), 1)
            dve.wait_ge(S("bog"), 1)
            V.tensor_tensor(MT[:, D:D + 1], MT[:, D:D + 1], BOG[:, :], ALU.add).then_inc(S("mt_step"), 1)
            dve.wait_ge(S("mt_step"), 2)
            V.tensor_scalar(DG[:, :], ident, MT[:, D:D + 1], None, ALU.mult).then_inc(S("mt_step"), 1)

            def attend(g):
                ts = slice(4 * g, 4 * g + 4)
                dve.wait_ge(S("o_ps"), g + 1)
                V.tensor_tensor(X[:, ts, :], B[OUT[g]][:, :].rearrange("p (t d) -> p t d", t=4), X[:, ts, :],
                                ALU.add).then_inc(S("x3"), 1)

            attend(0)
            for g in range(4):
                dve.wait_ge(S("x3"), g + 1)
                for t in range(4 * g, 4 * g + 4):
                    V.bn_stats(ST[:, t, :], X[:, t, :]).then_inc(S("st"), 1)
                stated[0] += 4
                if g < 3:
                    attend(g + 1)
                dve.wait_ge(S("st"), stated[0])
                for t in range(4 * g, 4 * g + 4):
                    V.bn_aggr(MV[:, 3, t, :], ST[:, t, :]).then_inc(S("mv4"), 1)
            for g in (2, 3):
                dve.wait_ge(S("rs4"), g + 1)
                for t in range(4 * g + NORMA[g], 4 * g + 4):
                    norm(Z4[:, t, :], t, 3, "z4d")
            dve.wait_ge(S("h4T_ps"), 3)
            V.tensor_scalar(H4T[:, 1024:1536], B[2][:, :], ONEC[:, 1, 1:2], MOD[:, 1, 3:4], ALU.mult, ALU.add)\
                .then_inc(S("h4T_d"), 1)

            def over_e(ap):
                return ap.unsqueeze(2).broadcast_to([128, T, NE])

            def shared_hid(n):
                dve.wait_ge(S("ssilu"), n + 1)
                if n >= 4:
                    dve.wait_ge(S("sy_ps"), n // 2 - 1)
                V.tensor_tensor(HS[n // 2 % 2][:, 512 * (n % 2):512 * (n % 2) + 512], SS[n % 2], B[UB[n]][:, :],
                                ALU.mult).then_inc(S("shid"), 1)

            def shared_x4(g):
                dve.wait_ge(S("sy_ps"), g + 1)
                for t in range(4 * g, 4 * g + 4):
                    V.scalar_tensor_tensor(out=X[:, t, :], in0=B[1][:, 128 * (t % 4):128 * (t % 4) + 128],
                                           scalar=GATE[:, t:t + 1], in1=X[:, t, :], op0=ALU.mult, op1=ALU.add)\
                        .then_inc(S("x4"), 1)

            def do(ins):
                steps[0] += 1
                ins.then_inc(S("dve_step"), 1)
                return steps[0]

            def after(n):
                dve.wait_ge(S("dve_step"), n)

            def pick(halves):
                dve.wait_ge(S("lg_ps"), 4)
                done = {}

                def both(make):
                    for g in halves:
                        if g in done:
                            after(done[g])
                        done[g] = do(make(slice(8 * g, 8 * g + 8)))

                def over(ap):
                    return ap.unsqueeze(2).broadcast_to([128, 8, NE])

                w = first_w.unsqueeze(1).broadcast_to([128, 8, NE])
                both(lambda ts: V.tensor_copy(LG[:, ts, :], B[LB[ts.start // 8]][:, 9 * ts.start:9 * ts.stop]
                                              .rearrange("p (t e) -> p t e", e=9)))
                for k in range(2):
                    L = (LG[:, :, 0:NE], L2)[k]
                    both(lambda ts: V.tensor_reduce(TOP[:, k, ts], L[:, ts, :], axis=AX.X, op=ALU.max))
                    both(lambda ts: V.tensor_tensor(SCR[:, ts, :], L[:, ts, :], over(TOP[:, k, ts]), ALU.is_equal))
                    both(lambda ts: V.tensor_tensor(SCR[:, ts, :], SCR[:, ts, :], w, ALU.mult))
                    both(lambda ts: V.tensor_reduce(RM[:, ts], SCR[:, ts, :], axis=AX.X, op=ALU.max))
                    both(lambda ts: V.tensor_tensor(OH[:, k, ts, :], SCR[:, ts, :], over(RM[:, ts]), ALU.is_equal))
                    if k == 0:
                        both(lambda ts: V.scalar_tensor_tensor(out=L2[:, ts, :], in0=OH[:, 0, ts, :], scalar=-1e30,
                                                               in1=LG[:, ts, 0:NE], op0=ALU.mult, op1=ALU.add))
                for g in halves:
                    ts = slice(8 * g, 8 * g + 8)
                    after(done[g])
                    V.tensor_tensor(MH[:, ts, :], OH[:, 0, ts, :], OH[:, 1, ts, :], ALU.add)\
                        .then_inc(S("picked"), 1)

            pick((0, 1))
            V.tensor_tensor(PR[:, :, :], LG[:, :, 0:NE], over_e(TOP[:, 0, :]), ALU.subtract).then_inc(S("rt_sub"), 1)
            V.tensor_tensor(WK[1], TOP[:, 1, :], TOP[:, 0, :], ALU.subtract).then_inc(S("rt_sub"), 1)

            dve.wait_ge(S("rank_ps"), 1)
            tiles = do(V.tensor_scalar(NTF[:, :], B[2][:, 8 * T:8 * T + 8], 1.0 / 128, 63.5 / 128, ALU.mult, ALU.add))
            sel = do(V.tensor_tensor(OHR[:, :, :, :], OH[:, :, :, :], B[2][:, 0:8 * T]
                                     .rearrange("p (t e) -> p t e", e=8).unsqueeze(1)
                                     .broadcast_to([128, 2, T, NE]), ALU.mult))
            after(tiles)
            tiles = do(V.tensor_scalar(NTF[:, :], NTF[:, :], MAGIC, -MAGIC, ALU.add, ALU.add))
            dve.wait_ge(S("rt_exp"), 2)
            sums = do(V.tensor_reduce(RSUM[:, :], PX[:, :, :], axis=AX.X, op=ALU.add))
            after(sel)
            rank = do(V.tensor_reduce(RANK[:, :], OHR[:, :, :, :].rearrange("p k t e -> p (k t) e"),
                                      axis=AX.X, op=ALU.add))
            after(tiles)
            start = do(V.tensor_tensor(STT[:, :, :], before.rearrange("p (e f) -> p e f", e=8),
                                       NTF[:, :].unsqueeze(1).broadcast_to([128, NE, NE]), ALU.mult))
            after(sums)
            V.reciprocal(WK[0], RSUM[:, :]).then_inc(S("weights"), 1)
            after(rank)
            row = do(V.tensor_scalar(RTILE[:, :], RANK[:, :], 1.0 / 128, -63.5 / 128, ALU.mult, ALU.add))
            after(start)
            start = do(V.tensor_reduce(START[:, :], STT[:, :, :], axis=AX.X, op=ALU.add))
            after(row)
            row = do(V.tensor_scalar(RTILE[:, :], RTILE[:, :], MAGIC, -MAGIC, ALU.add, ALU.add))
            dve.wait_ge(S("weights"), 1)
            V.tensor_tensor(WK[1], WK[1], WK[0], ALU.mult).then_inc(S("weights"), 1)
            after(start)
            sel = do(V.tensor_tensor(OHS[:, :, :, :], OH[:, :, :, :], START[:, :].unsqueeze(1).unsqueeze(1)
                                     .broadcast_to([128, 2, T, NE]), ALU.mult))
            after(row)
            V.scalar_tensor_tensor(out=ROW[:, :], in0=RTILE[:, :], scalar=-128.0, in1=RANK[:, :],
                                   op0=ALU.mult, op1=ALU.add).then_inc(S("row"), 1)
            after(sel)
            tile = do(V.tensor_reduce(FIRST[:, :], OHS[:, :, :, :].rearrange("p k t e -> p (k t) e"),
                                      axis=AX.X, op=ALU.add))
            end = do(V.tensor_tensor(ENDT[:, :], START[:, :], NTF[:, :], ALU.add))
            after(tile)
            tile = do(V.tensor_tensor(TILE[:, :], FIRST[:, :], RTILE[:, :], ALU.add))
            after(tile)
            for k in range(2):
                V.tensor_tensor(AH[:, T * k:T * k + T, SLOTS:2 * SLOTS],
                                TILE[:, T * k:T * k + T].unsqueeze(2).broadcast_to([128, T, SLOTS]),
                                iota_h[:, 0:SLOTS].unsqueeze(1).broadcast_to([128, T, SLOTS]), ALU.is_equal)\
                    .then_inc(S("tile_hot"), 1)
            dve.wait_ge(S("row"), 1)
            for a in range(0, 2 * T - 8, 8):
                V.tensor_tensor(BH[:, a:a + 8, :], iota_h.unsqueeze(1).broadcast_to([128, 8, 128]),
                                ROW[:, a:a + 8].unsqueeze(2).broadcast_to([128, 8, 128]), ALU.is_equal)\
                    .then_inc(S("row_hot"), 1)
            after(end)
            link(V.tensor_tensor(GEQ[0:1, :, :], slot_iota[0:1, :].unsqueeze(2).broadcast_to([1, SLOTS, NE]),
                                 ENDT[0:1, :].unsqueeze(1).broadcast_to([1, SLOTS, NE]), ALU.is_ge))
            link(V.tensor_reduce(EXF[0:1, :], GEQ[0:1, :, :], axis=AX.X, op=ALU.add))
            V.tensor_scalar(EXI[0:1, :], EXF[0:1, :], NE - 1.0, None, ALU.min).then_inc(S("idx"), 1)
            dve.wait_ge(S("idx_ps"), 1)
            link(V.tensor_copy(IDX[:, :, :, :], B[4][:, 0:4 * SLOTS].rearrange("p (k w s) -> p k w s", k=2, w=2)))
            V.tensor_tensor(GI[:, :], IDX[:, 0, 0, :], IDX[:, 1, 0, :], ALU.add).then_inc(S("gather_idx"), 1)
            dve.wait_ge(S("shid"), 2)
            shared_hid(2)
            shared_hid(3)
            a = do(V.tensor_tensor(ANY[:, :], IDX[:, 0, 1, :], IDX[:, 1, 1, :], ALU.add))
            d = do(V.scalar_tensor_tensor(out=DF[:, :], in0=IDX[:, 1, 1, :], scalar=float(TOKENS),
                                          in1=IDX[:, 1, 0, :], op0=ALU.mult, op1=ALU.add))
            after(a)
            do(V.scalar_tensor_tensor(out=PADF[:, :], in0=ANY[:, :], scalar=0.0, in1=pad_row,
                                      op0=ALU.is_equal, op1=ALU.mult))
            after(d)
            d = do(V.tensor_tensor(DF[:, :], DF[:, :], IDX[:, 0, 0, :], ALU.add))
            after(d)
            V.tensor_tensor(DI[:, :], DF[:, :], PADF[:, :], ALU.add).then_inc(S("idx"), 1)
            dve.wait_ge(S("rt_exp"), 3)
            link(V.tensor_scalar(GATE[:, :], GATE[:, :], 1.0, None, ALU.add))
            V.reciprocal(GATE[:, :], GATE[:, :]).then_inc(S("gate"), 1)
            dve.wait_ge(S("gate"), 1)
            shared_x4(0)
            shared_hid(4)


            def expert_hid(j):
                dve.wait_ge(S("esilu"), j + 1)
                if j >= 2:
                    dve.wait_ge(S("ht_ps"), j - 1)
                V.tensor_tensor(HX[j % 2], SX[j % 2], B[2 + j % 2][:, FE:2 * FE], ALU.mult).then_inc(S("ehid"), 1)

            def expert_hT(j):
                dve.wait_ge(S("ht_ps"), j + 1)
                if j >= 2:
                    dve.wait_ge(S("ey_ps"), j - 1)
                V.tensor_copy(HXT[j % 2], B[4][:, 0:2 * 128]).then_inc(S("ht"), 1)

            def expert_y(j):
                dve.wait_ge(S("ey_ps"), j + 1)
                if j >= SCATTERS:
                    dve.wait_ge(S(f"scattered{j % SCATTERS}"), 16 * (j // SCATTERS))
                dve.wait_ge(S("wrow"), 2 * j + 2)
                V.tensor_scalar(YX[j % SCATTERS], B[5][:, 0:128], WROW[:, j % 2, 1:2], None, ALU.mult)\
                    .then_inc(S("ey"), 1)

            def expert_weight(j, step):
                w = GX[j % GATHERS][:, D:D + 2]
                if step == 0:
                    dve.wait_ge(S(f"gathered{j % GATHERS}"), 16 * (j // GATHERS + 1))
                    V.tensor_scalar(WROW[:, j % 2, 0:1], w[:, 0:1], KROW[0][:, j:j + 1], None, ALU.mult)\
                        .then_inc(S("wrow"), 1)
                else:
                    dve.wait_ge(S("wrow"), 2 * j + 1)
                    V.scalar_tensor_tensor(out=WROW[:, j % 2, 1:2], in0=w[:, 1:2], scalar=KROW[1][:, j:j + 1],
                                           in1=WROW[:, j % 2, 0:1], op0=ALU.mult, op1=ALU.add)\
                        .then_inc(S("wrow"), 1)

            for j in range(-3, SLOTS + 1):
                if 0 <= j - 1:
                    expert_y(j - 1)
                if 0 <= j < SLOTS:
                    expert_weight(j, 0)
                    expert_hT(j)
                    expert_weight(j, 1)
                if 0 <= j + 1 < SLOTS:
                    expert_hid(j + 1)
                if j in SHARED_AT:
                    kind, n = SHARED_AT[j]
                    if kind == "gu":
                        shared_hid(n)
                    else:
                        shared_x4(n)

            for g in range(3):
                dve.wait_ge(S(f"y_in{g}"), 32)
                for k in range(2):
                    if k == 1:
                        dve.wait_ge(S("x5"), 2 * g + 1)
                    V.tensor_tensor(X[:, 4 * g:4 * g + 4, :], YB[g][:, k, :, :], X[:, 4 * g:4 * g + 4, :], ALU.add)\
                        .then_inc(S("x5"), 1)

        @blk.gpsimd
        def _(pool):
            G = nc.gpsimd

            added = [0]

            def rstd(k, a, b, mv, rs):
                pool.wait_ge(S(mv), b)
                G.tensor_scalar(VE[:, k, a:b], MV[:, k, a:b, 1], EPS, None, ALU.add).then_inc(S("var_eps"), 1)
                added[0] += 1
                pool.wait_ge(S("var_eps"), added[0])
                G.tensor_tensor(RS[:, k, a:b], VE[:, k, a:b], minus_half[:, a:b], ALU.pow).then_inc(S(rs), 1)

            pool.wait_ge(S("constants_set"), 2)
            for g in range(4):
                rstd(0, 4 * g, 4 * g + 4, "mv", "rs")
            pool.wait_ge(s_wi, 16)
            G.tensor_copy(WGU0[:, :], WGU0i[:, :]).then_inc(S("w0_cast"), 1)

            def layer1_weights():
                pool.wait_ge(s_w1, 144)
                pool.wait_ge(S("one_c"), 1)
                pool.wait_ge(S("gate_ok"), 1)
                pool.wait_ge(s_cf, 16)
                G.tensor_scalar(DG[:, :], ident, GT[:, 1, 1:2], None, ALU.mult).then_inc(S("diag_gb"), 1)
                G.tensor_scalar(BOG[:, :], BO[:, :], GT[:, 1, 0:1], None, ALU.mult).then_inc(S("bog"), 1)
                G.memset(MH[:, :, :], 0.0).then_inc(S("kv_zero"), 1)
                G.memset(KV[:, :, :], 0.0).then_inc(S("kv_zero"), 1)

            def front_sub(p):
                q = p % 2
                pool.wait_ge(S("mx"), 2 * (p + 1))
                if p >= 2:
                    pool.wait_ge(S("exp"), p - 1)
                G.tensor_tensor(heads(S0[:, q, :, 0:D]), heads(QKV[:, q, :, 0:D]),
                                MX[:, q, 0:32].rearrange("p (t h) -> p t h", t=2).unsqueeze(3)
                                .broadcast_to([128, 2, H0, HD0]), ALU.subtract).then_inc(S("sub"), 1)
                G.tensor_tensor(heads(S0[:, q, :, D:2 * D]), heads(QKV[:, q, :, D:2 * D]),
                                MX[:, q, 32:48].rearrange("p (t d) -> p t d", t=2).unsqueeze(2)
                                .broadcast_to([128, 2, H0, HD0]), ALU.subtract).then_inc(S("sub"), 1)

            def front_norm(p):
                q = p % 2
                pool.wait_ge(S("rec"), p + 1)
                if p >= 2:
                    pool.wait_ge(S("p2d"), 2 * (p - 1))
                G.tensor_tensor(heads(QH[:, q, :, :]), heads(E0[:, q, :, 0:D]),
                                RC[:, q, 0:32].rearrange("p (t h) -> p t h", t=2).unsqueeze(3)
                                .broadcast_to([128, 2, H0, HD0]), ALU.mult).then_inc(S("qh"), 1)
                pool.wait_ge(S("qh"), p + 1)
                G.tensor_tensor(heads(QN[:, q, :, :]), heads(QH[:, q, :, :]),
                                RC[:, q, 32:48].rearrange("p (t d) -> p t d", t=2).unsqueeze(2)
                                .broadcast_to([128, 2, H0, HD0]), ALU.mult).then_inc(S("qn"), 1)

            def mid_p1(p, j):
                pool.wait_ge(S("exp"), p + 1)
                if p >= 1:
                    pool.wait_ge(S("tvT_ps"), 2 * (p - 1) + j + 1)
                G.tensor_tensor(p1_out(j, K1, H0), p1_k(p % 2, j, K1, H0), p1_v(p % 2, j, K1, H0), ALU.mult)\
                    .then_inc(S("p1p"), 1)

            def mid_p2(p, j):
                pool.wait_ge(S("tv"), 2 * p + j + 1)
                if p >= 1:
                    pool.wait_ge(S("aT_ps"), 2 * (p - 1) + j + 1)
                if j == 0:
                    pool.wait_ge(S("qn"), p + 1)
                G.tensor_tensor(p2_out(j, K2, HD0), p2_q(p % 2, j, K2, HD0), p2_t(j, K2, HD0), ALU.mult)\
                    .then_inc(S("p2p"), 1)

            for i in STEPS:
                n, f, a, m, b, c = lead(i)
                if m is not None:
                    mid_p2(m, 0)
                    mid_p2(m, 1)
                if a is not None:
                    mid_p1(a, 0)
                    mid_p1(a, 1)
                if f is not None:
                    front_sub(f)
                if c is not None:
                    rstd(2, 2 * c, 2 * c + 2, "mv3", "rs3")
                if m is not None:
                    rstd(1, 2 * m, 2 * m + 2, "mv2", "rs2")
                if a is not None:
                    front_norm(a)
                if i == -1:
                    layer1_weights()
                if 1 <= i <= NE + 1:
                    e = (i - 2) % (NE + 1)
                    if i == 1:
                        pool.wait_ge(s_we, 96)
                        pool.wait_ge(S("gbb_sb"), 2)
                    G.tensor_tensor(WD1g[:, e, :, :], WD1[:, e, :, :],
                                    GBB[:, :].unsqueeze(1).broadcast_to([128, 2, D]), ALU.mult)\
                        .then_inc(S("wd1_scaled"), 1)
            pool.wait_ge(S("ab"), 1)
            for h in range(2):
                G.tensor_tensor(VSK[:, 512 * h:512 * h + 512].rearrange("p (c k) -> p c k", c=4),
                                BKVs[:, 0, 512 * h:512 * h + 512].rearrange("p (c k) -> p c k", c=4),
                                AB[:, 4 * h:4 * h + 4].unsqueeze(2).broadcast_to([128, 4, 128]), ALU.mult)\
                    .then_inc(S("vsk"), 1)
            for g in range(4):
                ts = slice(4 * g, 4 * g + 4)
                pool.wait_ge(S("mv4"), 4 * g + 4)
                G.tensor_scalar(NM[:, ts], MV[:, 3, ts, 0], -1.0, None, ALU.mult).then_inc(S("nm4"), 1)
                rstd(3, 4 * g, 4 * g + 4, "mv4", "rs4")
                pool.wait_ge(S("nm4"), 2 * g + 1)
                pool.wait_ge(S("rs4"), g + 1)
                G.tensor_tensor(NM[:, ts], NM[:, ts], RS[:, 3, ts], ALU.mult).then_inc(S("nm4"), 1)

            def tokens_hot():
                for k in range(2):
                    pool.wait_ge(S("tile_hot"), k + 1)
                    G.tensor_tensor(AH[:, T * k:T * k + T, 0:SLOTS], AH[:, T * k:T * k + T, SLOTS:2 * SLOTS],
                                    token_id.unsqueeze(2).broadcast_to([128, T, SLOTS]), ALU.mult)\
                        .then_inc(S("token_hot"), 1)

            def gather(j):
                if j >= GATHERS:
                    pool.wait_ge(S("xt_ps"), j - GATHERS + 1)
                    pool.wait_ge(S("wrow"), 2 * (j - GATHERS + 1))
                G.indirect_dma_start(GX[j % GATHERS], None, z_dram.ap(),
                                     bass.IndirectOffsetOnAxis(GI[:, j:j + 1].bitcast(U32), 0))\
                    .then_inc(S(f"gathered{j % GATHERS}"), 16)

            def scatter(j):
                if j == 0:
                    pool.wait_ge(S("idx"), 2)
                pool.wait_ge(S("ey"), j + 1)
                G.indirect_dma_start(y_dram.ap(), bass.IndirectOffsetOnAxis(DI[:, j:j + 1].bitcast(U32), 0),
                                     YX[j % SCATTERS], None).then_inc(S(f"scattered{j % SCATTERS}"), 16)

            def shared_hid(n):
                pool.wait_ge(S("ssilu"), n + 1)
                pool.wait_ge(S("u_sb"), n + 1)
                G.tensor_tensor(HS[n // 2 % 2][:, 512 * (n % 2):512 * (n % 2) + 512], SS[n % 2], US[n % 2],
                                ALU.mult).then_inc(S("shid"), 1)

            shared_hid(0)
            shared_hid(1)
            tokens_hot()
            pool.wait_ge(S("gather_idx"), 1)
            pool.wait_ge(S("z_rows"), 64)
            for j in range(SLOTS + GATHERS - 1):
                if j < SLOTS:
                    gather(j)
                if j >= GATHERS - 1:
                    scatter(j - GATHERS + 1)
            pool.wait_ge(S("x4"), T)
            pool.wait_ge(S("y_in3"), 32)
            for k in range(2):
                if k == 1:
                    pool.wait_ge(S("x5p"), 1)
                G.tensor_tensor(X[:, 12:16, :], YB[3][:, k, :, :], X[:, 12:16, :], ALU.add).then_inc(S("x5p"), 1)


def laid_out(i):
    def c(a):
        return np.ascontiguousarray(a)
    i = {k: np.asarray(v) for k, v in i.items()}
    cf, _, ch = constants()
    n = NE
    return dict(
        x_in=c(i["L0_attn_input_seq_embs"].reshape(TOKENS, D)),
        wqkv0=c(np.concatenate([i["L0_attn_W_Q"].T, i["L0_attn_W_K"].T, i["L0_attn_W_V"].T], 1)),
        wgu0=c(np.concatenate([i["L0_ffn_w_gate"].T, i["L0_ffn_w_up"].T], 1)),
        wd0=c(i["L0_ffn_w_down"]),
        c0=c(i["L0_c"].reshape(D, 1)), wmod0=c(i["L0_wmod"]),
        wq1=c(i["L1_attn_Wq"]), wk1=c(i["L1_attn_Wk"]), wv1=c(i["L1_attn_Wv"]),
        bqc1=c(i["L1_attn_bq"].reshape(C1, 128).T), bk1=c(i["L1_attn_bk"].reshape(1, HW1)),
        bvc1=c(i["L1_attn_bv"].reshape(C1, 128).T), bv1=c(i["L1_attn_bv"].reshape(1, HW1)), wo1=c(i["L1_attn_Wo"]),
        bo1=c(i["L1_attn_bo"].reshape(D, 1)),
        router=c(np.concatenate([i["L1_ffn_router_w"].T, i["L1_ffn_gate_w"].T], 1)),
        wgu1=c(np.concatenate([i["L1_ffn_w_gate"], i["L1_ffn_w_up"]], 2).transpose(1, 0, 2)),
        wd1=c(i["L1_ffn_w_down"].reshape(n, 2, 128, D).transpose(2, 0, 1, 3)),
        swgu1=c(np.concatenate([i["L1_ffn_sw_gate"], i["L1_ffn_sw_up"]], 1)),
        swd1=c(i["L1_ffn_sw_down"].reshape(2, 128, D).transpose(1, 0, 2)),
        c1=c(i["L1_c"].reshape(D, 1)), wmod1=c(i["L1_wmod"]),
        const_f=cf, const_h=ch,
    )


def kernel(**inputs):
    import concourse.bacc as _bacc
    from concourse.bass_utils import run_bass_kernel_spmd as _run

    arrays = laid_out(inputs)
    nc = _bacc.Bacc("TRN2", target_bir_lowering=False, num_devices=1)
    args = {name: nc.dram_tensor(name + "_dram", a.shape, mybir.dt.from_np(a.dtype), kind="ExternalInput").ap()
            for name, a in arrays.items()}
    out = nc.dram_tensor("out_dram", (TOKENS, D), F32, kind="ExternalOutput").ap()
    build(nc, out=out, **args)
    r = _run(nc, [{name + "_dram": a for name, a in arrays.items()}], core_ids=[0])
    return r.results[0]["out_dram"].reshape(1, TOKENS, D)
```
